# Optimizing a Trainium2 kernel written in Bass

```python
import numpy as np
import jax
import jax.numpy as jnp

def _softmax(x, axis=-1):
    return jax.nn.softmax(x, axis=axis)

def _gelu(x):
    return jax.nn.gelu(x, approximate=True)

def _silu(x):
    return jax.nn.silu(x)

def _sigmoid(x):
    return jax.nn.sigmoid(x)

def _layernorm(x, axis=-1, eps=1e-05):
    m = jnp.mean(x, axis=axis, keepdims=True)
    v = jnp.var(x, axis=axis, keepdims=True)
    return (x - m) / jnp.sqrt(v + eps)

def _scatter_add(tgt, idx, src, axis=0):
    return tgt.at[idx].add(src)

def _segment_sum(src, seg, n):
    return jax.ops.segment_sum(src, seg, n)
kernel_name = 'mk_gps_d1_gnn_r8_af257c'

def setup_inputs(seed: int=0):
    np.random.seed(seed)
    _w = jnp.asarray

    def _rec_inputs():
        import jax
        import jax.numpy as jnp
        _gk = jax.random.key(seed)
        x = -0.0001126 + 1 * jax.random.normal(jax.random.fold_in(_gk, 1), (1250, 768), jnp.float32)
        src = jax.random.randint(jax.random.fold_in(_gk, 2), (20000,), 0, 1250, jnp.int32)
        dst = jnp.minimum((1250 * jax.random.uniform(jax.random.fold_in(_gk, 3), (20000,)) ** 2.0).astype(jnp.int32), 9999)
        _o = jnp.argsort(dst, stable=True)
        src = src[_o]
        dst = dst[_o]
        edge_weight1 = -0.00472126 + 0.997171 * jax.random.normal(jax.random.fold_in(_gk, 13), (20000, 1), jnp.float32)
        return (x, src, dst, edge_weight1)
    x, src, dst, edge_weight1 = _rec_inputs()

    def _L0_gnn_setup():
        import jax, jax.numpy as jnp
        import numpy as np
        N, E, D, H, C = (1250, 12500, 768, 4, 192)
        NEG_SLOPE = 0.2

        def gat_conv(x, src, dst, W, a_src, a_dst, b):
            h = (x @ W).reshape(N, H, C)
            as_n = (h * a_src).sum(-1)
            ad_n = (h * a_dst).sum(-1)
            e = jax.nn.leaky_relu(as_n[src] + ad_n[dst], NEG_SLOPE)
            m = jax.ops.segment_max(e, dst, num_segments=N)
            p = jnp.exp(e - m[dst])
            s = jax.ops.segment_sum(p, dst, num_segments=N)
            alpha = p / (s[dst] + 1e-16)
            out = jax.ops.segment_sum(alpha[:, :, None] * h[src], dst, num_segments=N)
            return out.reshape(N, H * C) + b
        key = jax.random.key(seed)
        ks = jax.random.split(key, 16)
        w = lambda k, shape: jax.random.normal(k, shape, dtype=jnp.float32) * 0.02
        inp = {}
        inp['x'] = jax.random.normal(ks[0], (N, D), dtype=jnp.float32)
        inp['edge_index'] = jax.random.randint(ks[1], (2, E), 0, N, dtype=jnp.int32)
        inp['batch'] = jnp.zeros((N,), dtype=jnp.int32)
        inp['edge_attr'] = jax.random.normal(ks[2], (E, 1), dtype=jnp.float32)
        inp['W_ah'] = w(ks[3], (D, D))
        inp['b_ah'] = jnp.zeros((D,), jnp.float32)
        for i in range(3):
            inp[f'W{i}'] = w(ks[4 + 3 * i], (D, H * C))
            inp[f'a_src{i}'] = w(ks[5 + 3 * i], (H, C))
            inp[f'a_dst{i}'] = w(ks[6 + 3 * i], (H, C))
            inp[f'b{i}'] = jnp.zeros((H * C,), jnp.float32)
        inp['W_out'] = w(ks[13], (3 * D, D))
        inp['b_out'] = jnp.zeros((D,), jnp.float32)
        return inp
    _L0_gnn_all = _L0_gnn_setup()
    _L0_gnn_in = {k: v for k, v in _L0_gnn_all.items() if k in ('W_ah', 'b_ah', 'W0', 'a_src0', 'a_dst0', 'b0', 'W1', 'a_src1', 'a_dst1', 'b1', 'W2', 'a_src2', 'a_dst2', 'b2', 'W_out', 'b_out')}
    del _L0_gnn_all

    def _L0_mix_setup():
        import jax, jax.numpy as jnp
        import numpy as np
        NUM_HEADS = 12
        DIM = 768
        HEAD_DIM = DIM // NUM_HEADS
        key = jax.random.key(seed)
        k1, k2, k3, k4 = jax.random.split(key, 4)
        B, N, C = (4, 1024, DIM)
        x = jax.random.normal(k1, (B, N, C), dtype=jnp.float32)
        W_qkv = jax.random.normal(k2, (3 * C, C), dtype=jnp.float32) * (1.0 / np.sqrt(C))
        W_proj = jax.random.normal(k3, (C, C), dtype=jnp.float32) * (1.0 / np.sqrt(C))
        b_proj = jax.random.normal(k4, (C,), dtype=jnp.float32) * 0.01
        return {'x': x, 'W_qkv': W_qkv, 'W_proj': W_proj, 'b_proj': b_proj}
    _L0_mix_all = _L0_mix_setup()
    _L0_mix_in = {k: v for k, v in _L0_mix_all.items() if k in ('W_qkv', 'W_proj', 'b_proj')}
    del _L0_mix_all

    def _L0_ffn_setup():
        import jax, jax.numpy as jnp
        import numpy as np
        NUM_EXPERTS = 4
        TOPK = 1
        TEMPERATURE = 1.0
        NORM_TOPK_PROB = True
        N_CLS = 1
        N_REL = 4
        key = jax.random.key(seed)
        ks = jax.random.split(key, 7)
        B, N_total, D, r, E = (64, 1029, 768, 64, NUM_EXPERTS)
        x = jax.random.normal(ks[0], (B, N_total, D), dtype=jnp.float32)
        Wd = jax.random.normal(ks[1], (r, D), dtype=jnp.float32) * (1.0 / np.sqrt(D))
        Wg = jax.random.normal(ks[2], (E, r), dtype=jnp.float32) * (1.0 / np.sqrt(r))
        We = jax.random.normal(ks[3], (E, r, r), dtype=jnp.float32) * (1.0 / np.sqrt(r))
        be = jax.random.normal(ks[4], (E, r), dtype=jnp.float32) * 0.01
        Wu = jax.random.normal(ks[5], (D, r), dtype=jnp.float32) * (1.0 / np.sqrt(r))
        gamma = jnp.ones((D,), dtype=jnp.float32)
        return {'x': x, 'Wd': Wd, 'Wg': Wg, 'We': We, 'be': be, 'Wu': Wu, 'gamma': gamma}
    _L0_ffn_all = _L0_ffn_setup()
    _L0_ffn_in = {k: v for k, v in _L0_ffn_all.items() if k in ('Wd', 'Wg', 'We', 'be', 'Wu', 'gamma')}
    del _L0_ffn_all
    return {'x': x, 'src': src, 'dst': dst, 'edge_weight1': edge_weight1, 'L0_gnn_W_ah': _L0_gnn_in['W_ah'], 'L0_gnn_b_ah': _L0_gnn_in['b_ah'], 'L0_gnn_W0': _L0_gnn_in['W0'], 'L0_gnn_a_src0': _L0_gnn_in['a_src0'], 'L0_gnn_a_dst0': _L0_gnn_in['a_dst0'], 'L0_gnn_b0': _L0_gnn_in['b0'], 'L0_gnn_W1': _L0_gnn_in['W1'], 'L0_gnn_a_src1': _L0_gnn_in['a_src1'], 'L0_gnn_a_dst1': _L0_gnn_in['a_dst1'], 'L0_gnn_b1': _L0_gnn_in['b1'], 'L0_gnn_W2': _L0_gnn_in['W2'], 'L0_gnn_a_src2': _L0_gnn_in['a_src2'], 'L0_gnn_a_dst2': _L0_gnn_in['a_dst2'], 'L0_gnn_b2': _L0_gnn_in['b2'], 'L0_gnn_W_out': _L0_gnn_in['W_out'], 'L0_gnn_b_out': _L0_gnn_in['b_out'], 'L0_mix_W_qkv': _L0_mix_in['W_qkv'], 'L0_mix_W_proj': _L0_mix_in['W_proj'], 'L0_mix_b_proj': _L0_mix_in['b_proj'], 'L0_ffn_Wd': _L0_ffn_in['Wd'], 'L0_ffn_Wg': _L0_ffn_in['Wg'], 'L0_ffn_We': _L0_ffn_in['We'], 'L0_ffn_be': _L0_ffn_in['be'], 'L0_ffn_Wu': _L0_ffn_in['Wu'], 'L0_ffn_gamma': _L0_ffn_in['gamma']}

def reference(x, src, dst, edge_weight1, L0_gnn_W_ah, L0_gnn_b_ah, L0_gnn_W0, L0_gnn_a_src0, L0_gnn_a_dst0, L0_gnn_b0, L0_gnn_W1, L0_gnn_a_src1, L0_gnn_a_dst1, L0_gnn_b1, L0_gnn_W2, L0_gnn_a_src2, L0_gnn_a_dst2, L0_gnn_b2, L0_gnn_W_out, L0_gnn_b_out, L0_mix_W_qkv, L0_mix_W_proj, L0_mix_b_proj, L0_ffn_Wd, L0_ffn_Wg, L0_ffn_We, L0_ffn_be, L0_ffn_Wu, L0_ffn_gamma):
    import jax
    import jax.numpy as jnp

    def _L0_gnn_ref(x, edge_index, batch, edge_attr, W_ah, b_ah, W0, a_src0, a_dst0, b0, W1, a_src1, a_dst1, b1, W2, a_src2, a_dst2, b2, W_out, b_out):
        import jax, jax.numpy as jnp
        import numpy as np
        N, E, D, H, C = (1250, 12500, 768, 4, 192)
        NEG_SLOPE = 0.2

        def gat_conv(x, src, dst, W, a_src, a_dst, b):
            h = (x @ W).reshape(N, H, C)
            as_n = (h * a_src).sum(-1)
            ad_n = (h * a_dst).sum(-1)
            e = jax.nn.leaky_relu(as_n[src] + ad_n[dst], NEG_SLOPE)
            m = jax.ops.segment_max(e, dst, num_segments=N)
            p = jnp.exp(e - m[dst])
            s = jax.ops.segment_sum(p, dst, num_segments=N)
            alpha = p / (s[dst] + 1e-16)
            out = jax.ops.segment_sum(alpha[:, :, None] * h[src], dst, num_segments=N)
            return out.reshape(N, H * C) + b
        loops = jnp.arange(N, dtype=edge_index.dtype)
        src = jnp.concatenate([edge_index[0], loops])
        dst = jnp.concatenate([edge_index[1], loops])
        x1 = jax.nn.relu(x @ W_ah + b_ah)
        xs = [jax.nn.relu(gat_conv(x1, src, dst, W, a_s, a_d, b)) for W, a_s, a_d, b in ((W0, a_src0, a_dst0, b0), (W1, a_src1, a_dst1, b1), (W2, a_src2, a_dst2, b2))]
        node_emb = jnp.concatenate(xs, axis=1)
        return jax.nn.relu(node_emb @ W_out + b_out)

    def _L0_mix_ref(x, W_qkv, W_proj, b_proj):
        import jax, jax.numpy as jnp
        import numpy as np
        NUM_HEADS = 12
        DIM = 768
        HEAD_DIM = DIM // NUM_HEADS
        B, N, C = x.shape
        H, D = (NUM_HEADS, HEAD_DIM)
        qkv = x @ W_qkv.T
        qkv = qkv.reshape(B, N, 3, H, D).transpose(2, 0, 3, 1, 4)
        q, k, v = (qkv[0], qkv[1], qkv[2])
        q = jax.nn.elu(q) + 1.0
        k = jax.nn.elu(k) + 1.0
        k_sum = k.sum(axis=-2)
        kv = jnp.einsum('bhnd,bhne->bhde', k, v)
        numerator = jnp.einsum('bhnd,bhde->bhne', q, kv)
        denominator = jnp.einsum('bhnd,bhd->bhn', q, k_sum)
        out = numerator / (denominator[..., None] + 1e-06)
        out = out.transpose(0, 2, 1, 3).reshape(B, N, C)
        out = out @ W_proj.T + b_proj
        return out

    def _L0_ffn_ref(x, Wd, Wg, We, be, Wu, gamma):
        import jax, jax.numpy as jnp
        import numpy as np
        NUM_EXPERTS = 4
        TOPK = 1
        TEMPERATURE = 1.0
        NORM_TOPK_PROB = True
        N_CLS = 1
        N_REL = 4
        h = jax.nn.gelu(jnp.einsum('bnd,rd->bnr', x, Wd), approximate=False)
        cls_tok = h[:, :N_CLS, :]
        rel_tok = h[:, N_CLS:N_CLS + N_REL, :]
        t = h[:, N_CLS + N_REL:, :]
        B, N, r = t.shape
        logits = jnp.einsum('bnr,er->bne', t, Wg) / TEMPERATURE
        scores = jax.nn.softmax(logits, axis=-1)
        topk_w, topk_idx = jax.lax.top_k(scores, TOPK)
        if TOPK > 1 and NORM_TOPK_PROB:
            topk_w = topk_w / jnp.sum(topk_w, axis=-1, keepdims=True)
        expert_all = jnp.einsum('bnr,esr->bnes', t, We) + be
        idx_b = jnp.broadcast_to(topk_idx[..., None], (B, N, TOPK, r))
        sel = jnp.take_along_axis(expert_all, idx_b, axis=2)
        combine = jnp.sum(sel * topk_w[..., None], axis=2)
        full = jnp.concatenate([cls_tok, rel_tok, t + combine], axis=1)
        return jnp.einsum('bnr,dr->bnd', full, Wu) * gamma
    edge_index = jnp.stack([src, dst])
    batch0 = jnp.zeros((1250,), jnp.int32)
    xn = _layernorm(x, axis=-1)
    x = x + _L0_gnn_ref(xn, edge_index, batch0, edge_weight1, L0_gnn_W_ah, L0_gnn_b_ah, L0_gnn_W0, L0_gnn_a_src0, L0_gnn_a_dst0, L0_gnn_b0, L0_gnn_W1, L0_gnn_a_src1, L0_gnn_a_dst1, L0_gnn_b1, L0_gnn_W2, L0_gnn_a_src2, L0_gnn_a_dst2, L0_gnn_b2, L0_gnn_W_out, L0_gnn_b_out) + _L0_mix_ref(xn[None], L0_mix_W_qkv, L0_mix_W_proj, L0_mix_b_proj)[0]
    x = x + _L0_ffn_ref(_layernorm(x, axis=-1)[None], L0_ffn_Wd, L0_ffn_Wg, L0_ffn_We, L0_ffn_be, L0_ffn_Wu, L0_ffn_gamma)[0]
    return x

_drawn_inputs = setup_inputs


def setup_inputs(seed=0):
    import zlib

    import numpy as np

    out = dict(_drawn_inputs(seed))
    spreads = {'L0_gnn_b_ah': (0.0, 0.438),
     'L0_gnn_b0': (0.0, 0.286),
     'L0_gnn_b1': (0.0, 0.295),
     'L0_gnn_b2': (0.0, 0.299),
     'L0_gnn_b_out': (0.0, 0.1),
     'L0_ffn_gamma': (1.0, 0.2)}
    factors = {'L0_gnn_a_src0': 57.777,
     'L0_gnn_a_dst0': 64.0,
     'L0_gnn_a_src1': 64.0,
     'L0_gnn_a_dst1': 64.0,
     'L0_gnn_a_src2': 54.928,
     'L0_gnn_a_dst2': 64.0,
     'L0_mix_b_proj': 3.913,
     'L0_ffn_be': 8.0}
    for name, (base, spread) in spreads.items():
        noise = np.random.default_rng([zlib.crc32(name.encode()), seed]).standard_normal(out[name].shape)
        drawn = base * np.exp(spread * noise) if base else spread * noise
        out[name] = jnp.asarray(drawn.astype(out[name].dtype))
    for name, factor in factors.items():
        out[name] = (out[name] * factor).astype(out[name].dtype)
    return out
```

```python
from contextlib import ExitStack

import concourse.bass as bass
from concourse import mybir

F32 = mybir.dt.float32
BF16 = mybir.dt.bfloat16
FP16 = mybir.dt.float16
I16 = mybir.dt.int16
I32 = mybir.dt.int32
ALU = mybir.AluOpType
ACT = mybir.ActivationFunctionType
AX = mybir.AxisListType

N = 1250
P = 125
NT = N // P
D = 768
KT = D // 128
LAYERS = 3
HL = 4
C = D // HL
HEADS = LAYERS * HL
PAIRS = HEADS // 2
PC = 2 * C
PK = PC // 128
E = 20000
ET = E // P
CE = 4
CHUNKS = ET // CE
R = 64
EX = 4
CLS = 5
EPS = 1e-5
SLOPE = 0.2
BIG = 1e30
CH = [(0, 418), (418, 416), (834, 416)]
DH = 64


class Counter:

    def __init__(self, engine, sem):
        self.engine, self.sem, self.n = engine, sem, 0

    def done(self, instruction):
        self.n += 1
        instruction.then_inc(self.sem, 1)
        self.engine.wait_ge(self.sem, self.n)


def build(nc, x, src_t, dst_t, dst_c, w_ah, b_ah, w_gat, a_gat, w_pair, b_gat, w_out, b_out,
          w_qkv, w_proj, b_proj, w_down, w_route, b_exp, w_up, gamma, out):
    dram_a = nc.dram_tensor("scratch_a", (HEADS, N), F32, kind="Internal").ap()
    dram_uv = nc.dram_tensor("scratch_uv", (2 * HEADS, N), F32, kind="Internal").ap()
    dram_res = nc.dram_tensor("scratch_res", (NT, P, D), F32, kind="Internal").ap()
    ctx = ExitStack()
    with ctx:
        def sb(name, shape, dt=F32):
            return ctx.enter_context(nc.sbuf_tensor(name, shape, dt))

        r1 = sb("r1", [128, NT * D])
        r2 = sb("r2", [128, NT * 386 + 3 * N])
        r3 = sb("r3", [128, KT * N])
        cnt = sb("cnt", [P, NT, N], I16)
        r5 = sb("r5", [128, NT * N // 2])
        r6 = sb("r6", [128, 4 * N])
        r7 = sb("r7", [128, 4 * N])
        r8 = sb("r8", [128, KT * D])
        ident = sb("ident", [128, 128])
        identb = sb("identb", [128, 128], BF16)
        ones = sb("ones", [128, DH])
        ab = sb("ab", [P, NT, 2 * HEADS])
        acol = sb("acol", [P, HEADS, NT])
        ncol = sb("ncol", [P, HEADS, NT])
        bah = sb("bah", [128, KT])
        bgat = sb("bgat", [128, PAIRS * PK])
        amax = sb("amax", [P, HEADS, NT])
        uv = sb("uv", [P, NT, 2 * HEADS])
        flag_row = sb("flag_row", [1, CHUNKS * NT], I32)

        psum = ctx.enter_context(nc.psum_tensor("psum", [128, 8 * 512], F32))

        def bank(b):
            return psum[:, 512 * b:512 * (b + 1)]

        xN = r1[0:P, :].rearrange("p (t d) -> p t d", t=NT)
        yT = r1[:, 0:KT * N].rearrange("p (k n) -> p k n", k=KT)
        acc = xN
        xnT = r2[:, 0:KT * N].rearrange("p (k n) -> p k n", k=KT)
        hN = r2[0:P, 0:NT * 386].rearrange("p (t h c) -> p t h c", t=NT, h=2)
        xlT = r2[:, NT * 386:NT * 386 + PK * N].rearrange("p (k n) -> p k n", k=PK)
        x1T = r3[:, :].rearrange("p (k n) -> p k n", k=KT)
        xn2T = x1T
        mask = r5[0:P, :].bitcast(BF16).rearrange("p (t n) -> p t n", t=NT)
        gN = r5[0:P, 0:NT * PC].rearrange("p (t c) -> p t c", t=NT)

        front(nc, locals())
        attention(nc, locals())
        convolutions(nc, locals())
        adapter(nc, locals())


def front(nc, g):
    r1, r6, r7, r8 = g["r1"], g["r6"], g["r7"], g["r8"]
    xN, xnT, x1T, cnt, mask, ab, acol, ncol = (g[k] for k in "xN xnT x1T cnt mask ab acol ncol".split())
    ident, identb, ones, bank, psum = (g[k] for k in "ident identb ones bank psum".split())
    with ExitStack() as ctx:
        def sb(name, shape, dt=F32):
            return ctx.enter_context(nc.sbuf_tensor(name, shape, dt))

        def sem(name):
            return ctx.enter_context(nc.semaphore(name))

        wah = r8[:, :].rearrange("p (k c) -> p k c", k=KT)
        wl = r7[:, 0:KT * D].rearrange("p (k c) -> p k c", k=KT)
        a_bc = r6[:, 0:2 * D].rearrange("p (s c) -> p s c", s=2)
        prod = r6[:, 2 * D:2 * D + C]
        hot_src = r6[0:P, 0:CE * N // 2].bitcast(BF16).rearrange("p (e n) -> p e n", e=CE)
        hot_dst = r6[0:P, CE * N // 2:CE * N // 2 + CE * 64].bitcast(BF16).rearrange("p (e n) -> p e n", e=CE)
        zero = r6[0:P, 3000:3256].bitcast(BF16)
        node_i = r6[0:P, 3400:3400 + N].bitcast(I32)
        aT = r7[0:HEADS, 0:N]
        node_id = r7[0:P, 1300:1300 + N // 2].bitcast(FP16)
        some = [r7[0:P, 2000 + 700 * i:2000 + 700 * i + N // 2].bitcast(BF16) for i in range(2)]
        wa = sb("wa", [128, KT, 2 * HEADS])
        spare = sb("spare", [1, 1])
        src_i, dst_i = sb("src_i", [P, ET], I32), sb("dst_i", [P, ET], I32)
        src_f, dst_f = sb("src_f", [P, ET]), sb("dst_f", [P, ET])
        chunk_i = r6[0:CHUNKS, 2200:2200 + CE * P].bitcast(I32)
        chunk_f = r6[0:CHUNKS, 2700:2700 + CE * P]
        ends = sb("ends", [CHUNKS, 2])
        starts_i, starts = sb("starts_i", [CHUNKS, NT], I32), sb("starts", [CHUNKS, NT])
        below = sb("below", [CHUNKS, NT])
        flags = sb("flags", [CHUNKS, NT], I32)
        stats = sb("stats", [P, 2, 2, 6])
        moments = sb("moments", [P, NT, 2])
        rstd, std, eps = sb("rstd", [P, NT]), sb("std", [P, NT]), sb("eps", [P, 1])

        x_in = [sem(f"x_in{t}") for t in range(NT)]
        edges_in, wah_in, bias_in, wl_in, flags_in = (sem(s) for s in "edges_in wah_in bias_in wl_in flags_in".split())
        const_ready, wl_used, flags_ready, scores_out = (sem(s) for s in "const_ready wl_used flags_ready scores_out".split())
        xn_ready, xt_full, xt_free, x1_full, x1_free = (sem(s) for s in "xn_ready xt_full xt_free x1_full x1_free".split())
        wa_ready, ab_full, at_full, at_ready = (sem(s) for s in "wa_ready ab_full at_full at_ready".split())
        hot_ready, hot_free, cnt_full, cnt_free = (sem(s) for s in "hot_ready hot_free cnt_full cnt_free".split())
        some_ready, some_full, some_free, dve_own, pool_own = (
            sem(s) for s in "some_ready some_full some_free dve_own pool_own".split())
        eps_ready = sem("eps_ready")
        node_ready, var_ready, std_ready = sem("node_ready"), sem("var_ready"), sem("std_ready")
        block = ctx.enter_context(nc.Block())

        @block.sync
        def _(sp):
            for t in range(NT):
                sp.dma_start(xN[:, t, :], g["x"][t * P:(t + 1) * P, :]).then_inc(x_in[t], 16)
                if t == 1:
                    sp.dma_start(chunk_i, g["dst_c"]).then_inc(edges_in, 16)
                    sp.dma_start(src_i[:, :], g["src_t"]).then_inc(edges_in, 16)
                    sp.dma_start(dst_i[:, :], g["dst_t"]).then_inc(edges_in, 16)
            sp.dma_start(wah, g["w_ah"]).then_inc(wah_in, 16)
            sp.dma_start(g["bah"][:, :], g["b_ah"]).then_inc(bias_in, 16)
            sp.dma_start(g["bgat"][:, :], g["b_gat"]).then_inc(bias_in, 16)
            for layer in range(LAYERS):
                if layer:
                    sp.wait_ge(wl_used, layer)
                sp.dma_start(wl, g["w_gat"][layer]).then_inc(wl_in, 16)
                sp.dma_start(a_bc, g["a_gat"][layer].partition_broadcast(128)).then_inc(wl_in, 16)
            sp.wait_ge(flags_ready, 1)
            sp.dma_start(g["flag_row"][0:1, :], flags[:, :]).then_inc(flags_in, 16)
            sp.wait_ge(at_ready, len(CH))
            sp.dma_start(g["dram_a"], aT).then_inc(scores_out, 16)
            sp.wait_ge(scores_out, 16)
            sp.wait_ge(bias_in, 32)
            sp.wait_ge(flags_in, 16)

        @block.gpsimd
        def _(pool):
            own = Counter(pool, pool_own)
            nc.gpsimd.iota(starts_i[:, :], pattern=[[P, NT]], base=0, channel_multiplier=0).then_inc(const_ready, 1)
            own.done(nc.gpsimd.memset(ident[:, :], 0.0))
            nc.gpsimd.affine_select(out=ident[:, :], in_=ident[:, :], compare_op=ALU.not_equal, fill=1.0,
                                    base=0, pattern=[[-1, 128]], channel_multiplier=1).then_inc(const_ready, 1)
            pool.wait_ge(const_ready, 2)
            nc.gpsimd.tensor_copy(identb[:, :], ident[:, :]).then_inc(const_ready, 1)
            nc.gpsimd.memset(ones[:, :], 1.0).then_inc(const_ready, 1)
            pool.wait_ge(wl_used, LAYERS)
            nc.gpsimd.iota(node_i, pattern=[[1, N]], base=0, channel_multiplier=0).then_inc(node_ready, 1)
            nc.gpsimd.memset(zero, 0.0).then_inc(node_ready, 1)

        @block.vector
        def _(dve):
            own = Counter(dve, dve_own)
            nc.vector.memset(eps[:, :], EPS).then_inc(eps_ready, 1)

            def statistics(t):
                dve.wait_ge(x_in[t], 16)
                nc.vector.bn_stats(stats[:, t % 2, 0, :], xN[:, t, 0:D // 2]).then_inc(dve_own, 1)
                own.n += 1
                own.done(nc.vector.bn_stats(stats[:, t % 2, 1, :], xN[:, t, D // 2:D]))
                nc.vector.bn_aggr(moments[:, t, :], stats[:, t % 2, :, :]).then_inc(var_ready, 1)

            statistics(0)
            for t in range(NT):
                if t + 1 < NT:
                    statistics(t + 1)
                dve.wait_ge(std_ready, t + 1)
                own.done(nc.vector.reciprocal(rstd[:, t:t + 1], std[:, t:t + 1]))
                nc.vector.tensor_scalar(xN[:, t, :], xN[:, t, :], moments[:, t, 0:1], rstd[:, t:t + 1],
                                        ALU.subtract, ALU.mult).then_inc(xn_ready, 1)
                if t == 2:
                    dve.wait_ge(edges_in, 48)
                    dve.wait_ge(const_ready, 1)
                    own.done(nc.vector.tensor_copy(chunk_f, chunk_i))
                    own.done(nc.vector.tensor_copy(src_f[:, :], src_i[:, :]))
                    own.done(nc.vector.tensor_copy(dst_f[:, :], dst_i[:, :]))
                    own.done(nc.vector.tensor_copy(starts[:, :], starts_i[:, :]))
                    own.done(nc.vector.tensor_reduce(ends[:, 0:1], chunk_f, axis=AX.X, op=ALU.min))
                    own.done(nc.vector.tensor_reduce(ends[:, 1:2], chunk_f, axis=AX.X, op=ALU.max))
                    own.done(nc.vector.tensor_scalar(below[:, :], starts[:, :], float(P), ends[:, 0:1], ALU.add, ALU.is_gt))
                    nc.vector.scalar_tensor_tensor(flags[:, :], starts[:, :], ends[:, 1:2], below[:, :],
                                                   op0=ALU.is_le, op1=ALU.mult).then_inc(flags_ready, 1)
            for layer in range(LAYERS):
                dve.wait_ge(wl_in, 32 * (layer + 1))
                for k in range(KT):
                    for s in range(2):
                        for h in range(HL):
                            at = s * HEADS + layer * HL + h
                            last = nc.vector.tensor_tensor_reduce(
                                out=prod, in0=wl[:, k, h * C:(h + 1) * C], in1=a_bc[:, s, h * C:(h + 1) * C],
                                scale=1.0, scalar=0.0, op0=ALU.mult, op1=ALU.add, accum_out=wa[:, k, at:at + 1])
                            own.done(last)
                nc.vector.tensor_copy(prod[:, 0:1], ident[:, 0:1]).then_inc(wl_used, 1)
            dve.wait_ge(wl_used, LAYERS)
            nc.vector.tensor_copy(prod[:, 1:2], ident[:, 0:1]).then_inc(wa_ready, 1)
            dve.wait_ge(node_ready, 1)
            own.done(nc.vector.tensor_copy(node_id, node_i))
            dve.sem_inc(hot_free, CE)
            dve.wait_ge(flags_in, 16)
            units = dve.alloc_register("dve_units")
            dve.reg_mov(units, 0)
            with dve.Fori(0, NT) as it:
                with dve.Fori(0, CHUNKS) as c:
                    reaches = dve.value_load(g["flag_row"][0:1, bass.ds(c * NT + it, 1)], min_val=0, max_val=1)
                    with dve.If(reaches == 1):
                        for e in range(CE):
                            dve.reg_add(units, units, 1)
                            dve.wait_ge(hot_free, dve.snap(units))
                            nc.vector.tensor_scalar(hot_dst[:, e, 0:P], node_id[:, bass.ds(it * P, P)],
                                                    dst_f[:, bass.ds(c * CE + e, 1)], None, ALU.is_equal)\
                                .then_inc(hot_ready, 1)
                            nc.vector.tensor_scalar(hot_src[:, e, :], node_id, src_f[:, bass.ds(c * CE + e, 1)],
                                                    None, ALU.is_equal).then_inc(hot_ready, 1)
            for j in range(NT):
                dve.wait_ge(cnt_free, 1 + 4 * NT)
                if j >= 2:
                    dve.wait_ge(some_full, 2 * (j - 1))
                nc.vector.tensor_scalar(some[j % 2], cnt[:, j, :], 1.0, None, ALU.min).then_inc(some_ready, 1)
            dve.wait_ge(ab_full, 1)
            own.done(nc.vector.tensor_copy(ab[:, :, :], bank(7)[0:P, 0:NT * 2 * HEADS].rearrange("p (t h) -> p t h", t=NT)))
            own.done(nc.vector.tensor_copy(acol[:, :, :], ab[:, :, 0:HEADS].rearrange("p t h -> p h t")))
            own.done(nc.vector.tensor_scalar(ncol[:, :, :], acol[:, :, :], SLOPE - 1.0, None, ALU.mult))

        @block.scalar
        def _(act):
            def deviation(t):
                act.wait_ge(var_ready, t + 1)
                nc.scalar.activation(std[:, t:t + 1], moments[:, t, 1:2], ACT.Sqrt, bias=eps[:, :]).then_inc(std_ready, 1)

            act.wait_ge(eps_ready, 1)
            deviation(0)
            for i in range(2 * NT):
                t, half = i // 2, i % 2
                if half == 0 and t + 1 < NT:
                    deviation(t + 1)
                act.wait_ge(xt_full, i + 1)
                nc.scalar.activation(xnT[:, 3 * half:3 * half + 3, t * P:(t + 1) * P],
                                     bank(i % 4)[:, 0:3 * P].rearrange("p (k n) -> p k n", k=3), ACT.Copy)\
                    .then_inc(xt_free, 1)
            act.wait_ge(bias_in, 32)
            for i in range(KT * 3):
                o, (at, n) = i // 3, CH[i % 3]
                act.wait_ge(x1_full, i + 1)
                nc.scalar.activation(x1T[:, o, at:at + n], bank(4 + i % 3)[:, 0:n], ACT.Relu,
                                     bias=g["bah"][:, o:o + 1]).then_inc(x1_free, 1)
            act.wait_ge(wl_used, LAYERS)
            for i, (at, n) in enumerate(CH):
                act.wait_ge(at_full, i + 1)
                nc.scalar.activation(aT[:, at:at + n], bank(4 + i)[0:HEADS, 0:n], ACT.Copy).then_inc(at_ready, 1)
            act.sem_inc(cnt_free, 1)
            with act.Fori(0, NT) as it:
                act.wait_ge(cnt_full, it + 1)
                nc.scalar.activation(spare[:, :], eps[0:1, :], ACT.Copy).then_inc(cnt_free, 1)
                for b, tiles in enumerate((4, 4, 2)):
                    nc.scalar.activation(cnt[:, 4 * b:4 * b + tiles, bass.ds(it * P, P)],
                                         bank(b)[0:P, 0:128 * tiles].rearrange("p (j n) -> p j n", n=128)[:, :, 0:P],
                                         ACT.Copy).then_inc(cnt_free, 1)
            for i in range(2 * NT):
                j, half = i // 2, i % 2
                act.wait_ge(some_full, i + 1)
                nc.scalar.activation(mask[:, 5 * half:5 * half + 5, j * P:(j + 1) * P],
                                     bank(3 + i % 4)[0:P, :].bitcast(BF16)[:, 0:640].rearrange("p (t n) -> p t n", n=128)[:, :, 0:P],
                                     ACT.Copy, scale=BIG, bias=-BIG).then_inc(some_free, 1)

        @block.tensor
        def _(pe):
            pe.wait_ge(const_ready, 4)
            for i in range(2 * NT):
                t, half = i // 2, i % 2
                if not half:
                    pe.wait_ge(xn_ready, t + 1)
                if i >= 4:
                    pe.wait_ge(xt_free, i - 3)
                for k in range(3):
                    f = 3 * half + k
                    last = nc.tensor.transpose(bank(i % 4)[:, k * P:(k + 1) * P], xN[:, t, f * 128:(f + 1) * 128],
                                               ident[0:P, 0:P])
                last.then_inc(xt_full, 1)
            pe.wait_ge(xt_free, 2 * NT)
            pe.wait_ge(wah_in, 16)
            for i in range(KT * 3):
                o, (at, n) = i // 3, CH[i % 3]
                if i >= 3:
                    pe.wait_ge(x1_free, i - 2)
                for k in range(KT):
                    last = nc.tensor.matmul(bank(4 + i % 3)[:, 0:n], wah[:, k, o * 128:(o + 1) * 128],
                                            xnT[:, k, at:at + n], start=k == 0, stop=k == KT - 1)
                last.then_inc(x1_full, 1)
            pe.wait_ge(x1_free, KT * 3)
            pe.wait_ge(wa_ready, 1)
            for t in range(NT):
                for k in range(KT):
                    last = nc.tensor.matmul(bank(7)[0:P, t * 2 * HEADS:(t + 1) * 2 * HEADS],
                                            x1T[:, k, t * P:(t + 1) * P], wa[:, k, :], start=k == 0, stop=k == KT - 1)
            last.then_inc(ab_full, 1)
            for i, (at, n) in enumerate(CH):
                for k in range(KT):
                    last = nc.tensor.matmul(bank(4 + i)[0:HEADS, 0:n], wa[:, k, 0:HEADS], x1T[:, k, at:at + n],
                                            start=k == 0, stop=k == KT - 1)
                last.then_inc(at_full, 1)
            pe.wait_ge(node_ready, 2)
            pe.wait_ge(flags_in, 16)
            units = pe.alloc_register("pe_units")
            pe.reg_mov(units, 0)
            with pe.Fori(0, NT) as it:
                pe.wait_ge(cnt_free, 4 * it + 1)
                for b, n in enumerate((512, 512, 256)):
                    nc.tensor.matmul(bank(b)[0:P, 0:n], zero[:, 0:P], zero[:, 0:1].to_broadcast([P, n]), start=True,
                                     stop=False, skip_group_check=True)
                with pe.Fori(0, CHUNKS) as c:
                    reaches = pe.value_load(g["flag_row"][0:1, bass.ds(c * NT + it, 1)], min_val=0, max_val=1)
                    with pe.If(reaches == 1):
                        for e in range(CE):
                            pe.reg_add(units, units, 2)
                            pe.wait_ge(hot_ready, pe.snap(units))
                            for j in range(NT):
                                last = nc.tensor.matmul(psum[0:P, 128 * j:128 * j + P], hot_src[:, e, j * P:(j + 1) * P],
                                                        hot_dst[:, e, 0:P], start=False, stop=False, skip_group_check=True)
                            last.then_inc(hot_free, 1)
                nc.tensor.matmul(psum[0:P, bass.ds(it * 128, P)], identb[0:P, 0:P], identb[0:P, 0:P], start=False,
                                 stop=True, skip_group_check=True).then_inc(cnt_full, 1)
            for i in range(2 * NT):
                j, half = i // 2, i % 2
                if not half:
                    pe.wait_ge(some_ready, j + 1)
                if i >= 4:
                    pe.wait_ge(some_free, i - 3)
                if i < 4:
                    pe.wait_ge(at_ready, len(CH))
                for k in range(5):
                    t = 5 * half + k
                    last = nc.tensor.transpose(bank(3 + i % 4)[0:P, :].bitcast(BF16)[:, 128 * k:128 * k + P],
                                               some[j % 2][:, t * P:(t + 1) * P], identb[0:P, 0:P])
                last.then_inc(some_full, 1)


def attention(nc, g):
    r6, r7, r8 = g["r6"], g["r7"], g["r8"]
    xnT, yT, mask, ab, amax, uv, ident, ones, bank = (g[k] for k in "xnT yT mask ab amax uv ident ones bank".split())
    with ExitStack() as ctx:
        def sb(name, shape, dt=F32):
            return ctx.enter_context(nc.sbuf_tensor(name, shape, dt))

        def sem(name):
            return ctx.enter_context(nc.semaphore(name))

        kf = r6[0:P, 0:NT * 128].rearrange("p (t c) -> p t c", t=NT)
        vf = r6[0:P, NT * 128:NT * 257].rearrange("p (t c) -> p t c", t=NT)
        qf = r6[:, NT * 257:NT * 257 + N]
        ke = r6[0:P, 3840:3840 + 512].rearrange("p (s t c) -> p s t c", s=2, t=2)
        arow = [r7[0:P, i * N:(i + 1) * N] for i in range(2)]
        qe = r7[:, 2 * N:3 * N]
        junk = r7[0:P, 3 * N:3 * N + 640].bitcast(BF16)
        den = r7[:, 3 * N + 640:3 * N + 640 + 418]
        wq = [r8[:, i * KT * 384:(i + 1) * KT * 384].rearrange("p (k c) -> p k c", k=KT) for i in range(2)]
        wproj = r8[:, :].rearrange("p (k c) -> p k c", k=KT)
        kvb, ksb = sb("kvb", [128, 128]), sb("ksb", [128, 128])
        ksum = sb("ksum", [128, 1])
        spare = sb("spare2", [1, 1])
        head_amax = sb("head_amax", [P, 2, NT])
        low = sb("low", [P, NT, HEADS])
        xt = [r6[0:P, i * D:(i + 1) * D] for i in range(3)]
        bp = r6[0:P, 3 * D:4 * D]
        uvT = r6[0:2 * HEADS, 4 * D:4 * D + N]

        w_in = [sem(f"w_in{i}") for i in range(2)]
        arow_in = [sem(f"arow_in{i}") for i in range(2)]
        x_in = [sem(f"xt_in{i}") for i in range(3)]
        res_out = [sem(f"res_out{i}") for i in range(3)]
        (proj_in, bp_in, kv_full, k_low, k_exp, k_ready, v_ready, q_full, q_low, q_exp, q_ready, acc_full, kvb_ready,
         num_full, y_ready, head_max, p_full, p_free, xb_ready, uv_ready, uvt_full, uvt_ready, uv_out, dve_own, zeroed,
         ones_col, kv_mm) = (sem(s) for s in (
             "proj_in bp_in kv_full k_low k_exp k_ready v_ready q_full q_low q_exp q_ready acc_full kvb_ready num_full "
             "y_ready head_max p_full p_free xb_ready uv_ready uvt_full uvt_ready uv_out attn_own zeroed ones_col "
             "kv_mm").split())
        block = ctx.enter_context(nc.Block())
        KG = NT // 2

        @block.sync
        def _(sp):
            with sp.Fori(0, PAIRS // 2) as i2:
                for s in range(2):
                    i = i2 * 2 + s
                    sp.wait_ge(q_full, 1 + 3 * 2 * i2 + 0)
                    sp.dma_start(wq[s], g["w_qkv"][bass.ds(i, 1), :, :, :].rearrange("a p k c -> (a p) k c"))\
                        .then_inc(w_in[s], 16)
            sp.wait_ge(q_full, 1 + 3 * PAIRS)
            sp.dma_start(wproj, g["w_proj"]).then_inc(proj_in, 16)
            sp.wait_ge(y_ready, 1 + 3 * PAIRS)
            sp.dma_start(bp, g["b_proj"].partition_broadcast(P)).then_inc(bp_in, 16)
            for t in range(NT):
                if t >= 3:
                    sp.wait_ge(res_out[t % 3], 16 * (t // 3))
                sp.dma_start(xt[t % 3], g["x"][t * P:(t + 1) * P, :]).then_inc(x_in[t % 3], 16)
                if t >= 2:
                    sp.wait_ge(p_free, 2 * (t - 1))
                    sp.dma_start(g["dram_res"][t - 2], xt[(t - 2) % 3]).then_inc(res_out[(t - 2) % 3], 16)
            for t in (NT - 2, NT - 1):
                sp.wait_ge(p_free, 2 * (t + 1))
                sp.dma_start(g["dram_res"][t], xt[t % 3]).then_inc(res_out[t % 3], 16)
            for i in range(3):
                sp.wait_ge(res_out[i], 16 * len(range(i, NT, 3)))
            sp.wait_ge(uvt_ready, 3)
            sp.dma_start(g["dram_uv"], uvT).then_inc(uv_out, 16)
            sp.wait_ge(uv_out, 16)

        @block.gpsimd
        def _(pool):
            nc.gpsimd.memset(kvb[:, :], 0.0).then_inc(zeroed, 1)
            nc.gpsimd.memset(ksb[:, :], 0.0).then_inc(zeroed, 1)
            nc.gpsimd.memset(vf[:, :, 128:129], 1.0).then_inc(ones_col, 1)
            with pool.Fori(0, PAIRS) as i:
                for s in range(2):
                    pool.wait_ge(head_max, 1 + 2 * i)
                    pool.dma_start(arow[s], g["dram_a"][bass.ds(2 * i + s, 1), :].to_broadcast([P, N]))\
                        .then_inc(arow_in[s], 16)
            pool.wait_ge(bp_in, 16)
            for t in range(NT):
                pool.wait_ge(x_in[t % 3], 16 * (t // 3 + 1))
                nc.gpsimd.tensor_tensor(xt[t % 3], xt[t % 3], bp, ALU.add).then_inc(xb_ready, 1)

        @block.vector
        def _(dve):
            own = Counter(dve, dve_own)
            dve.wait_ge(zeroed, 2)
            with dve.Fori(0, PAIRS) as i:
                steps = [(s, t) for s in range(2) for t in range(NT)]
                link = [0]

                def chain(instruction):
                    link[0] += 1
                    instruction.then_inc(dve_own, 1)
                    dve.wait_ge(dve_own, i * LINKS_PER_PAIR + link[0])

                def maxima(n):
                    for _ in range(n):
                        s, t = steps.pop(0)
                        if t == 0:
                            dve.wait_ge(arow_in[s], 16 * (i + 1))
                            nc.vector.memset(spare[:, :], 0.0)
                        last = nc.vector.tensor_tensor_reduce(
                            out=junk[:, 0:N], in0=mask[:, t, :], in1=arow[s], scale=1.0, scalar=-3e38, op0=ALU.add,
                            op1=ALU.max, accum_out=head_amax[:, s, t:t + 1])
                        chain(last)
                        if steps:
                            nc.vector.memset(spare[:, :], 0.0)
                        if t == NT - 1:
                            nc.vector.tensor_copy(amax[:, bass.ds(2 * i + s, 1), :].rearrange("p a t -> p (a t)"),
                                                  head_amax[:, s, :]).then_inc(head_max, 1)
                            dve.wait_ge(head_max, 1 + 2 * i + s + 1)

                LINKS_PER_PAIR = 2 * NT + 1 + 2 * 3
                for gr in range(KG):
                    kb = bank(gr % 2)[0:P, :].rearrange("p (t c) -> p t c", t=2)
                    dve.wait_ge(kv_full, KG * i + gr + 1)
                    dve.wait_ge(k_ready, 1 + KG * i + gr)
                    nc.vector.tensor_scalar(ke[:, gr % 2, :, :], kb[:, :, 0:128], 0.0, None, ALU.min).then_inc(k_low, 1)
                    maxima(2)
                    dve.wait_ge(k_exp, KG * i + gr + 1)
                    nc.vector.scalar_tensor_tensor(kf[:, 2 * gr:2 * gr + 2, :], kb[:, :, 0:128], 1.0, ke[:, gr % 2, :, :],
                                                   op0=ALU.add, op1=ALU.max).then_inc(k_ready, 1)
                for c, (at, n) in enumerate(CH):
                    dve.wait_ge(q_full, 1 + 3 * i + c + 1)
                    nc.vector.tensor_scalar(qe[:, at:at + n], bank(2 + c)[:, 0:n], 0.0, None, ALU.min).then_inc(q_low, 1)
                    maxima(2)
                    dve.wait_ge(q_exp, 3 * i + c + 1)
                    nc.vector.scalar_tensor_tensor(qf[:, at:at + n], bank(2 + c)[:, 0:n], 1.0, qe[:, at:at + n],
                                                   op0=ALU.add, op1=ALU.max).then_inc(q_ready, 1)
                dve.wait_ge(acc_full, i + 1)
                for h in range(2):
                    b = slice(DH * h, DH * (h + 1))
                    nc.vector.tensor_copy(kvb[b, b], bank(5)[b, b]).then_inc(kvb_ready, 1)
                chain(nc.vector.tensor_copy(ksum[:, :], bank(5)[:, 128:129]))
                for h in range(2):
                    b = slice(DH * h, DH * (h + 1))
                    nc.vector.tensor_scalar(ksb[b, b], ones[b, :], ksum[b, :], None, ALU.mult).then_inc(kvb_ready, 1)
                maxima(4)
                for c, (at, n) in enumerate(CH):
                    dve.wait_ge(num_full, 3 * i + c + 1)
                    chain(nc.vector.tensor_scalar(den[:, 0:n], bank(7)[:, 0:n], 1e-6, None, ALU.add))
                    chain(nc.vector.reciprocal(den[:, 0:n], den[:, 0:n]))
                    nc.vector.tensor_tensor(yT[:, bass.ds(i, 1), at:at + n].rearrange("p a n -> p (a n)"),
                                            bank(6)[:, 0:n], den[:, 0:n], ALU.mult).then_inc(y_ready, 1)
                    dve.wait_ge(y_ready, 1 + 3 * i + c + 1)
                maxima(len(steps))
            own.n = PAIRS * LINKS_PER_PAIR
            b_, mx = ab[:, :, HEADS:2 * HEADS], amax[:, :, :].rearrange("p h t -> p t h")
            own.done(nc.vector.tensor_tensor(uv[:, :, 0:HEADS], b_, mx, ALU.add))
            own.done(nc.vector.scalar_tensor_tensor(low[:, :, :], uv[:, :, 0:HEADS], SLOPE, uv[:, :, 0:HEADS],
                                                    op0=ALU.mult, op1=ALU.max))
            own.done(nc.vector.tensor_tensor(uv[:, :, 0:HEADS], b_, low[:, :, :], ALU.subtract))
            nc.vector.scalar_tensor_tensor(uv[:, :, HEADS:2 * HEADS], b_, SLOPE, low[:, :, :],
                                           op0=ALU.mult, op1=ALU.subtract).then_inc(uv_ready, 1)
            for t in range(NT):
                dve.wait_ge(xb_ready, t + 1)
                for half in range(2):
                    c = slice(384 * half, 384 * (half + 1))
                    dve.wait_ge(p_full, 2 * t + half + 1)
                    nc.vector.tensor_tensor(xt[t % 3][:, c], xt[t % 3][:, c], bank((2 * t + half) % 4)[0:P, 0:384], ALU.add)\
                        .then_inc(p_free, 1)

        @block.scalar
        def _(act):
            with act.Fori(0, PAIRS) as i:
                for gr in range(KG):
                    kb = bank(gr % 2)[0:P, :].rearrange("p (t c) -> p t c", t=2)
                    act.wait_ge(k_low, KG * i + gr + 1)
                    nc.scalar.activation(ke[:, gr % 2, :, :], ke[:, gr % 2, :, :], ACT.Exp).then_inc(k_exp, 1)
                    act.wait_ge(k_ready, 1 + KG * i + gr + 1)
                    nc.scalar.activation(vf[:, 2 * gr:2 * gr + 2, 0:128], kb[:, :, 128:256], ACT.Copy).then_inc(v_ready, 1)
                for c, (at, n) in enumerate(CH):
                    act.wait_ge(q_low, 3 * i + c + 1)
                    nc.scalar.activation(qe[:, at:at + n], qe[:, at:at + n], ACT.Exp).then_inc(q_exp, 1)
            for b, (t0, n) in enumerate(((0, 4), (4, 4), (8, 2))):
                act.wait_ge(uvt_full, b + 1)
                if b == 0:
                    act.wait_ge(y_ready, 1 + 3 * PAIRS)
                nc.scalar.activation(uvT[:, t0 * P:(t0 + n) * P].rearrange("p (t n) -> p t n", t=n),
                                     bank(4 + b)[0:2 * HEADS, 0:128 * n].rearrange("p (t n) -> p t n", t=n)[:, :, 0:P],
                                     ACT.Copy).then_inc(uvt_ready, 1)

        @block.tensor
        def _(pe):
            for s in (q_full, head_max, k_ready, v_ready, q_ready, kvb_ready, y_ready):
                pe.sem_inc(s, 1)
            pe.wait_ge(ones_col, 1)
            with pe.Fori(0, PAIRS // 2) as i2:
                for s in range(2):
                    i = i2 * 2 + s
                    pe.wait_ge(w_in[s], 16 * (i2 + 1))
                    for gr in range(KG):
                        if gr >= 2:
                            pe.wait_ge(v_ready, 1 + KG * i + gr - 1)
                        else:
                            pe.wait_ge(v_ready, 1 + KG * i)
                        for t in range(2):
                            nt = 2 * gr + t
                            for k in range(KT):
                                last = nc.tensor.matmul(bank(gr % 2)[0:P, 256 * t:256 * (t + 1)],
                                                        xnT[:, k, nt * P:(nt + 1) * P], wq[s][:, k, 128:384],
                                                        start=k == 0, stop=k == KT - 1)
                        last.then_inc(kv_full, 1)
                    for c, (at, n) in enumerate(CH):
                        pe.wait_ge(q_ready, 1 + 3 * i)
                        for k in range(KT):
                            last = nc.tensor.matmul(bank(2 + c)[:, 0:n], wq[s][:, k, 0:128], xnT[:, k, at:at + n],
                                                    start=k == 0, stop=k == KT - 1)
                        last.then_inc(q_full, 1)
                    pe.wait_ge(v_ready, 1 + KG * (i + 1))
                    pe.wait_ge(k_ready, 1 + KG * (i + 1))
                    pe.wait_ge(kvb_ready, 1 + 4 * i)
                    for t in range(NT):
                        last = nc.tensor.matmul(bank(5)[:, 0:129], kf[:, t, :], vf[:, t, :], start=t == 0, stop=t == NT - 1)
                    last.then_inc(acc_full, 1)
                    pe.wait_ge(kvb_ready, 1 + 4 * (i + 1))
                    for c, (at, n) in enumerate(CH):
                        pe.wait_ge(q_ready, 1 + 3 * i + c + 1)
                        pe.wait_ge(y_ready, 1 + 3 * i + c)
                        nc.tensor.matmul(bank(7)[:, 0:n], ksb[:, :], qf[:, at:at + n], start=True, stop=True)
                        nc.tensor.matmul(bank(6)[:, 0:n], kvb[:, :], qf[:, at:at + n], start=True, stop=True)\
                            .then_inc(num_full, 1)
            pe.wait_ge(y_ready, 1 + 3 * PAIRS)
            pe.wait_ge(proj_in, 16)
            for t in range(NT):
                for half in range(2):
                    i = 2 * t + half
                    if i >= 4:
                        pe.wait_ge(p_free, i - 3)
                    for k in range(KT):
                        last = nc.tensor.matmul(bank(i % 4)[0:P, 0:384], yT[:, k, t * P:(t + 1) * P],
                                                wproj[:, k, 384 * half:384 * (half + 1)], start=k == 0, stop=k == KT - 1)
                    last.then_inc(p_full, 1)
            pe.wait_ge(uv_ready, 1)
            for b, (t0, n) in enumerate(((0, 4), (4, 4), (8, 2))):
                for t in range(n):
                    last = nc.tensor.transpose(bank(4 + b)[0:2 * HEADS, 128 * t:128 * t + P], uv[:, t0 + t, :], ident[0:P, 0:P])
                last.then_inc(uvt_full, 1)


def convolutions(nc, g):
    r6, r7, r8 = g["r6"], g["r7"], g["r8"]
    acc, x1T, hN, xlT, gN, cnt, acol, ncol, bgat, ident, bank = (
        g[k] for k in "acc x1T hN xlT gN cnt acol ncol bgat ident bank".split())
    with ExitStack() as ctx:
        def sb(name, shape, dt=F32):
            return ctx.enter_context(nc.sbuf_tensor(name, shape, dt))

        def sem(name):
            return ctx.enter_context(nc.semaphore(name))

        RING = 4
        prob = [r6[0:P, i * N:(i + 1) * N] for i in range(RING)]
        urow = [r7[0:P, 2 * i * N:(2 * i + 1) * N] for i in range(2)]
        vrow = [r7[0:P, (2 * i + 1) * N:(2 * i + 2) * N] for i in range(2)]
        wp = r8[:, 0:KT * PC].rearrange("p (k c) -> p k c", k=KT)
        wo = r8[:, KT * PC:KT * PC + PK * D].rearrange("p (k c) -> p k c", k=PK)
        bo = sb("bo", [P, D])
        a_pair, b_pair = sb("a_pair", [P, 2, NT]), sb("b_pair", [128, PK])
        pair_ready = sem("pair_ready")
        total = sb("total", [P, 5, 2])
        rows_in = [sem(f"rows_in{i}") for i in range(2)]
        (wp_in, wo_in, bo_in, acc_init, ones_col, h_full, h_ready, z_ready, e_ready, prob_ready, prob_free, sum_full,
         sum_free, g_ready, t_full, t_ready, o_full, o_free, total_own) = (sem(s) for s in (
             "wp_in wo_in bo_in acc_init h_ones h_full h_ready z_ready e_ready prob_ready prob_free sum_full sum_free "
             "g_ready t_full t_ready o_full o_free total_own").split())
        block = ctx.enter_context(nc.Block())
        TILES = 2 * NT
        TG = [(k, t0, n) for k in range(PK) for t0, n in ((0, 4), (4, 4), (8, 2))]
        HT, TT, OT = NT, len(TG), 2 * NT

        @block.sync
        def _(sp):
            sp.dma_start(bo[:, :], g["b_out"].partition_broadcast(P)).then_inc(bo_in, 16)
            with sp.Fori(0, PAIRS) as i:
                sp.wait_ge(h_full, 1 + HT * i)
                sp.dma_start(wp, g["w_pair"][bass.ds(i, 1), :, :, :].rearrange("a p k c -> (a p) k c")).then_inc(wp_in, 16)
                for s in range(2):
                    sp.wait_ge(z_ready, 1 + TILES * i)
                    for row, off in ((urow[s], 0), (vrow[s], HEADS)):
                        sp.dma_start(row, g["dram_uv"][bass.ds(2 * i + s + off, 1), :].to_broadcast([P, N]))\
                            .then_inc(rows_in[s], 16)
                sp.wait_ge(o_full, 1 + OT * i)
                sp.dma_start(wo, g["w_out"][bass.ds(i, 1), :, :, :].rearrange("a p k c -> (a p) k c")).then_inc(wo_in, 16)

        @block.gpsimd
        def _(pool):
            nc.gpsimd.memset(hN[:, :, :, C:C + 1], 1.0).then_inc(ones_col, 1)
            pool.wait_ge(bo_in, 16)
            for t in range(NT):
                nc.gpsimd.tensor_copy(acc[:, t, :], bo[:, :]).then_inc(acc_init, 1)

        @block.vector
        def _(dve):
            dve.sem_inc(prob_free, 3)
            dve.wait_ge(acc_init, NT)
            with dve.Fori(0, PAIRS) as i:
                chain = [0]

                def own(instruction):
                    chain[0] += 1
                    instruction.then_inc(total_own, 1)
                    dve.wait_ge(total_own, i * 20 + chain[0])

                def scores(n):
                    s, j = n // NT, n % NT
                    if j == 0:
                        dve.wait_ge(rows_in[s], 32 * (i + 1))
                    used = (n - RING) % TILES
                    if used % NT == NT - 1:
                        dve.wait_ge(sum_full, 1 + (10 * i + (0 if n < RING else 5)))
                    else:
                        dve.wait_ge(prob_free, (TILES - 2) * i + (1 + n if n < RING else 4 + used - used // NT))
                    nc.vector.scalar_tensor_tensor(
                        prob[n % RING], vrow[s], ncol[:, bass.ds(2 * i + s, 1), j:j + 1].rearrange("p a t -> p (a t)"),
                        urow[s], op0=ALU.add, op1=ALU.max).then_inc(z_ready, 1)

                def weigh(n):
                    dve.wait_ge(e_ready, TILES * i + n + 1)
                    nc.vector.scalar_tensor_tensor(prob[n % RING], prob[n % RING], 1.0, cnt[:, n % NT, :],
                                                   op0=ALU.min, op1=ALU.mult).then_inc(prob_ready, 1)

                def normalise(s):
                    for b in range(5):
                        dve.wait_ge(sum_full, 1 + 10 * i + 5 * s + b + 1)
                        both = bank(b)[0:P, 0:386].rearrange("p (t c) -> p t c", t=2)
                        own(nc.vector.tensor_scalar(total[:, b, :], both[:, :, C], 1e-16, None, ALU.add))
                        own(nc.vector.reciprocal(total[:, b, :], total[:, b, :]))
                        for t in range(2):
                            nc.vector.tensor_scalar(gN[:, 2 * b + t, C * s:C * (s + 1)], both[:, t, 0:C],
                                                    total[:, b, t:t + 1], None, ALU.mult).then_inc(g_ready, 1)

                scores(0)
                for n in range(TILES):
                    if n + 1 < TILES:
                        scores(n + 1)
                    weigh(n)
                    if n == NT + 1:
                        normalise(0)
                normalise(1)
                for o in range(OT):
                    t, half = o // 2, o % 2
                    dve.wait_ge(o_full, 1 + OT * i + o + 1)
                    here = acc[:, t, 384 * half:384 * (half + 1)]
                    nc.vector.tensor_tensor(here, here, bank(5 + (HT + TT + o) % 3)[0:P, 0:384], ALU.add).then_inc(o_free, 1)
                dve.wait_ge(o_free, 1 + OT * (i + 1))

        @block.scalar
        def _(act):
            act.wait_ge(ones_col, 1)
            with act.Fori(0, PAIRS) as i:
                for t in range(HT):
                    act.wait_ge(h_full, 1 + HT * i + t + 1)
                    nc.scalar.activation(hN[:, t, :, 0:C], bank(5 + t % 3)[0:P, 0:PC].rearrange("p (h c) -> p h c", h=2),
                                         ACT.Copy).then_inc(h_ready, 1)
                nc.scalar.activation(a_pair[:, :, :], acol[:, bass.ds(2 * i, 2), :], ACT.Copy).then_inc(pair_ready, 1)
                nc.scalar.activation(b_pair[:, :], bgat[:, bass.ds(PK * i, PK)], ACT.Copy).then_inc(pair_ready, 1)
                act.wait_ge(pair_ready, 2 * (i + 1))
                for n in range(TILES):
                    s, j = n // NT, n % NT
                    act.wait_ge(z_ready, 1 + TILES * i + n + 1)
                    nc.scalar.activation(prob[n % RING], prob[n % RING], ACT.Exp,
                                         bias=a_pair[:, s, j:j + 1])\
                        .then_inc(e_ready, 1)
                for m, (k, t0, n) in enumerate(TG):
                    act.wait_ge(t_full, TT * i + m + 1)
                    nc.scalar.activation(xlT[:, k, t0 * P:(t0 + n) * P], bank(5 + (HT + m) % 3)[:, 0:n * P], ACT.Relu,
                                         bias=b_pair[:, k:k + 1]).then_inc(t_ready, 1)

        @block.tensor
        def _(pe):
            for s in (h_full, z_ready, o_full, o_free, g_ready, sum_full):
                pe.sem_inc(s, 1)
            pe.wait_ge(ones_col, 1)
            with pe.Fori(0, PAIRS) as i:
                pe.wait_ge(wp_in, 16 * (i + 1))
                pe.wait_ge(o_free, 1 + OT * i)
                for t in range(HT):
                    if t >= 3:
                        pe.wait_ge(h_ready, HT * i + t - 2)
                    for k in range(KT):
                        last = nc.tensor.matmul(bank(5 + t % 3)[0:P, 0:PC], x1T[:, k, t * P:(t + 1) * P], wp[:, k, :],
                                                start=k == 0, stop=k == KT - 1)
                    last.then_inc(h_full, 1)
                pe.wait_ge(h_ready, HT * (i + 1))
                for s in range(2):
                    for j in range(NT):
                        n = NT * s + j
                        pe.wait_ge(prob_ready, TILES * i + n + 1)
                        for t in range(NT):
                            if j == 0 and t % 2 == 0:
                                pe.wait_ge(g_ready, 1 + (20 * i + 10 * s - 10 + t + 2 if s else 20 * i))
                            last = nc.tensor.matmul(bank(t // 2)[0:P, 193 * (t % 2):193 * (t % 2) + 193],
                                                    prob[n % RING][:, t * P:(t + 1) * P], hN[:, j, s, :],
                                                    start=j == 0 and t % 2 == 0, stop=j == NT - 1, skip_group_check=True)
                            if j == NT - 1 and t % 2:
                                last.then_inc(sum_full, 1)
                        if j < NT - 1:
                            last.then_inc(prob_free, 1)
                for m, (k, t0, n) in enumerate(TG):
                    if m < 3:
                        pe.wait_ge(h_ready, HT * (i + 1))
                    else:
                        pe.wait_ge(t_ready, TT * i + m - 2)
                    pe.wait_ge(g_ready, 1 + 20 * i + 10 + t0 + n)
                    for t in range(n):
                        last = nc.tensor.transpose(bank(5 + (HT + m) % 3)[:, t * P:(t + 1) * P],
                                                   gN[:, t0 + t, 128 * k:128 * (k + 1)], ident[0:P, 0:P])
                    last.then_inc(t_full, 1)
                pe.wait_ge(wo_in, 16 * (i + 1))
                pe.wait_ge(t_ready, TT * (i + 1))
                for o in range(OT):
                    t, half = o // 2, o % 2
                    if o >= 3:
                        pe.wait_ge(o_free, 1 + OT * i + o - 2)
                    for k in range(PK):
                        last = nc.tensor.matmul(bank(5 + (HT + TT + o) % 3)[0:P, 0:384], xlT[:, k, t * P:(t + 1) * P],
                                                wo[:, k, 384 * half:384 * (half + 1)], start=k == 0, stop=k == PK - 1)
                    last.then_inc(o_full, 1)


def adapter(nc, g):
    r2, r6, r7, r8 = g["r2"], g["r6"], g["r7"], g["r8"]
    acc, xn2T, ident, bank = (g[k] for k in "acc xn2T ident bank".split())
    with ExitStack() as ctx:
        def sb(name, shape, dt=F32):
            return ctx.enter_context(nc.sbuf_tensor(name, shape, dt))

        def sem(name):
            return ctx.enter_context(nc.semaphore(name))

        W = EX + EX * R
        xn = [r6[0:P, i * D:(i + 1) * D] for i in range(3)]
        res = [r7[0:P, i * D:(i + 1) * D] for i in range(4)]
        wd = r8[:, 0:KT * R].rearrange("p (k c) -> p k c", k=KT)
        wr = r8[0:R, 400:400 + W]
        wu = r8[0:R, 700:700 + D]
        gam = r8[0:R, 1500:1500 + D]
        be = r8[0:P, 2300:2300 + EX * R]
        fT = r8[0:R, 2600:2600 + N]
        le = r2[0:P, 0:NT * W].rearrange("p (t w) -> p t w", t=NT)
        pick = r2[0:P, NT * W:NT * W + NT * EX * R].rearrange("p (t e r) -> p t e r", t=NT, e=EX)
        comb = r2[0:P, 5300:5300 + NT * R].rearrange("p (t r) -> p t r", t=NT)
        best, total = sb("best", [P, NT]), sb("esum", [P, NT])
        hot, taken, el = sb("hot", [P, NT, EX]), sb("taken", [P, NT]), sb("el", [P, NT, EX])
        stats = sb("stats2", [P, 2, 2, 6])
        moments, rstd = sb("moments2", [P, NT, 2]), sb("rstd2", [P, NT])
        std, eps = sb("std2", [P, NT]), sb("eps2", [P, 1])
        res_in = [sem(f"res_in{i}") for i in range(4)]
        eps_ready = sem("eps2_ready")
        x2_ready, var_ready, std_ready = sem("x2_ready"), sem("var2_ready"), sem("std2_ready")
        (w_in, own_s, xn_ready, xt_full, xt_free, d_full, f_ready, r_full, r_free, el_ready, ex_ready, wu_ready,
         comb_ready, c_full, full_ready, up_full, y_ready, out_done) = (sem(s) for s in (
             "aw_in own2 xn2_ready xt2_full xt2_free d_full f_ready r_full r_free el_ready ex_ready wu_ready comb_ready "
             "c_full full_ready up_full ay_ready out_done").split())
        block = ctx.enter_context(nc.Block())

        @block.sync
        def _(sp):
            for t in range(NT):
                if t >= 4:
                    sp.wait_ge(x2_ready, t - 3)
                sp.dma_start(res[t % 4], g["dram_res"][t]).then_inc(res_in[t % 4], 16)
                if t == 3:
                    sp.dma_start(wd, g["w_down"]).then_inc(w_in, 16)
                    sp.dma_start(wr, g["w_route"]).then_inc(w_in, 16)
                    sp.dma_start(wu, g["w_up"]).then_inc(w_in, 16)
                    sp.dma_start(gam, g["gamma"].partition_broadcast(R)).then_inc(w_in, 16)
                    sp.dma_start(be, g["b_exp"].partition_broadcast(P)).then_inc(w_in, 16)
            for t in range(NT):
                sp.wait_ge(y_ready, 2 * (t + 1))
                sp.dma_start(g["out"][t * P:(t + 1) * P, :], acc[:, t, :]).then_inc(out_done, 16)
            sp.wait_ge(out_done, 16 * NT)

        @block.vector
        def _(dve):
            own = Counter(dve, own_s)
            nc.vector.memset(eps[:, :], EPS).then_inc(eps_ready, 1)


            def statistics(t):
                dve.wait_ge(res_in[t % 4], 16 * (t // 4 + 1))
                nc.vector.scalar_tensor_tensor(acc[:, t, :], acc[:, t, :], 0.0, res[t % 4], op0=ALU.max, op1=ALU.add)\
                    .then_inc(x2_ready, 1)
                dve.wait_ge(x2_ready, t + 1)
                nc.vector.bn_stats(stats[:, t % 2, 0, :], acc[:, t, 0:D // 2]).then_inc(own_s, 1)
                own.n += 1
                own.done(nc.vector.bn_stats(stats[:, t % 2, 1, :], acc[:, t, D // 2:D]))
                nc.vector.bn_aggr(moments[:, t, :], stats[:, t % 2, :, :]).then_inc(var_ready, 1)

            statistics(0)
            for t in range(NT):
                if t + 1 < NT:
                    statistics(t + 1)
                dve.wait_ge(std_ready, t + 1)
                own.done(nc.vector.reciprocal(rstd[:, t:t + 1], std[:, t:t + 1]))
                if t >= 3:
                    dve.wait_ge(xt_full, 2 * (t - 2))
                nc.vector.tensor_scalar(xn[t % 3], acc[:, t, :], moments[:, t, 0:1], rstd[:, t:t + 1],
                                        ALU.subtract, ALU.mult).then_inc(xn_ready, 1)
            dve.wait_ge(w_in, 80)
            nc.vector.tensor_tensor(wu, wu, gam, ALU.mult).then_inc(wu_ready, 1)
            dve.wait_ge(r_free, NT)
            logit = le[:, :, 0:EX]
            own.done(nc.vector.tensor_reduce(best[:, :], logit, axis=AX.X, op=ALU.max))
            best_b = best[:, :].unsqueeze(2).to_broadcast([P, NT, EX])
            nc.vector.tensor_tensor(el[:, :, :], logit, best_b, ALU.subtract).then_inc(el_ready, 1)
            own.done(nc.vector.tensor_tensor(hot[:, :, :], logit, best_b, ALU.is_ge))
            own.done(nc.vector.tensor_copy(taken[:, :], hot[:, :, 0]))
            for e in range(1, EX):
                own.done(nc.vector.tensor_tensor(hot[:, :, e], hot[:, :, e], taken[:, :], ALU.is_gt))
                if e < EX - 1:
                    own.done(nc.vector.tensor_tensor(taken[:, :], hot[:, :, e], taken[:, :], ALU.max))
            dve.wait_ge(ex_ready, 1)
            own.done(nc.vector.tensor_reduce(total[:, :], el[:, :, :], axis=AX.X, op=ALU.add))
            own.done(nc.vector.reciprocal(total[:, :], total[:, :]))
            own.done(nc.vector.memset(total[0:CLS, 0:1], 0.0))
            own.done(nc.vector.tensor_tensor(hot[:, :, :], hot[:, :, :], total[:, :].unsqueeze(2).to_broadcast([P, NT, EX]), ALU.mult))
            own.done(nc.vector.tensor_tensor(pick, le[:, :, EX:W].rearrange("p t (e r) -> p t e r", e=EX),
                                             be.rearrange("p (e r) -> p e r", e=EX).unsqueeze(1).to_broadcast([P, NT, EX, R]), ALU.add))
            own.done(nc.vector.tensor_tensor(pick, pick, hot[:, :, :].unsqueeze(3).to_broadcast([P, NT, EX, R]), ALU.mult))
            own.done(nc.vector.tensor_tensor(pick[:, :, 0:2, :], pick[:, :, 0:2, :], pick[:, :, 2:4, :], ALU.add))
            nc.vector.tensor_tensor(comb, pick[:, :, 0, :], pick[:, :, 1, :], ALU.add).then_inc(comb_ready, 1)
            for b, (t0, n) in enumerate(((0, 4), (4, 4), (8, 2))):
                dve.wait_ge(c_full, b + 1)
                here = fT[:, t0 * P:(t0 + n) * P]
                nc.vector.tensor_tensor(here, here, bank(b)[0:R, 0:n * P], ALU.add).then_inc(full_ready, 1)
            for t in range(NT):
                for half in range(2):
                    i = 2 * t + half
                    dve.wait_ge(up_full, i + 1)
                    here = acc[:, t, 384 * half:384 * (half + 1)]
                    nc.vector.tensor_tensor(here, here, bank(3 + i % 5)[0:P, 0:384], ALU.add).then_inc(y_ready, 1)

        @block.scalar
        def _(act):
            def deviation(t):
                act.wait_ge(var_ready, t + 1)
                nc.scalar.activation(std[:, t:t + 1], moments[:, t, 1:2], ACT.Sqrt, bias=eps[:, :]).then_inc(std_ready, 1)

            act.wait_ge(eps_ready, 1)
            deviation(0)
            for i in range(2 * NT):
                t, half = i // 2, i % 2
                if half == 0 and t + 1 < NT:
                    deviation(t + 1)
                act.wait_ge(xt_full, i + 1)
                nc.scalar.activation(xn2T[:, 3 * half:3 * half + 3, t * P:(t + 1) * P],
                                     bank(i % 4)[:, 0:3 * P].rearrange("p (k n) -> p k n", k=3), ACT.Copy).then_inc(xt_free, 1)
            for i, (at, n) in enumerate(CH):
                act.wait_ge(d_full, i + 1)
                nc.scalar.activation(fT[:, at:at + n], bank(4 + i)[0:R, 0:n], ACT.Gelu).then_inc(f_ready, 1)
            for t in range(NT):
                act.wait_ge(r_full, t + 1)
                nc.scalar.activation(le[:, t, :], bank(t % 4)[0:P, 0:W], ACT.Copy).then_inc(r_free, 1)
            act.wait_ge(el_ready, 1)
            nc.scalar.activation(el[:, :, :], el[:, :, :], ACT.Exp).then_inc(ex_ready, 1)

        @block.tensor
        def _(pe):
            for i in range(2 * NT):
                t, half = i // 2, i % 2
                if not half:
                    pe.wait_ge(xn_ready, t + 1)
                if i >= 4:
                    pe.wait_ge(xt_free, i - 3)
                for k in range(3):
                    f = 3 * half + k
                    last = nc.tensor.transpose(bank(i % 4)[:, k * P:(k + 1) * P], xn[t % 3][:, f * 128:(f + 1) * 128], ident[0:P, 0:P])
                last.then_inc(xt_full, 1)
            pe.wait_ge(xt_free, 2 * NT)
            pe.wait_ge(w_in, 80)
            for i, (at, n) in enumerate(CH):
                for k in range(KT):
                    last = nc.tensor.matmul(bank(4 + i)[0:R, 0:n], wd[:, k, :], xn2T[:, k, at:at + n], start=k == 0, stop=k == KT - 1)
                last.then_inc(d_full, 1)
            pe.wait_ge(f_ready, len(CH))
            for t in range(NT):
                if t >= 4:
                    pe.wait_ge(r_free, t - 3)
                nc.tensor.matmul(bank(t % 4)[0:P, 0:W], fT[:, t * P:(t + 1) * P], wr, start=True, stop=True).then_inc(r_full, 1)
            pe.wait_ge(comb_ready, 1)
            for b, (t0, n) in enumerate(((0, 4), (4, 4), (8, 2))):
                for t in range(n):
                    last = nc.tensor.transpose(bank(b)[0:R, t * P:(t + 1) * P], comb[:, t0 + t, :], ident[0:P, 0:P])
                last.then_inc(c_full, 1)
            pe.wait_ge(wu_ready, 1)
            for t in range(NT):
                if t in (0, 4, 8):
                    pe.wait_ge(full_ready, t // 4 + 1)
                for half in range(2):
                    i = 2 * t + half
                    if i >= 5:
                        pe.wait_ge(y_ready, i - 4)
                    nc.tensor.matmul(bank(3 + i % 5)[0:P, 0:384], fT[:, t * P:(t + 1) * P], wu[:, 384 * half:384 * (half + 1)],
                                     start=True, stop=True).then_inc(up_full, 1)


def kernel(**inputs):
    import numpy as np
    import concourse.bacc as bacc
    from concourse.bass_utils import run_bass_kernel_spmd

    a = {k: np.asarray(v) for k, v in inputs.items()}

    def tiles(w):
        return w.reshape(-1, 128, w.shape[-1]).transpose(1, 0, 2)

    gat = [a[f"L0_gnn_W{i}"] for i in range(LAYERS)]
    qkv = a["L0_mix_W_qkv"].T.reshape(KT, 128, 3, PAIRS, 128)
    data = {
        "x": a["x"],
        "src_t": a["src"].reshape(ET, P).T,
        "dst_t": a["dst"].reshape(ET, P).T,
        "dst_c": a["dst"].reshape(CHUNKS, CE * P),
        "w_ah": tiles(a["L0_gnn_W_ah"]),
        "b_ah": a["L0_gnn_b_ah"].reshape(KT, 128).T,
        "w_gat": np.stack([tiles(w) for w in gat]),
        "a_gat": np.stack([np.stack([a[f"L0_gnn_a_src{i}"].reshape(D), a[f"L0_gnn_a_dst{i}"].reshape(D)]) for i in range(LAYERS)]),
        "w_pair": np.stack([tiles(w[:, c:c + PC]) for w in gat for c in (0, PC)]),
        "b_gat": np.stack([a[f"L0_gnn_b{i}"] for i in range(LAYERS)]).reshape(PAIRS * PK, 128).T,
        "w_out": a["L0_gnn_W_out"].reshape(PAIRS, PK, 128, D).transpose(0, 2, 1, 3),
        "b_out": a["L0_gnn_b_out"],
        "w_qkv": qkv.transpose(3, 1, 0, 2, 4).reshape(PAIRS, 128, KT, 384),
        "w_proj": tiles(a["L0_mix_W_proj"].T),
        "b_proj": a["L0_mix_b_proj"],
        "w_down": tiles(a["L0_ffn_Wd"].T),
        "w_route": np.concatenate([a["L0_ffn_Wg"].T, a["L0_ffn_We"].reshape(EX * R, R).T], axis=1),
        "b_exp": a["L0_ffn_be"].reshape(EX * R),
        "w_up": a["L0_ffn_Wu"].T,
        "gamma": a["L0_ffn_gamma"],
    }
    nc = bacc.Bacc("TRN2", target_bir_lowering=False, num_devices=1)
    arrays, args = {}, []
    for name, v in data.items():
        arrays[f"in_{name}"] = np.ascontiguousarray(v)
        args.append(nc.dram_tensor(f"in_{name}", v.shape, mybir.dt.from_np(v.dtype), kind="ExternalInput").ap())
    args.append(nc.dram_tensor("out_0", (N, D), F32, kind="ExternalOutput").ap())
    build(nc, *args)
    r = run_bass_kernel_spmd(nc, [arrays], core_ids=[0])
    return r.results[0]["out_0"]
```

```python
from contextlib import ExitStack

import concourse.bass as bass
from concourse import mybir

F32 = mybir.dt.float32
F32R = mybir.dt.float32r
BF16 = mybir.dt.bfloat16
FP16 = mybir.dt.float16
I16 = mybir.dt.int16
I32 = mybir.dt.int32
U8 = mybir.dt.uint8
ALU = mybir.AluOpType
ACT = mybir.ActivationFunctionType
AX = mybir.AxisListType

N = 1250
P = 125
NT = N // P
D = 768
KT = D // 128
LAYERS = 3
HL = 4
C = D // HL
HEADS = LAYERS * HL
PAIRS = HEADS // 2
PC = 2 * C
PK = PC // 128
E = 20000
ET = E // P
CE = 4
CHUNKS = ET // CE
R = 64
EX = 4
CLS = 5
EPS = 1e-5
SLOPE = 0.2


def whole(n):
    return -(-n // 32) * 32


ROW = 4 * N
X1_AT = whole(2 * NT * N)
MASK_AT = whole(X1_AT + KT * ROW)
XN_AT = whole(MASK_AT + NT * N)
XL_AT = whole(XN_AT + KT * ROW)
STAGE_AT = whole(XL_AT + KT * ROW)
ACC_AT = MASK_AT + 4 * 3008
ARENA = 201600
CH = [(0, 418), (418, 416), (834, 416)]
DH = 64


class Counter:

    def __init__(self, engine, sem):
        self.engine, self.sem, self.n = engine, sem, 0

    def done(self, instruction):
        self.n += 1
        instruction.then_inc(self.sem, 1)
        self.engine.wait_ge(self.sem, self.n)


def split_matmul(nc, psum, stationary, moving, first, last):
    (s_high, s_low), (m_high, m_low) = stationary, moving
    nc.tensor.matmul(psum, s_high, m_high, start=first, stop=False)
    nc.tensor.matmul(psum, s_high, m_low, start=False, stop=False)
    return nc.tensor.matmul(psum, s_low, m_high, start=False, stop=last)


def build(nc, x, src_t, dst_t, dst_c, w_ah, b_ah, w_gat, a_gat, w_pair, b_gat, w_out, b_out,
          w_qkv, w_proj, b_proj, w_down, w_route, b_exp, w_up, gamma, out):
    def scratch(name, shape):
        return nc.dram_tensor("scratch_" + name, shape, F32, kind="Internal").ap()

    dram_ends = scratch("ends", (CHUNKS, 2))
    dram_a, dram_low = scratch("a", (HEADS, N)), scratch("low", (HEADS, 1))
    dram_uv = scratch("uv", (2 * HEADS, N))
    dram_y = scratch("y", (PAIRS, 128, N))
    dram_res = scratch("res", (NT, P, D))
    ctx = ExitStack()
    with ctx:
        def sb(name, shape, dt=F32):
            return ctx.enter_context(nc.sbuf_tensor(name, shape, dt))

        base = -(-nc.sbuf_base // 32) * 32
        sb("arena", [128, ARENA // 4])

        def at(name, offset, shape, dt=F32):
            return nc.alloc_sbuf_tensor_at(name, shape, dt, offset=base + offset)

        cnt = at("cnt", 0, [P, NT, N], I16)
        x1T = at("x1T", X1_AT, [128, KT, N])
        mask = at("mask", MASK_AT, [P, NT, N], U8)
        xnh = at("xnh", XN_AT, [128, KT, N], F32R)
        xnl = at("xnl", XL_AT, [128, KT, N], F32R)
        acc = at("acc", ACC_AT, [P, NT, D])
        ident = sb("ident", [128, 128])
        identb = sb("identb", [128, 128], BF16)
        ones = sb("ones", [128, DH])
        ab = sb("ab", [P, NT, 2 * HEADS])
        acol = sb("acol", [P, HEADS, NT])
        ncol = sb("ncol", [P, HEADS, NT])
        bah = sb("bah", [128, KT])
        uv = sb("uv", [P, NT, 2 * HEADS])
        reach_row = sb("reach_row", [1, NT * 2], I32)

        psum = ctx.enter_context(nc.psum_tensor("psum", [128, 8 * 512], F32))

        def bank(b):
            return psum[:, 512 * b:512 * (b + 1)]

        front(nc, locals())
        attention(nc, locals())
        projection(nc, locals())
        convolutions(nc, locals())
        adapter(nc, locals())


def front(nc, g):
    at, x1T, cnt, mask, xnh, xnl, ab, acol, ncol = (g[k] for k in "at x1T cnt mask xnh xnl ab acol ncol".split())
    ident, identb, ones, bank, psum = (g[k] for k in "ident identb ones bank psum".split())
    with ExitStack() as ctx:
        def sb(name, shape, dt=F32):
            return ctx.enter_context(nc.sbuf_tensor(name, shape, dt))

        def sem(name):
            return ctx.enter_context(nc.semaphore(name))

        xN = at("xN", STAGE_AT, [P, NT, D])
        wl = at("wl", STAGE_AT, [128, KT, D])
        a_bc = at("a_bc", STAGE_AT + 4 * KT * D, [128, 2, D])
        prod = at("prod", STAGE_AT + 4 * (KT + 2) * D, [128, C])
        hot_src = at("hot_src", STAGE_AT, [P, CE, N], BF16)
        hot_dst = at("hot_dst", STAGE_AT + 10016, [P, CE, 128], BF16)
        zero = at("zero", STAGE_AT + 11040, [P, 512], BF16)
        node_i = at("node_i", STAGE_AT + 12064, [P, N], I32)
        node_id = at("node_id", STAGE_AT + 17088, [P, N], FP16)
        some = [at(f"some{i}", STAGE_AT + 19616 + 2528 * i, [P, N], BF16) for i in range(2)]
        aT = at("aT", STAGE_AT + 24672, [HEADS, N])
        WS = STAGE_AT + 30720
        w_raw = [at(f"wah_raw{i}", WS + 3072 * i, [128, KT, 128]) for i in range(2)]
        w_high = [at(f"wah_high{i}", WS + 3072 * (2 + i), [128, KT, 128], F32R) for i in range(2)]
        w_low = [at(f"wah_low{i}", WS + 3072 * (4 + i), [128, KT, 128], F32R) for i in range(2)]
        chunk_i = at("chunk_i", MASK_AT, [CHUNKS, CE * P], I32)
        chunk_f = at("chunk_f", MASK_AT + 2048, [CHUNKS, CE * P])
        wa = sb("wa", [128, KT, 2 * HEADS])
        spare = sb("spare", [1, 1])
        low = sb("low_a", [HEADS, 1])
        src_i, dst_i = sb("src_i", [P, ET], I32), sb("dst_i", [P, ET], I32)
        src_f, dst_f = sb("src_f", [P, ET]), sb("dst_f", [P, ET])
        ends = sb("ends", [CHUNKS, 2])
        ends_bc = sb("ends_bc", [NT, CHUNKS, 2])
        start_i, start = sb("start_i", [NT, 1], I32), sb("start", [NT, 2])
        chunk_no_i, chunk_no = sb("chunk_no_i", [NT, CHUNKS], I32), sb("chunk_no", [NT, CHUNKS])
        in_reach = sb("in_reach", [NT, CHUNKS])
        reach_f, reach = sb("reach_f", [NT, 2]), sb("reach", [NT, 2], I32)
        stats = sb("stats", [P, 2, 2, 6])
        moments = sb("moments", [P, NT, 2])
        rstd, std, eps = sb("rstd", [P, NT]), sb("std", [P, NT]), sb("eps", [P, 1])

        x_in = [sem(f"x_in{t}") for t in range(NT)]
        raw_in = [sem(f"raw_in{i}") for i in range(2)]
        edges_in, high_ready, low_ready, xl_ready, a_low, bias_in, wl_in, reach_in = (sem(s) for s in "edges_in high_ready low_ready xl_ready a_low bias_in wl_in reach_in".split())
        const_ready, wl_used, reach_ready, scores_out = (sem(s) for s in "const_ready wl_used reach_ready scores_out".split())
        xn_ready, xt_full, xt_free, x1_full, x1_free = (sem(s) for s in "xn_ready xt_full xt_free x1_full x1_free".split())
        wa_ready, ab_full, at_full, at_ready = (sem(s) for s in "wa_ready ab_full at_full at_ready".split())
        hot_ready, hot_free, cnt_full, cnt_free = (sem(s) for s in "hot_ready hot_free cnt_full cnt_free".split())
        some_ready, some_full, some_free, dve_own, pool_own = (
            sem(s) for s in "some_ready some_full some_free dve_own pool_own".split())
        eps_ready, ends_ready, ends_in = sem("eps_ready"), sem("ends_ready"), sem("ends_in")
        node_ready, var_ready, std_ready = sem("node_ready"), sem("var_ready"), sem("std_ready")
        block = ctx.enter_context(nc.Block())

        @block.sync
        def _(sp):
            for t in range(NT):
                sp.dma_start(xN[:, t, :], g["x"][t * P:(t + 1) * P, :]).then_inc(x_in[t], 16)
                if t == 1:
                    sp.dma_start(chunk_i[:, :], g["dst_c"]).then_inc(edges_in, 16)
                    sp.dma_start(src_i[:, :], g["src_t"]).then_inc(edges_in, 16)
                    sp.dma_start(dst_i[:, :], g["dst_t"]).then_inc(edges_in, 16)
            for o in range(2):
                sp.dma_start(w_raw[o][:, :, :], g["w_ah"][o]).then_inc(raw_in[o], 16)
            sp.dma_start(g["bah"][:, :], g["b_ah"]).then_inc(bias_in, 16)
            sp.wait_ge(ends_ready, 1)
            sp.dma_start(g["dram_ends"], ends[:, :]).then_inc(ends_in, 16)
            sp.wait_ge(ends_in, 16)
            sp.dma_start(ends_bc[:, :, :], g["dram_ends"].partition_broadcast(NT)).then_inc(ends_in, 16)
            for layer in range(LAYERS):
                if layer == 0:
                    sp.wait_ge(xt_full, 2 * NT)
                if layer == 1:
                    sp.wait_ge(reach_ready, 1)
                    sp.dma_start(g["reach_row"][0:1, :], reach[:, :]).then_inc(reach_in, 16)
                if layer:
                    sp.wait_ge(wl_used, layer)
                sp.dma_start(wl[:, :, :], g["w_gat"][layer]).then_inc(wl_in, 16)
                sp.dma_start(a_bc[:, :, :], g["a_gat"][layer].partition_broadcast(128)).then_inc(wl_in, 16)
            sp.wait_ge(a_low, 2)
            sp.dma_start(g["dram_a"], aT[:, :]).then_inc(scores_out, 16)
            sp.dma_start(g["dram_low"], low[:, :]).then_inc(scores_out, 16)
            sp.wait_ge(scores_out, 32)
            sp.wait_ge(bias_in, 16)

        @block.gpsimd
        def _(pool):
            own = Counter(pool, pool_own)
            nc.gpsimd.iota(start_i[:, :], pattern=[[0, 1]], base=0, channel_multiplier=P).then_inc(const_ready, 1)
            nc.gpsimd.iota(chunk_no_i[:, :], pattern=[[1, CHUNKS]], base=0, channel_multiplier=0).then_inc(const_ready, 1)
            own.done(nc.gpsimd.memset(ident[:, :], 0.0))
            nc.gpsimd.affine_select(out=ident[:, :], in_=ident[:, :], compare_op=ALU.not_equal, fill=1.0,
                                    base=0, pattern=[[-1, 128]], channel_multiplier=1).then_inc(const_ready, 1)
            pool.wait_ge(const_ready, 3)
            nc.gpsimd.tensor_copy(identb[:, :], ident[:, :]).then_inc(const_ready, 1)
            nc.gpsimd.memset(ones[:, :], 1.0).then_inc(const_ready, 1)
            for o in range(KT):
                pool.wait_ge(high_ready, o + 1)
                if o >= 2:
                    pool.wait_ge(x1_full, 3 * (o - 1))
                nc.gpsimd.tensor_tensor(w_low[o % 2][:, :, :], w_raw[o % 2][:, :, :], w_high[o % 2][:, :, :].bitcast(F32),
                                        ALU.subtract).then_inc(low_ready, 1)
            pool.wait_ge(wl_used, LAYERS)
            nc.gpsimd.iota(node_i[:, :], pattern=[[1, N]], base=0, channel_multiplier=0).then_inc(node_ready, 1)
            nc.gpsimd.memset(zero[:, :], 0.0).then_inc(node_ready, 1)

        @block.vector
        def _(dve):
            own = Counter(dve, dve_own)
            nc.vector.memset(eps[:, :], EPS).then_inc(eps_ready, 1)

            def statistics(t):
                dve.wait_ge(x_in[t], 16)
                nc.vector.bn_stats(stats[:, t % 2, 0, :], xN[:, t, 0:D // 2]).then_inc(dve_own, 1)
                own.n += 1
                own.done(nc.vector.bn_stats(stats[:, t % 2, 1, :], xN[:, t, D // 2:D]))
                nc.vector.bn_aggr(moments[:, t, :], stats[:, t % 2, :, :]).then_inc(var_ready, 1)

            def low_part(i):
                t, half = i // 2, i % 2
                dve.wait_ge(xt_free, i + 1)
                part = (slice(None), slice(3 * half, 3 * half + 3), slice(t * P, (t + 1) * P))
                nc.vector.tensor_tensor(xnl[part], bank(i % 4)[:, 0:3 * P].rearrange("p (k n) -> p k n", k=3),
                                        xnh[part].bitcast(F32), ALU.subtract).then_inc(xl_ready, 1)

            statistics(0)
            for t in range(NT):
                if t + 1 < NT:
                    statistics(t + 1)
                if t >= 1:
                    low_part(2 * t - 2)
                    low_part(2 * t - 1)
                dve.wait_ge(std_ready, t + 1)
                own.done(nc.vector.reciprocal(rstd[:, t:t + 1], std[:, t:t + 1]))
                nc.vector.tensor_scalar(xN[:, t, :], xN[:, t, :], moments[:, t, 0:1], rstd[:, t:t + 1],
                                        ALU.subtract, ALU.mult).then_inc(xn_ready, 1)
                if t == 2:
                    dve.wait_ge(edges_in, 48)
                    own.done(nc.vector.tensor_copy(chunk_f[:, :], chunk_i[:, :]))
                    own.done(nc.vector.tensor_copy(src_f[:, :], src_i[:, :]))
                    own.done(nc.vector.tensor_copy(dst_f[:, :], dst_i[:, :]))
                    own.done(nc.vector.tensor_reduce(ends[:, 0:1], chunk_f[:, :], axis=AX.X, op=ALU.min))
                    nc.vector.tensor_reduce(ends[:, 1:2], chunk_f[:, :], axis=AX.X, op=ALU.max).then_inc(ends_ready, 1)
            low_part(2 * NT - 2)
            low_part(2 * NT - 1)
            dve.wait_ge(const_ready, 2)
            own.done(nc.vector.tensor_copy(start[:, 0:1], start_i[:, :]))
            own.done(nc.vector.tensor_scalar(start[:, 1:2], start[:, 0:1], float(P), None, ALU.add))
            own.done(nc.vector.tensor_copy(chunk_no[:, :], chunk_no_i[:, :]))
            dve.wait_ge(ends_in, 32)
            own.done(nc.vector.tensor_scalar(in_reach[:, :], ends_bc[:, :, 0], start[:, 1:2], None, ALU.is_lt))
            own.done(nc.vector.scalar_tensor_tensor(in_reach[:, :], ends_bc[:, :, 1], start[:, 0:1], in_reach[:, :],
                                                    op0=ALU.is_ge, op1=ALU.mult))
            far = float(2 * CHUNKS)
            own.done(nc.vector.tensor_scalar(in_reach[:, :], in_reach[:, :], -1.0, -far, ALU.add, ALU.mult))
            own.done(nc.vector.tensor_tensor(ends_bc[:, :, 0], chunk_no[:, :], in_reach[:, :], ALU.add))
            own.done(nc.vector.tensor_tensor(ends_bc[:, :, 1], chunk_no[:, :], in_reach[:, :], ALU.subtract))
            own.done(nc.vector.tensor_reduce(reach_f[:, 0:1], ends_bc[:, :, 0], axis=AX.X, op=ALU.min))
            own.done(nc.vector.tensor_reduce(reach_f[:, 1:2], ends_bc[:, :, 1], axis=AX.X, op=ALU.max))
            own.done(nc.vector.tensor_scalar(reach_f[:, 0:1], reach_f[:, 0:1], float(CHUNKS - 1), None, ALU.min))
            own.done(nc.vector.tensor_scalar(reach_f[:, 1:2], reach_f[:, 1:2], 0.0, 1.0, ALU.max, ALU.add))
            nc.vector.tensor_copy(reach[:, :], reach_f[:, :]).then_inc(reach_ready, 1)
            for layer in range(LAYERS):
                dve.wait_ge(wl_in, 32 * (layer + 1))
                for k in range(KT):
                    for s in range(2):
                        for h in range(HL):
                            col = s * HEADS + layer * HL + h
                            last = nc.vector.tensor_tensor_reduce(
                                out=prod[:, :], in0=wl[:, k, h * C:(h + 1) * C], in1=a_bc[:, s, h * C:(h + 1) * C],
                                scale=1.0, scalar=0.0, op0=ALU.mult, op1=ALU.add, accum_out=wa[:, k, col:col + 1])
                            own.done(last)
                nc.vector.tensor_copy(prod[:, 0:1], ident[:, 0:1]).then_inc(wl_used, 1)
            dve.wait_ge(wl_used, LAYERS)
            nc.vector.tensor_copy(prod[:, 1:2], ident[:, 0:1]).then_inc(wa_ready, 1)
            dve.wait_ge(at_ready, len(CH))
            own.done(nc.vector.tensor_reduce(low[:, :], aT[:, :], axis=AX.X, op=ALU.min))
            nc.vector.tensor_scalar(aT[:, :], aT[:, :], low[:, :], None, ALU.subtract).then_inc(a_low, 2)
            dve.wait_ge(node_ready, 1)
            own.done(nc.vector.tensor_copy(node_id[:, :], node_i[:, :]))
            dve.sem_inc(hot_free, CE)
            dve.wait_ge(reach_in, 16)
            units = dve.alloc_register("dve_units")
            dve.reg_mov(units, 0)
            with dve.Fori(0, NT) as it:
                first = dve.value_load(g["reach_row"][0:1, bass.ds(2 * it, 1)], min_val=0, max_val=CHUNKS - 1)
                final = dve.value_load(g["reach_row"][0:1, bass.ds(2 * it + 1, 1)], min_val=1, max_val=CHUNKS)
                with dve.Fori(first, final) as c:
                    for e in range(CE):
                        dve.reg_add(units, units, 1)
                        dve.wait_ge(hot_free, dve.snap(units))
                        nc.vector.tensor_scalar(hot_dst[:, e, 0:P], node_id[:, bass.ds(it * P, P)],
                                                dst_f[:, bass.ds(c * CE + e, 1)], None, ALU.is_equal)\
                            .then_inc(hot_ready, 1)
                        nc.vector.tensor_scalar(hot_src[:, e, :], node_id[:, :], src_f[:, bass.ds(c * CE + e, 1)],
                                                None, ALU.is_equal).then_inc(hot_ready, 1)
            for j in range(NT):
                dve.wait_ge(cnt_free, 1 + 4 * NT)
                if j >= 2:
                    dve.wait_ge(some_full, 2 * (j - 1))
                nc.vector.tensor_scalar(some[j % 2][:, :], cnt[:, j, :], 1.0, None, ALU.min).then_inc(some_ready, 1)
            dve.wait_ge(ab_full, 1)
            own.done(nc.vector.tensor_copy(ab[:, :, :], bank(7)[0:P, 0:NT * 2 * HEADS].rearrange("p (t h) -> p t h", t=NT)))
            own.done(nc.vector.tensor_copy(acol[:, :, :], ab[:, :, 0:HEADS].rearrange("p t h -> p h t")))
            own.done(nc.vector.tensor_scalar(ncol[:, :, :], acol[:, :, :], SLOPE - 1.0, None, ALU.mult))

        @block.scalar
        def _(act):
            def deviation(t):
                act.wait_ge(var_ready, t + 1)
                nc.scalar.activation(std[:, t:t + 1], moments[:, t, 1:2], ACT.Sqrt, bias=eps[:, :]).then_inc(std_ready, 1)

            act.wait_ge(eps_ready, 1)
            deviation(0)
            for i in range(2 * NT):
                t, half = i // 2, i % 2
                if half == 0 and t + 1 < NT:
                    deviation(t + 1)
                act.wait_ge(xt_full, i + 1)
                nc.scalar.activation(xnh[:, 3 * half:3 * half + 3, t * P:(t + 1) * P],
                                     bank(i % 4)[:, 0:3 * P].rearrange("p (k n) -> p k n", k=3), ACT.Copy)\
                    .then_inc(xt_free, 1)
            def high_part(o):
                act.wait_ge(raw_in[o % 2], 16 * (o // 2 + 1))
                if o >= 2:
                    act.wait_ge(x1_full, 3 * (o - 1))
                nc.scalar.activation(w_high[o % 2][:, :, :], w_raw[o % 2][:, :, :], ACT.Copy).then_inc(high_ready, 1)

            high_part(0)
            high_part(1)
            act.wait_ge(bias_in, 16)
            for i in range(KT * 3):
                o, (c0, n) = i // 3, CH[i % 3]
                if i % 3 == 0 and 1 <= o < KT - 1:
                    high_part(o + 1)
                act.wait_ge(x1_full, i + 1)
                nc.scalar.activation(x1T[:, o, c0:c0 + n], bank(4 + i % 3)[:, 0:n], ACT.Relu,
                                     bias=g["bah"][:, o:o + 1]).then_inc(x1_free, 1)
                if i % 3 == 0 and o + 2 < KT:
                    act.wait_ge(low_ready, o + 1)
                    act.dma_start(w_raw[o % 2][:, :, :], g["w_ah"][o + 2]).then_inc(raw_in[o % 2], 16)
            act.wait_ge(wl_used, LAYERS)
            for i, (c0, n) in enumerate(CH):
                act.wait_ge(at_full, i + 1)
                nc.scalar.activation(aT[:, c0:c0 + n], bank(4 + i)[0:HEADS, 0:n], ACT.Copy).then_inc(at_ready, 1)
            act.sem_inc(cnt_free, 1)
            with act.Fori(0, NT) as it:
                act.wait_ge(cnt_full, it + 1)
                nc.scalar.activation(spare[:, :], eps[0:1, :], ACT.Copy).then_inc(cnt_free, 1)
                for b, tiles in enumerate((4, 4, 2)):
                    nc.scalar.activation(cnt[:, 4 * b:4 * b + tiles, bass.ds(it * P, P)],
                                         bank(b)[0:P, 0:128 * tiles].rearrange("p (j n) -> p j n", n=128)[:, :, 0:P],
                                         ACT.Copy).then_inc(cnt_free, 1)
            for i in range(2 * NT):
                j, half = i // 2, i % 2
                act.wait_ge(some_full, i + 1)
                nc.scalar.activation(mask[:, 5 * half:5 * half + 5, j * P:(j + 1) * P],
                                     bank(3 + i % 4)[0:P, :].bitcast(BF16)[:, 0:640].rearrange("p (t n) -> p t n", n=128)[:, :, 0:P],
                                     ACT.Copy).then_inc(some_free, 1)

        @block.tensor
        def _(pe):
            pe.wait_ge(const_ready, 5)
            for i in range(2 * NT):
                t, half = i // 2, i % 2
                if not half:
                    pe.wait_ge(xn_ready, t + 1)
                if i >= 4:
                    pe.wait_ge(xl_ready, i - 3)
                for k in range(3):
                    f = 3 * half + k
                    last = nc.tensor.transpose(bank(i % 4)[:, k * P:(k + 1) * P], xN[:, t, f * 128:(f + 1) * 128],
                                               ident[0:P, 0:P])
                last.then_inc(xt_full, 1)
            pe.wait_ge(xl_ready, 2 * NT)
            for i in range(KT * 3):
                o, (c0, n) = i // 3, CH[i % 3]
                if i % 3 == 0:
                    pe.wait_ge(low_ready, o + 1)
                if i >= 3:
                    pe.wait_ge(x1_free, i - 2)
                for k in range(KT):
                    last = split_matmul(nc, bank(4 + i % 3)[:, 0:n], (w_high[o % 2][:, k, :], w_low[o % 2][:, k, :]),
                                        (xnh[:, k, c0:c0 + n], xnl[:, k, c0:c0 + n]), k == 0, k == KT - 1)
                last.then_inc(x1_full, 1)
            pe.wait_ge(x1_free, KT * 3)
            pe.wait_ge(wa_ready, 1)
            for t in range(NT):
                for k in range(KT):
                    last = nc.tensor.matmul(bank(7)[0:P, t * 2 * HEADS:(t + 1) * 2 * HEADS],
                                            x1T[:, k, t * P:(t + 1) * P], wa[:, k, :], start=k == 0, stop=k == KT - 1)
            last.then_inc(ab_full, 1)
            for i, (c0, n) in enumerate(CH):
                for k in range(KT):
                    last = nc.tensor.matmul(bank(4 + i)[0:HEADS, 0:n], wa[:, k, 0:HEADS], x1T[:, k, c0:c0 + n],
                                            start=k == 0, stop=k == KT - 1)
                last.then_inc(at_full, 1)
            pe.wait_ge(node_ready, 2)
            pe.wait_ge(reach_in, 16)
            units = pe.alloc_register("pe_units")
            pe.reg_mov(units, 0)
            with pe.Fori(0, NT) as it:
                pe.wait_ge(cnt_free, 4 * it + 1)
                for b, n in enumerate((512, 512, 256)):
                    nc.tensor.matmul(bank(b)[0:P, 0:n], zero[:, 0:P], zero[:, 0:n], start=True,
                                     stop=False, skip_group_check=True)
                first = pe.value_load(g["reach_row"][0:1, bass.ds(2 * it, 1)], min_val=0, max_val=CHUNKS - 1)
                final = pe.value_load(g["reach_row"][0:1, bass.ds(2 * it + 1, 1)], min_val=1, max_val=CHUNKS)
                with pe.Fori(first, final) as c:
                    for e in range(CE):
                        pe.reg_add(units, units, 2)
                        pe.wait_ge(hot_ready, pe.snap(units))
                        for j in range(NT):
                            last = nc.tensor.matmul(psum[0:P, 128 * j:128 * j + P], hot_src[:, e, j * P:(j + 1) * P],
                                                    hot_dst[:, e, 0:P], start=False, stop=False, skip_group_check=True)
                        last.then_inc(hot_free, 1)
                nc.tensor.matmul(psum[0:P, bass.ds(it * 128, P)], identb[0:P, 0:P], identb[0:P, 0:P], start=False,
                                 stop=True, skip_group_check=True).then_inc(cnt_full, 1)
            for i in range(2 * NT):
                j, half = i // 2, i % 2
                if not half:
                    pe.wait_ge(some_ready, j + 1)
                if i >= 4:
                    pe.wait_ge(some_free, i - 3)
                if i < 4:
                    pe.wait_ge(at_ready, len(CH))
                for k in range(5):
                    t = 5 * half + k
                    last = nc.tensor.transpose(bank(3 + i % 4)[0:P, :].bitcast(BF16)[:, 128 * k:128 * k + P],
                                               some[j % 2][:, t * P:(t + 1) * P], identb[0:P, 0:P])
                last.then_inc(some_full, 1)


def attention(nc, g):
    at, xnh, xnl, mask, ab, uv, ident, ones, bank = (g[k] for k in "at xnh xnl mask ab uv ident ones bank".split())
    with ExitStack() as ctx:
        def sb(name, shape, dt=F32):
            return ctx.enter_context(nc.sbuf_tensor(name, shape, dt))

        def sem(name):
            return ctx.enter_context(nc.semaphore(name))

        S = STAGE_AT
        w_raw = at("wq_raw", S, [128, KT, 384])
        w_high = at("wq_high", S + 9216, [128, KT, 384], F32R)
        w_low = at("wq_low", S + 18432, [128, KT, 384], F32R)
        kf = at("kf", S + 27648, [P, NT, 128])
        vf = at("vf", S + 32768, [P, NT, 129])
        qf = at("qf", S + 37952, [128, N])
        ke = at("ke", S + 42976, [P, 2, 2, 128])
        qe = [at(f"qe{i}", S + 45024 + 1696 * i, [128, 418]) for i in range(2)]
        den = at("den", S + 48416, [128, 418])
        y = at("y", S + 50112, [128, N])
        junk = at("junk", S + 55136, [P, N], BF16)
        arow = [at(f"arow{i}", S + 57664 + 5024 * i, [P, N]) for i in range(2)]
        uvT = at("uvT", S + 57664, [2 * HEADS, N])
        kvb, ksb = sb("kvb", [128, 128]), sb("ksb", [128, 128])
        ksum = sb("ksum", [128, 1])
        amax = sb("amax", [P, HEADS, NT])
        head_amax = sb("head_amax", [P, 2, NT])
        spare = sb("spare2", [1, 1])
        low = sb("low", [P, HEADS])
        m = sb("m", [P, NT, HEADS])

        arow_in = [sem(f"arow_in{i}") for i in range(2)]
        (raw_in, low_in, kv_high, kv_low, q_high, q_low_w, kv_full, k_exp, k_ready, q_full,
         q_exp, q_ready, acc_full, kvb_ready, num_full, y_ready, y_out, head_max, uv_ready, uvt_full, uvt_ready,
         uv_out, dve_own, zeroed, ones_col) = (sem(s) for s in (
             "raw_in low_in kv_high kv_low q_high q_low_w kv_full k_exp k_ready q_full "
             "q_exp q_ready acc_full kvb_ready num_full y_ready y_out head_max uv_ready uvt_full uvt_ready uv_out "
             "attn_own zeroed ones_col").split())
        block = ctx.enter_context(nc.Block())
        KG = NT // 2
        ND = [(6, 7), (5, 2), (6, 7)]

        @block.sync
        def _(sp):
            sp.dma_start(low[:, :], g["dram_low"].rearrange("h a -> (h a)").partition_broadcast(P)).then_inc(low_in, 16)
            sp.dma_start(w_raw[:, :, :], g["w_qkv"][PAIRS - 1]).then_inc(raw_in, 16)
            with sp.Fori(0, PAIRS) as i:
                sp.wait_ge(q_low_w, i + 1)
                sp.dma_start(w_raw[:, :, :], g["w_qkv"][bass.ds(i, 1), :, :, :].rearrange("a p k c -> (a p) k c"))\
                    .then_inc(raw_in, 16)
                sp.wait_ge(y_ready, 1 + 3 * (i + 1))
                sp.dma_start(g["dram_y"][bass.ds(i, 1), :, :].rearrange("a p n -> (a p) n"), y[:, :]).then_inc(y_out, 16)
            sp.wait_ge(uvt_ready, 3)
            sp.dma_start(g["dram_uv"], uvT[:, :]).then_inc(uv_out, 16)
            sp.wait_ge(y_out, 1 + 16 * PAIRS)
            sp.wait_ge(raw_in, 16 * (PAIRS + 1))
            sp.wait_ge(uv_out, 16)

        @block.gpsimd
        def _(pool):
            nc.gpsimd.memset(kvb[:, :], 0.0).then_inc(zeroed, 1)
            nc.gpsimd.memset(ksb[:, :], 0.0).then_inc(zeroed, 1)
            nc.gpsimd.memset(vf[:, :, 128:129], 1.0).then_inc(ones_col, 1)

            def low_parts(part, high, low_sem, n):
                pool.wait_ge(high, n)
                nc.gpsimd.tensor_tensor(w_low[:, :, part], w_raw[:, :, part], w_high[:, :, part].bitcast(F32),
                                        ALU.subtract).then_inc(low_sem, 1)

            low_parts(slice(128, 384), kv_high, kv_low, 1)
            low_parts(slice(0, 128), q_high, q_low_w, 1)
            with pool.Fori(0, PAIRS) as i:
                for s in range(2):
                    pool.wait_ge(head_max, 2 * i + s + 1)
                    pool.dma_start(arow[s][:, :], g["dram_a"][bass.ds(2 * i + s, 1), :].to_broadcast([P, N]))\
                        .then_inc(arow_in[s], 16)
                low_parts(slice(128, 384), kv_high, kv_low, i + 2)
                low_parts(slice(0, 128), q_high, q_low_w, i + 2)

        @block.vector
        def _(dve):
            own = Counter(dve, dve_own)
            dve.sem_inc(head_max, 2)
            dve.wait_ge(zeroed, 2)
            LINKS_PER_PAIR = 2 * NT + 1 + 2 * 3
            with dve.Fori(0, PAIRS) as i:
                steps = [(s, t) for s in range(2) for t in range(NT)]
                link = [0]

                def chain(instruction):
                    link[0] += 1
                    instruction.then_inc(dve_own, 1)
                    dve.wait_ge(dve_own, i * LINKS_PER_PAIR + link[0])

                def maxima(n):
                    for _ in range(n):
                        s, t = steps.pop(0)
                        if t == 0:
                            dve.wait_ge(arow_in[s], 16 * (i + 1))
                        nc.vector.memset(spare[:, :], 0.0)
                        chain(nc.vector.tensor_tensor_reduce(
                            out=junk[:, :], in0=mask[:, t, :], in1=arow[s][:, :], scale=1.0, scalar=0.0, op0=ALU.mult,
                            op1=ALU.max, accum_out=head_amax[:, s, t:t + 1]))
                        if t == NT - 1:
                            nc.vector.tensor_copy(amax[:, bass.ds(2 * i + s, 1), :].rearrange("p a t -> p (a t)"),
                                                  head_amax[:, s, :]).then_inc(head_max, 1)
                            dve.wait_ge(head_max, 2 * i + s + 3)

                def k_features(gr):
                    dve.wait_ge(k_exp, 1 + KG * i + gr + 1)
                    here = kf[:, 2 * gr:2 * gr + 2, :]
                    nc.vector.scalar_tensor_tensor(here, ke[:, gr % 2, :, :], 1.0, here, op0=ALU.min, op1=ALU.max)\
                        .then_inc(k_ready, 1)

                def q_features(c):
                    c0, n = CH[c]
                    dve.wait_ge(q_exp, 1 + 3 * i + c + 1)
                    nc.vector.scalar_tensor_tensor(qf[:, c0:c0 + n], qe[c % 2][:, 0:n], 1.0, qf[:, c0:c0 + n],
                                                   op0=ALU.min, op1=ALU.max).then_inc(q_ready, 1)

                for gr in range(KG):
                    maxima(2)
                    k_features(gr)
                for c, (c0, n) in enumerate(CH):
                    maxima(2)
                    q_features(c)
                    if c == 1:
                        dve.wait_ge(acc_full, i + 1)
                        for h in range(2):
                            b = slice(DH * h, DH * (h + 1))
                            nc.vector.tensor_copy(kvb[b, b], bank(5)[b, b]).then_inc(kvb_ready, 1)
                        chain(nc.vector.tensor_copy(ksum[:, :], bank(5)[:, 128:129]))
                        for h in range(2):
                            b = slice(DH * h, DH * (h + 1))
                            nc.vector.tensor_scalar(ksb[b, b], ones[b, :], ksum[b, :], None, ALU.mult).then_inc(kvb_ready, 1)
                dve.wait_ge(y_out, 1 + 16 * i)
                for c, (c0, n) in enumerate(CH):
                    num, dn = ND[c]
                    dve.wait_ge(num_full, 3 * i + c + 1)
                    chain(nc.vector.tensor_scalar(den[:, 0:n], bank(dn)[:, 0:n], 1e-6, None, ALU.add))
                    chain(nc.vector.reciprocal(den[:, 0:n], den[:, 0:n]))
                    nc.vector.tensor_tensor(y[:, c0:c0 + n], bank(num)[:, 0:n], den[:, 0:n], ALU.mult).then_inc(y_ready, 1)
                    dve.wait_ge(y_ready, 1 + 3 * i + c + 1)
                maxima(len(steps))
            own.n = PAIRS * LINKS_PER_PAIR
            b_, mx = ab[:, :, HEADS:2 * HEADS], amax[:, :, :].rearrange("p h t -> p t h")
            dve.wait_ge(low_in, 16)
            own.done(nc.vector.tensor_tensor(uv[:, :, 0:HEADS], mx, low[:, :].unsqueeze(1).to_broadcast([P, NT, HEADS]), ALU.add))
            own.done(nc.vector.tensor_tensor(uv[:, :, 0:HEADS], b_, uv[:, :, 0:HEADS], ALU.add))
            own.done(nc.vector.scalar_tensor_tensor(m[:, :, :], uv[:, :, 0:HEADS], SLOPE, uv[:, :, 0:HEADS],
                                                    op0=ALU.mult, op1=ALU.max))
            own.done(nc.vector.tensor_tensor(uv[:, :, 0:HEADS], b_, m[:, :, :], ALU.subtract))
            nc.vector.scalar_tensor_tensor(uv[:, :, HEADS:2 * HEADS], b_, SLOPE, m[:, :, :],
                                           op0=ALU.mult, op1=ALU.subtract).then_inc(uv_ready, 1)

        @block.scalar
        def _(act):
            def high_parts(part, high, turn, used, count):
                act.wait_ge(raw_in, 16 * turn)
                if used is not None:
                    act.wait_ge(used, count)
                nc.scalar.activation(w_high[:, :, part], w_raw[:, :, part], ACT.Copy).then_inc(high, 1)

            high_parts(slice(128, 384), kv_high, 1, None, 0)
            high_parts(slice(0, 128), q_high, 1, None, 0)
            with act.Fori(0, PAIRS) as i:
                for gr in range(KG):
                    kb = bank(gr % 3)[0:P, :].rearrange("p (t c) -> p t c", t=2)
                    act.wait_ge(kv_full, KG * i + gr + 1)
                    nc.scalar.activation(kf[:, 2 * gr:2 * gr + 2, :], kb[:, :, 0:128], ACT.Copy, bias=1.0)
                    nc.scalar.activation(vf[:, 2 * gr:2 * gr + 2, 0:128], kb[:, :, 128:256], ACT.Copy)
                    act.wait_ge(k_ready, 1 + KG * i + gr - 1 if gr else 1 + KG * i)
                    nc.scalar.activation(ke[:, gr % 2, :, :], kb[:, :, 0:128], ACT.Exp).then_inc(k_exp, 1)
                high_parts(slice(128, 384), kv_high, i + 2, kv_full, KG * (i + 1))
                for c, (c0, n) in enumerate(CH):
                    act.wait_ge(q_full, 3 * i + c + 1)
                    nc.scalar.activation(qf[:, c0:c0 + n], bank(3 + c % 2)[:, 0:n], ACT.Copy, bias=1.0)
                    act.wait_ge(q_ready, 1 + 3 * i + c - 1 if c else 1 + 3 * i)
                    nc.scalar.activation(qe[c % 2][:, 0:n], bank(3 + c % 2)[:, 0:n], ACT.Exp).then_inc(q_exp, 1)
                high_parts(slice(0, 128), q_high, i + 2, q_full, 3 * (i + 1))
            for b, (t0, n) in enumerate(((0, 4), (4, 4), (8, 2))):
                act.wait_ge(uvt_full, b + 1)
                nc.scalar.activation(uvT[:, t0 * P:(t0 + n) * P].rearrange("p (t n) -> p t n", t=n),
                                     bank(b)[0:2 * HEADS, 0:128 * n].rearrange("p (t n) -> p t n", t=n)[:, :, 0:P],
                                     ACT.Copy).then_inc(uvt_ready, 1)

        @block.tensor
        def _(pe):
            for s in (y_ready, y_out, kvb_ready, k_ready, k_exp, q_ready, q_exp):
                pe.sem_inc(s, 1)
            pe.wait_ge(ones_col, 1)
            with pe.Fori(0, PAIRS) as i:
                pe.wait_ge(kv_low, i + 1)
                for gr in range(KG):
                    pe.wait_ge(k_exp, 1 + KG * i + (gr - 2 if gr >= 3 else 0))
                    if gr == 2:
                        pe.wait_ge(y_ready, 1 + 3 * i)
                    for t in range(2):
                        nt = slice((2 * gr + t) * P, (2 * gr + t + 1) * P)
                        for k in range(KT):
                            last = split_matmul(nc, bank(gr % 3)[0:P, 256 * t:256 * (t + 1)],
                                                (xnh[:, k, nt], xnl[:, k, nt]),
                                                (w_high[:, k, 128:384], w_low[:, k, 128:384]), k == 0, k == KT - 1)
                    last.then_inc(kv_full, 1)
                pe.wait_ge(q_low_w, i + 1)
                pe.wait_ge(q_exp, 1 + 3 * i)
                for c, (c0, n) in enumerate(CH):
                    if c == 2:
                        pe.wait_ge(k_ready, 1 + KG * (i + 1))
                        for t in range(NT):
                            last = nc.tensor.matmul(bank(5)[:, 0:129], kf[:, t, :], vf[:, t, :], start=t == 0, stop=t == NT - 1)
                        last.then_inc(acc_full, 1)
                        pe.wait_ge(q_exp, 1 + 3 * i + 1)
                    for k in range(KT):
                        last = split_matmul(nc, bank(3 + c % 2)[:, 0:n], (w_high[:, k, 0:128], w_low[:, k, 0:128]),
                                            (xnh[:, k, c0:c0 + n], xnl[:, k, c0:c0 + n]), k == 0, k == KT - 1)
                    last.then_inc(q_full, 1)
                pe.wait_ge(kvb_ready, 1 + 4 * (i + 1))
                for c, (c0, n) in enumerate(CH):
                    num, dn = ND[c]
                    pe.wait_ge(q_ready, 1 + 3 * i + c + 1)
                    if c == 2:
                        pe.wait_ge(y_ready, 1 + 3 * i + 1)
                    nc.tensor.matmul(bank(dn)[:, 0:n], ksb[:, :], qf[:, c0:c0 + n], start=True, stop=True)
                    nc.tensor.matmul(bank(num)[:, 0:n], kvb[:, :], qf[:, c0:c0 + n], start=True, stop=True)\
                        .then_inc(num_full, 1)
            pe.wait_ge(y_ready, 1 + 3 * PAIRS)
            pe.wait_ge(uv_ready, 1)
            for b, (t0, n) in enumerate(((0, 4), (4, 4), (8, 2))):
                for t in range(n):
                    last = nc.tensor.transpose(bank(b)[0:2 * HEADS, 128 * t:128 * t + P], uv[:, t0 + t, :], ident[0:P, 0:P])
                last.then_inc(uvt_full, 1)


def projection(nc, g):
    at, bank = g["at"], g["bank"]
    with ExitStack() as ctx:
        def sem(name):
            return ctx.enter_context(nc.semaphore(name))

        yh = at("yh", XN_AT, [128, KT, N], F32R)
        yl = at("yl", XL_AT, [128, KT, N], F32R)
        wh = at("wproj_high", STAGE_AT, [128, KT, D], F32R)
        wl = at("wproj_low", STAGE_AT + 18432, [128, KT, D], F32R)
        S = STAGE_AT + 36864
        w_raw = [at(f"wproj_raw{i}", S + 3072 * i, [128, D]) for i in range(2)]
        y_raw = [at(f"y_raw{i}", S + 6144 + 5024 * i, [128, N]) for i in range(2)]
        xt = [at(f"xt{i}", S + 16192 + 3072 * i, [P, D]) for i in range(3)]
        bp = at("bp", S + 25408, [P, D])
        y_in = [sem(f"y_in{i}") for i in range(2)]
        w_in = [sem(f"wproj_in{i}") for i in range(2)]
        x_in = [sem(f"xt_in{i}") for i in range(3)]
        res_out = [sem(f"res_out{i}") for i in range(3)]
        bp_in, wh_ready, wl_ready, yh_ready, yl_ready, xb_ready, p_full, p_free = (
            sem(s) for s in "bp_in wph_ready wpl_ready yh_ready yl_ready xb_ready p_full p_free".split())
        block = ctx.enter_context(nc.Block())

        @block.sync
        def _(sp):
            for k in range(KT):
                if k >= 2:
                    sp.wait_ge(yl_ready, k - 1)
                    sp.wait_ge(wl_ready, k - 1)
                sp.dma_start(w_raw[k % 2][:, :], g["w_proj"][:, k, :]).then_inc(w_in[k % 2], 16)
                sp.dma_start(y_raw[k % 2][:, :], g["dram_y"][k]).then_inc(y_in[k % 2], 16)
            sp.dma_start(bp[:, :], g["b_proj"].partition_broadcast(P)).then_inc(bp_in, 16)
            for t in range(NT + 2):
                if t < NT:
                    if t >= 3:
                        sp.wait_ge(res_out[t % 3], 16 * (t // 3))
                    sp.dma_start(xt[t % 3][:, :], g["x"][t * P:(t + 1) * P, :]).then_inc(x_in[t % 3], 16)
                if t >= 2:
                    sp.wait_ge(p_free, 2 * (t - 1))
                    sp.dma_start(g["dram_res"][t - 2], xt[(t - 2) % 3][:, :]).then_inc(res_out[(t - 2) % 3], 16)
            for i in range(3):
                sp.wait_ge(res_out[i], 16 * len(range(i, NT, 3)))

        @block.gpsimd
        def _(pool):
            for k in range(KT):
                pool.wait_ge(wh_ready, k + 1)
                nc.gpsimd.tensor_tensor(wl[:, k, :], w_raw[k % 2][:, :], wh[:, k, :].bitcast(F32), ALU.subtract)\
                    .then_inc(wl_ready, 1)
            pool.wait_ge(bp_in, 16)
            for t in range(NT):
                pool.wait_ge(x_in[t % 3], 16 * (t // 3 + 1))
                nc.gpsimd.tensor_tensor(xt[t % 3][:, :], xt[t % 3][:, :], bp[:, :], ALU.add).then_inc(xb_ready, 1)

        @block.scalar
        def _(act):
            for k in range(KT):
                act.wait_ge(w_in[k % 2], 16 * (k // 2 + 1))
                nc.scalar.activation(wh[:, k, :], w_raw[k % 2][:, :], ACT.Copy).then_inc(wh_ready, 1)
                act.wait_ge(y_in[k % 2], 16 * (k // 2 + 1))
                nc.scalar.activation(yh[:, k, :], y_raw[k % 2][:, :], ACT.Copy).then_inc(yh_ready, 1)

        @block.vector
        def _(dve):
            for k in range(KT):
                dve.wait_ge(yh_ready, k + 1)
                nc.vector.tensor_tensor(yl[:, k, :], y_raw[k % 2][:, :], yh[:, k, :].bitcast(F32), ALU.subtract)\
                    .then_inc(yl_ready, 1)
            for t in range(NT):
                dve.wait_ge(xb_ready, t + 1)
                for half in range(2):
                    i, c = 2 * t + half, slice(384 * half, 384 * (half + 1))
                    dve.wait_ge(p_full, i + 1)
                    nc.vector.tensor_tensor(xt[t % 3][:, c], xt[t % 3][:, c], bank(i % 8)[0:P, 0:384], ALU.add)\
                        .then_inc(p_free, 1)

        @block.tensor
        def _(pe):
            for k in range(KT):
                pe.wait_ge(yl_ready, k + 1)
                pe.wait_ge(wl_ready, k + 1)
                for i in range(8):
                    t, c = i // 2, slice(384 * (i % 2), 384 * (i % 2 + 1))
                    nodes = slice(t * P, (t + 1) * P)
                    last = split_matmul(nc, bank(i)[0:P, 0:384], (yh[:, k, nodes], yl[:, k, nodes]),
                                        (wh[:, k, c], wl[:, k, c]), k == 0, k == KT - 1)
                    if k == KT - 1:
                        last.then_inc(p_full, 1)
            for i in range(8, 2 * NT):
                t, c = i // 2, slice(384 * (i % 2), 384 * (i % 2 + 1))
                nodes = slice(t * P, (t + 1) * P)
                pe.wait_ge(p_free, i - 7)
                for k in range(KT):
                    last = split_matmul(nc, bank(i % 8)[0:P, 0:384], (yh[:, k, nodes], yl[:, k, nodes]),
                                        (wh[:, k, c], wl[:, k, c]), k == 0, k == KT - 1)
                last.then_inc(p_full, 1)


def convolutions(nc, g):
    at, acc, x1T, cnt, acol, ncol, ident, bank = (g[k] for k in "at acc x1T cnt acol ncol ident bank".split())
    with ExitStack() as ctx:
        def sb(name, shape, dt=F32):
            return ctx.enter_context(nc.sbuf_tensor(name, shape, dt))

        def sem(name):
            return ctx.enter_context(nc.semaphore(name))

        RING = 4
        LEAD = 2
        x1h = [at(f"x1h{i}", MASK_AT + 3008 * i, [128, KT, P], F32R) for i in range(2)]
        x1l = [at(f"x1l{i}", MASK_AT + 3008 * (2 + i), [128, KT, P], F32R) for i in range(2)]
        S = ACC_AT + 4 * NT * D
        prob = [at(f"prob{i}", S + 5024 * i, [P, N]) for i in range(RING)]
        urow, vrow = at("urow", S + 20096, [P, N]), at("vrow", S + 25120, [P, N])
        hN = at("hN", S + 30144, [P, NT, PC + 2])
        gN = hN[:, :, 1:PC + 1]
        xlh = [at(f"xlh{i}", S + 45600 + 3008 * i, [128, PK, 2 * P], F32R) for i in range(2)]
        xll = [at(f"xll{i}", S + 51616 + 3008 * i, [128, PK, 2 * P], F32R) for i in range(2)]
        w_raw = at("w_raw", S + 57632, [128, KT * PC])
        wp_raw = w_raw[:, :].rearrange("p (k c) -> p k c", k=KT)
        wo_raw = w_raw[:, :].rearrange("p (k c) -> p k c", k=PK)
        wph, wpl = (at(n, S + 66848 + 9216 * i, [128, KT, PC], F32R) for i, n in enumerate(("wph", "wpl")))
        woh, wol = (at(n, S + 85280 + 9216 * i, [128, PK, D], F32R) for i, n in enumerate(("woh", "wol")))
        a_pair, b_pair = sb("a_pair", [P, 2, NT]), sb("b_pair", [P, PC])
        total = sb("total", [P, 5, 2])
        (raw_in, row_in, bias_in, bias_used, acc_in, ones_col, wh_ready, wl_ready, xh_ready, xl_ready, h_full, h_ready,
         pair_ready, z_ready, e_ready, prob_ready, prob_free, sum_full, g_ready, t_full, t_high, t_ready, o_full, o_free,
         total_own) = (sem(s) for s in (
             "raw_in row_in bias_in bias_used acc_in h_ones wh_ready wl_ready xh_ready xl_ready h_full h_ready pair_ready "
             "z_ready e_ready prob_ready prob_free sum_full g_ready t_full t_high t_ready o_full o_free total_own").split())
        block = ctx.enter_context(nc.Block())
        TILES = 2 * NT
        GR = NT // 2
        OT = 2 * NT
        TB = [(5, 6), (7, 0)]
        OB = [1, 2, 3, 4]

        @block.sync
        def _(sp):
            for t in range(NT):
                sp.dma_start(acc[:, t, :], g["b_out"].partition_broadcast(P)).then_inc(acc_in, 16)
            sp.dma_start(wp_raw, g["w_pair"][PAIRS - 1]).then_inc(raw_in, 16)
            with sp.Fori(0, PAIRS) as i:
                sp.wait_ge(z_ready, 1 + TILES * i)
                for s in range(2):
                    if s:
                        sp.wait_ge(z_ready, 1 + TILES * i + NT)
                    for row, off in ((urow, 0), (vrow, HEADS)):
                        sp.dma_start(row[:, :], g["dram_uv"][bass.ds(2 * i + s + off, 1), :].to_broadcast([P, N]))\
                            .then_inc(row_in, 16)
                    if not s:
                        sp.wait_ge(wl_ready, 2 * i + 1)
                        sp.dma_start(wo_raw, g["w_out"][bass.ds(i, 1), :, :, :].rearrange("a p k c -> (a p) k c"))\
                            .then_inc(raw_in, 16)
                        sp.wait_ge(g_ready, 1 + TILES * i)
                        sp.dma_start(b_pair[:, :], g["b_gat"][bass.ds(i, 1), :].to_broadcast([P, PC])).then_inc(bias_in, 16)
                sp.wait_ge(wl_ready, 2 * i + 2)
                sp.dma_start(wp_raw, g["w_pair"][bass.ds(i, 1), :, :, :].rearrange("a p k c -> (a p) k c"))\
                    .then_inc(raw_in, 16)
            sp.wait_ge(raw_in, 16 * (2 * PAIRS + 1))

        @block.gpsimd
        def _(pool):
            nc.gpsimd.memset(hN[:, :, 0:1], 1.0).then_inc(ones_col, 1)
            nc.gpsimd.memset(hN[:, :, PC + 1:PC + 2], 1.0).then_inc(ones_col, 1)

            def low_part(low, raw, high, n):
                pool.wait_ge(wh_ready, n)
                nc.gpsimd.tensor_tensor(low[:, :, :], raw, high[:, :, :].bitcast(F32), ALU.subtract).then_inc(wl_ready, 1)

            low_part(wpl, wp_raw, wph, 1)
            with pool.Fori(0, PAIRS) as i:
                low_part(wol, wo_raw, woh, 2 * i + 2)
                low_part(wpl, wp_raw, wph, 2 * i + 3)

        @block.vector
        def _(dve):
            dve.sem_inc(prob_free, 3)
            dve.wait_ge(acc_in, 16 * NT)
            with dve.Fori(0, PAIRS) as i:
                chain = [0]

                def own(instruction):
                    chain[0] += 1
                    instruction.then_inc(total_own, 1)
                    dve.wait_ge(total_own, i * 20 + chain[0])

                def scores(n):
                    s, j = n // NT, n % NT
                    if j == 0:
                        dve.wait_ge(row_in, 64 * i + 32 * (s + 1))
                    used = (n - RING) % TILES
                    if used % NT == NT - 1:
                        dve.wait_ge(sum_full, 1 + 10 * i + (0 if n < RING else 5))
                    else:
                        dve.wait_ge(prob_free, (TILES - 2) * i + (1 + n if n < RING else 4 + used - used // NT))
                    nc.vector.scalar_tensor_tensor(
                        prob[n % RING][:, :], vrow[:, :], ncol[:, bass.ds(2 * i + s, 1), j:j + 1].rearrange("p a t -> p (a t)"),
                        urow[:, :], op0=ALU.add, op1=ALU.max).then_inc(z_ready, 1)

                def weigh(n):
                    dve.wait_ge(e_ready, TILES * i + n + 1)
                    nc.vector.scalar_tensor_tensor(prob[n % RING][:, :], prob[n % RING][:, :], 1.0, cnt[:, n % NT, :],
                                                   op0=ALU.min, op1=ALU.mult).then_inc(prob_ready, 1)

                def normalise(s):
                    if s == 0:
                        dve.wait_ge(bias_in, 16 * (i + 1))
                    for b in range(5):
                        dve.wait_ge(sum_full, 1 + 10 * i + 5 * s + b + 1)
                        both = bank(b)[0:P, 0:386].rearrange("p (t c) -> p t c", t=2)
                        own(nc.vector.tensor_scalar(total[:, b, :], both[:, :, C * s], 1e-16, None, ALU.add))
                        own(nc.vector.reciprocal(total[:, b, :], total[:, b, :]))
                        for t in range(2):
                            nc.vector.scalar_tensor_tensor(gN[:, 2 * b + t, C * s:C * (s + 1)], both[:, t, 1 - s:C + 1 - s], total[:, b, t:t + 1],
                                                           b_pair[:, C * s:C * (s + 1)], op0=ALU.mult, op1=ALU.add)\
                                .then_inc(g_ready, 1)

                for t in range(NT):
                    dve.wait_ge(xh_ready, NT * i + t + 1)
                    nc.vector.tensor_tensor(x1l[t % 2][:, :, 0:P], x1T[:, :, t * P:(t + 1) * P],
                                            x1h[t % 2][:, :, 0:P].bitcast(F32), ALU.subtract).then_inc(xl_ready, 1)
                    if t >= NT - RING:
                        scores(t - (NT - RING))
                for n in range(TILES):
                    if RING <= n + LEAD < TILES:
                        scores(n + LEAD)
                    weigh(n)
                    if n == NT:
                        normalise(0)
                normalise(1)

                def low_part(gr):
                    for part, (ks, b) in enumerate(((slice(0, 2), TB[gr % 2][0]), (slice(2, 3), TB[gr % 2][1]))):
                        n = ks.stop - ks.start
                        dve.wait_ge(t_high, 2 * (GR * i + gr) + part + 1)
                        nc.vector.scalar_tensor_tensor(
                            xll[gr % 2][:, ks, :], bank(b)[:, 0:n * 2 * P].rearrange("p (k n) -> p k n", k=n), 0.0,
                            xlh[gr % 2][:, ks, :].bitcast(F32), op0=ALU.max, op1=ALU.subtract).then_inc(t_ready, 1)

                low_part(0)
                for gr in range(GR):
                    if gr + 1 < GR:
                        low_part(gr + 1)
                    for o in range(4 * gr, 4 * gr + 4):
                        t, half = o // 2, o % 2
                        dve.wait_ge(o_full, 1 + OT * i + o + 1)
                        here = acc[:, t, 384 * half:384 * (half + 1)]
                        nc.vector.tensor_tensor(here, here, bank(OB[o % 4])[0:P, 0:384], ALU.add).then_inc(o_free, 1)
                dve.wait_ge(o_free, 1 + OT * (i + 1))

        @block.scalar
        def _(act):
            def high_part(high, raw, n, used, count):
                act.wait_ge(raw_in, 16 * n)
                if used is not None:
                    act.wait_ge(used, count)
                nc.scalar.activation(high[:, :, :], raw, ACT.Copy).then_inc(wh_ready, 1)

            high_part(wph, wp_raw, 1, None, 0)
            act.wait_ge(ones_col, 2)
            with act.Fori(0, PAIRS) as i:
                def exponential(n):
                    act.wait_ge(z_ready, 1 + TILES * i + n + 1)
                    nc.scalar.activation(prob[n % RING][:, :], prob[n % RING][:, :], ACT.Exp,
                                         bias=a_pair[:, n // NT, n % NT:n % NT + 1]).then_inc(e_ready, 1)

                def take_h(t):
                    act.wait_ge(h_full, 1 + NT * i + t + 1)
                    nc.scalar.activation(hN[:, t, 1:PC + 1], bank(5 + t % 3)[0:P, 0:PC], ACT.Copy).then_inc(h_ready, 1)

                for t in range(NT):
                    act.wait_ge(h_full, 1 + NT * i + (t - 1 if t >= 2 else 0))
                    nc.scalar.activation(x1h[t % 2][:, :, 0:P], x1T[:, :, t * P:(t + 1) * P], ACT.Copy).then_inc(xh_ready, 1)
                    if t == 1:
                        nc.scalar.activation(a_pair[:, :, :], acol[:, bass.ds(2 * i, 2), :], ACT.Copy).then_inc(pair_ready, 1)
                        act.wait_ge(pair_ready, i + 1)
                    if t >= 1:
                        take_h(t - 1)
                    if t >= NT - RING + 1:
                        exponential(t - (NT - RING + 1))
                take_h(NT - 1)
                for n in range(RING - 1, TILES):
                    exponential(n)
                    if n == 6:
                        high_part(woh, wo_raw, 2 * i + 2, o_full, 1 + OT * i)
                    if n == 13:
                        high_part(wph, wp_raw, 2 * i + 3, h_full, 1 + NT * (i + 1))
                for gr in range(GR):
                    for part, (ks, b) in enumerate(((slice(0, 2), TB[gr % 2][0]), (slice(2, 3), TB[gr % 2][1]))):
                        n = ks.stop - ks.start
                        act.wait_ge(t_full, 2 * (GR * i + gr) + part + 1)
                        if gr >= 2 and part == 0:
                            act.wait_ge(o_full, 1 + OT * i + 4 * (gr - 1))
                        nc.scalar.activation(xlh[gr % 2][:, ks, :], bank(b)[:, 0:n * 2 * P].rearrange("p (k n) -> p k n", k=n),
                                             ACT.Relu).then_inc(t_high, 1)

        @block.tensor
        def _(pe):
            for s in (h_full, z_ready, o_full, o_free, g_ready, sum_full, t_ready):
                pe.sem_inc(s, 1)
            pe.wait_ge(ones_col, 2)
            with pe.Fori(0, PAIRS) as i:
                pe.wait_ge(wl_ready, 2 * i + 1)
                pe.wait_ge(t_ready, 1 + 2 * GR * i)
                for t in range(NT):
                    pe.wait_ge(xl_ready, NT * i + t + 1)
                    if t >= 3:
                        pe.wait_ge(h_ready, NT * i + t - 2)
                    for k in range(KT):
                        last = split_matmul(nc, bank(5 + t % 3)[0:P, 0:PC], (x1h[t % 2][:, k, 0:P], x1l[t % 2][:, k, 0:P]),
                                            (wph[:, k, :], wpl[:, k, :]), k == 0, k == KT - 1)
                    last.then_inc(h_full, 1)
                pe.wait_ge(h_ready, NT * (i + 1))
                for s in range(2):
                    for j in range(NT):
                        n = NT * s + j
                        pe.wait_ge(prob_ready, TILES * i + n + 1)
                        for t in range(NT):
                            if j == 0 and t % 2 == 0:
                                if s:
                                    pe.wait_ge(g_ready, 1 + 20 * i + t + 2)
                                elif t == 0:
                                    pe.wait_ge(o_free, 1 + OT * i)
                            last = nc.tensor.matmul(bank(t // 2)[0:P, 193 * (t % 2):193 * (t % 2) + 193],
                                                    prob[n % RING][:, t * P:(t + 1) * P], hN[:, j, 193 * s:193 * (s + 1)],
                                                    start=j == 0 and t % 2 == 0, stop=j == NT - 1, skip_group_check=True)
                            if j == NT - 1 and t % 2:
                                last.then_inc(sum_full, 1)
                        if j < NT - 1:
                            last.then_inc(prob_free, 1)

                def transposes(gr):
                    pe.wait_ge(g_ready, 1 + 20 * i + 10 + 2 * (gr + 1))
                    if gr == 1:
                        pe.wait_ge(g_ready, 1 + 20 * (i + 1))
                    for k in range(PK):
                        b, c0 = (TB[gr % 2][0], 250 * k) if k < 2 else (TB[gr % 2][1], 0)
                        for t in range(2):
                            last = nc.tensor.transpose(bank(b)[:, c0 + t * P:c0 + (t + 1) * P],
                                                       gN[:, 2 * gr + t, 128 * k:128 * (k + 1)], ident[0:P, 0:P])
                        if k:
                            last.then_inc(t_full, 1)

                def outputs(gr):
                    pe.wait_ge(t_ready, 1 + 2 * (GR * i + gr) + 2)
                    for o in range(4 * gr, 4 * gr + 4):
                        t, c = o // 2 % 2, slice(384 * (o % 2), 384 * (o % 2 + 1))
                        if o >= 4:
                            pe.wait_ge(o_free, 1 + OT * i + o - 3)
                        nodes = slice(t * P, (t + 1) * P)
                        for k in range(PK):
                            last = split_matmul(nc, bank(OB[o % 4])[0:P, 0:384], (xlh[gr % 2][:, k, nodes], xll[gr % 2][:, k, nodes]),
                                                (woh[:, k, c], wol[:, k, c]), k == 0, k == PK - 1)
                        last.then_inc(o_full, 1)

                transposes(0)
                transposes(1)
                pe.wait_ge(wl_ready, 2 * i + 2)
                for gr in range(GR):
                    outputs(gr)
                    if gr + 2 < GR:
                        transposes(gr + 2)


def adapter(nc, g):
    at, acc, ident, bank = (g[k] for k in "at acc ident bank".split())
    with ExitStack() as ctx:
        def sb(name, shape, dt=F32):
            return ctx.enter_context(nc.sbuf_tensor(name, shape, dt))

        def sem(name):
            return ctx.enter_context(nc.semaphore(name))

        W = EX + EX * R
        S = ACC_AT + 4 * NT * D
        xn2T = at("xn2T", X1_AT, [128, KT, N])
        xn = [at(f"xn2_{i}", S + 3072 * i, [P, D])[:, :] for i in range(3)]
        res = [at(f"res{i}", S + 9216 + 3072 * i, [P, D])[:, :] for i in range(4)]
        wd = at("wd", S + 21504, [128, KT, R])[:, :, :]
        wr = at("wr", S + 23040, [R, W])[:, :]
        wu = at("wu", S + 24128, [R, D])[:, :]
        gam = at("gam", S + 27200, [R, D])[:, :]
        be = at("be", S + 30272, [P, EX * R])[:, :]
        fT = at("fT", S + 31296, [R, N])[:, :]
        le = at("le", S + 36320, [P, NT, W])[:, :, :]
        pick = at("pick", S + 46720, [P, NT, EX, R])[:, :, :, :]
        comb = at("comb", S + 56960, [P, NT, R])[:, :, :]
        best, total = sb("best", [P, NT]), sb("esum", [P, NT])
        hot, taken, el = sb("hot", [P, NT, EX]), sb("taken", [P, NT]), sb("el", [P, NT, EX])
        stats = sb("stats2", [P, 2, 2, 6])
        moments, rstd = sb("moments2", [P, NT, 2]), sb("rstd2", [P, NT])
        std, eps = sb("std2", [P, NT]), sb("eps2", [P, 1])
        res_in = [sem(f"res_in{i}") for i in range(4)]
        eps_ready = sem("eps2_ready")
        x2_ready, var_ready, std_ready = sem("x2_ready"), sem("var2_ready"), sem("std2_ready")
        (w_in, own_s, xn_ready, xt_full, xt_free, d_full, f_ready, r_full, r_free, el_ready, ex_ready, wu_ready,
         comb_ready, c_full, full_ready, up_full, y_ready, out_done) = (sem(s) for s in (
             "aw_in own2 xn2_ready xt2_full xt2_free d_full f_ready r_full r_free el_ready ex_ready wu_ready comb_ready "
             "c_full full_ready up_full ay_ready out_done").split())
        block = ctx.enter_context(nc.Block())

        @block.sync
        def _(sp):
            for t in range(NT):
                if t >= 4:
                    sp.wait_ge(x2_ready, t - 3)
                sp.dma_start(res[t % 4], g["dram_res"][t]).then_inc(res_in[t % 4], 16)
                if t == 3:
                    sp.dma_start(wd, g["w_down"]).then_inc(w_in, 16)
                    sp.dma_start(wr, g["w_route"]).then_inc(w_in, 16)
                    sp.dma_start(wu, g["w_up"]).then_inc(w_in, 16)
                    sp.dma_start(gam, g["gamma"].partition_broadcast(R)).then_inc(w_in, 16)
                    sp.dma_start(be, g["b_exp"].partition_broadcast(P)).then_inc(w_in, 16)
            for t in range(NT):
                sp.wait_ge(y_ready, 2 * (t + 1))
                sp.dma_start(g["out"][t * P:(t + 1) * P, :], acc[:, t, :]).then_inc(out_done, 16)
            sp.wait_ge(out_done, 16 * NT)

        @block.vector
        def _(dve):
            own = Counter(dve, own_s)
            nc.vector.memset(eps[:, :], EPS).then_inc(eps_ready, 1)


            def statistics(t):
                dve.wait_ge(res_in[t % 4], 16 * (t // 4 + 1))
                nc.vector.scalar_tensor_tensor(acc[:, t, :], acc[:, t, :], 0.0, res[t % 4], op0=ALU.max, op1=ALU.add)\
                    .then_inc(x2_ready, 1)
                dve.wait_ge(x2_ready, t + 1)
                nc.vector.bn_stats(stats[:, t % 2, 0, :], acc[:, t, 0:D // 2]).then_inc(own_s, 1)
                own.n += 1
                own.done(nc.vector.bn_stats(stats[:, t % 2, 1, :], acc[:, t, D // 2:D]))
                nc.vector.bn_aggr(moments[:, t, :], stats[:, t % 2, :, :]).then_inc(var_ready, 1)

            statistics(0)
            for t in range(NT):
                if t + 1 < NT:
                    statistics(t + 1)
                dve.wait_ge(std_ready, t + 1)
                own.done(nc.vector.reciprocal(rstd[:, t:t + 1], std[:, t:t + 1]))
                if t >= 3:
                    dve.wait_ge(xt_full, 2 * (t - 2))
                nc.vector.tensor_scalar(xn[t % 3], acc[:, t, :], moments[:, t, 0:1], rstd[:, t:t + 1],
                                        ALU.subtract, ALU.mult).then_inc(xn_ready, 1)
            dve.wait_ge(w_in, 80)
            nc.vector.tensor_tensor(wu, wu, gam, ALU.mult).then_inc(wu_ready, 1)
            dve.wait_ge(r_free, NT)
            logit = le[:, :, 0:EX]
            own.done(nc.vector.tensor_reduce(best[:, :], logit, axis=AX.X, op=ALU.max))
            best_b = best[:, :].unsqueeze(2).to_broadcast([P, NT, EX])
            nc.vector.tensor_tensor(el[:, :, :], logit, best_b, ALU.subtract).then_inc(el_ready, 1)
            own.done(nc.vector.tensor_tensor(hot[:, :, :], logit, best_b, ALU.is_ge))
            own.done(nc.vector.tensor_copy(taken[:, :], hot[:, :, 0]))
            for e in range(1, EX):
                own.done(nc.vector.tensor_tensor(hot[:, :, e], hot[:, :, e], taken[:, :], ALU.is_gt))
                if e < EX - 1:
                    own.done(nc.vector.tensor_tensor(taken[:, :], hot[:, :, e], taken[:, :], ALU.max))
            dve.wait_ge(ex_ready, 1)
            own.done(nc.vector.tensor_reduce(total[:, :], el[:, :, :], axis=AX.X, op=ALU.add))
            own.done(nc.vector.reciprocal(total[:, :], total[:, :]))
            own.done(nc.vector.memset(total[0:CLS, 0:1], 0.0))
            own.done(nc.vector.tensor_tensor(hot[:, :, :], hot[:, :, :], total[:, :].unsqueeze(2).to_broadcast([P, NT, EX]), ALU.mult))
            own.done(nc.vector.tensor_tensor(pick, le[:, :, EX:W].rearrange("p t (e r) -> p t e r", e=EX),
                                             be.rearrange("p (e r) -> p e r", e=EX).unsqueeze(1).to_broadcast([P, NT, EX, R]), ALU.add))
            own.done(nc.vector.tensor_tensor(pick, pick, hot[:, :, :].unsqueeze(3).to_broadcast([P, NT, EX, R]), ALU.mult))
            own.done(nc.vector.tensor_tensor(pick[:, :, 0:2, :], pick[:, :, 0:2, :], pick[:, :, 2:4, :], ALU.add))
            nc.vector.tensor_tensor(comb, pick[:, :, 0, :], pick[:, :, 1, :], ALU.add).then_inc(comb_ready, 1)
            for b, (t0, n) in enumerate(((0, 4), (4, 4), (8, 2))):
                dve.wait_ge(c_full, b + 1)
                here = fT[:, t0 * P:(t0 + n) * P]
                nc.vector.tensor_tensor(here, here, bank(b)[0:R, 0:n * P], ALU.add).then_inc(full_ready, 1)
            for t in range(NT):
                for half in range(2):
                    i = 2 * t + half
                    dve.wait_ge(up_full, i + 1)
                    here = acc[:, t, 384 * half:384 * (half + 1)]
                    nc.vector.tensor_tensor(here, here, bank(3 + i % 5)[0:P, 0:384], ALU.add).then_inc(y_ready, 1)

        @block.scalar
        def _(act):
            def deviation(t):
                act.wait_ge(var_ready, t + 1)
                nc.scalar.activation(std[:, t:t + 1], moments[:, t, 1:2], ACT.Sqrt, bias=eps[:, :]).then_inc(std_ready, 1)

            act.wait_ge(eps_ready, 1)
            deviation(0)
            for i in range(2 * NT):
                t, half = i // 2, i % 2
                if half == 0 and t + 1 < NT:
                    deviation(t + 1)
                act.wait_ge(xt_full, i + 1)
                nc.scalar.activation(xn2T[:, 3 * half:3 * half + 3, t * P:(t + 1) * P],
                                     bank(i % 4)[:, 0:3 * P].rearrange("p (k n) -> p k n", k=3), ACT.Copy).then_inc(xt_free, 1)
            for i, (c0, n) in enumerate(CH):
                act.wait_ge(d_full, i + 1)
                nc.scalar.activation(fT[:, c0:c0 + n], bank(4 + i)[0:R, 0:n], ACT.Gelu).then_inc(f_ready, 1)
            for t in range(NT):
                act.wait_ge(r_full, t + 1)
                nc.scalar.activation(le[:, t, :], bank(t % 4)[0:P, 0:W], ACT.Copy).then_inc(r_free, 1)
            act.wait_ge(el_ready, 1)
            nc.scalar.activation(el[:, :, :], el[:, :, :], ACT.Exp).then_inc(ex_ready, 1)

        @block.tensor
        def _(pe):
            for i in range(2 * NT):
                t, half = i // 2, i % 2
                if not half:
                    pe.wait_ge(xn_ready, t + 1)
                if i >= 4:
                    pe.wait_ge(xt_free, i - 3)
                for k in range(3):
                    f = 3 * half + k
                    last = nc.tensor.transpose(bank(i % 4)[:, k * P:(k + 1) * P], xn[t % 3][:, f * 128:(f + 1) * 128], ident[0:P, 0:P])
                last.then_inc(xt_full, 1)
            pe.wait_ge(xt_free, 2 * NT)
            pe.wait_ge(w_in, 80)
            for i, (c0, n) in enumerate(CH):
                for k in range(KT):
                    last = nc.tensor.matmul(bank(4 + i)[0:R, 0:n], wd[:, k, :], xn2T[:, k, c0:c0 + n], start=k == 0, stop=k == KT - 1)
                last.then_inc(d_full, 1)
            pe.wait_ge(f_ready, len(CH))
            for t in range(NT):
                if t >= 4:
                    pe.wait_ge(r_free, t - 3)
                nc.tensor.matmul(bank(t % 4)[0:P, 0:W], fT[:, t * P:(t + 1) * P], wr, start=True, stop=True).then_inc(r_full, 1)
            pe.wait_ge(comb_ready, 1)
            for b, (t0, n) in enumerate(((0, 4), (4, 4), (8, 2))):
                for t in range(n):
                    last = nc.tensor.transpose(bank(b)[0:R, t * P:(t + 1) * P], comb[:, t0 + t, :], ident[0:P, 0:P])
                last.then_inc(c_full, 1)
            pe.wait_ge(wu_ready, 1)
            for t in range(NT):
                if t in (0, 4, 8):
                    pe.wait_ge(full_ready, t // 4 + 1)
                for half in range(2):
                    i = 2 * t + half
                    if i >= 5:
                        pe.wait_ge(y_ready, i - 4)
                    nc.tensor.matmul(bank(3 + i % 5)[0:P, 0:384], fT[:, t * P:(t + 1) * P], wu[:, 384 * half:384 * (half + 1)],
                                     start=True, stop=True).then_inc(up_full, 1)


def kernel(**inputs):
    import numpy as np
    import concourse.bacc as bacc
    from concourse.bass_utils import run_bass_kernel_spmd

    a = {k: np.asarray(v) for k, v in inputs.items()}

    def tiles(w):
        return w.reshape(-1, 128, w.shape[-1]).transpose(1, 0, 2)

    gat = [a[f"L0_gnn_W{i}"] for i in range(LAYERS)]
    qkv = a["L0_mix_W_qkv"].T.reshape(KT, 128, 3, PAIRS, 128).transpose(3, 1, 0, 2, 4).reshape(PAIRS, 128, KT, 384)
    data = {
        "x": a["x"],
        "src_t": a["src"].reshape(ET, P).T,
        "dst_t": a["dst"].reshape(ET, P).T,
        "dst_c": a["dst"].reshape(CHUNKS, CE * P),
        "w_ah": a["L0_gnn_W_ah"].reshape(KT, 128, KT, 128).transpose(2, 1, 0, 3),
        "b_ah": a["L0_gnn_b_ah"].reshape(KT, 128).T,
        "w_gat": np.stack([tiles(w) for w in gat]),
        "a_gat": np.stack([np.stack([a[f"L0_gnn_a_src{i}"].reshape(D), a[f"L0_gnn_a_dst{i}"].reshape(D)]) for i in range(LAYERS)]),
        "w_pair": np.stack(([tiles(w[:, c:c + PC]) for w in gat for c in (0, PC)] * 2)[1:PAIRS + 1]),
        "b_gat": np.stack([a[f"L0_gnn_b{i}"] for i in range(LAYERS)]).reshape(PAIRS, PC),
        "w_out": a["L0_gnn_W_out"].reshape(PAIRS, PK, 128, D).transpose(0, 2, 1, 3),
        "b_out": a["L0_gnn_b_out"],
        "w_qkv": np.concatenate([qkv[1:], qkv[:1]]),
        "w_proj": tiles(a["L0_mix_W_proj"].T),
        "b_proj": a["L0_mix_b_proj"],
        "w_down": tiles(a["L0_ffn_Wd"].T),
        "w_route": np.concatenate([a["L0_ffn_Wg"].T, a["L0_ffn_We"].reshape(EX * R, R).T], axis=1),
        "b_exp": a["L0_ffn_be"].reshape(EX * R),
        "w_up": a["L0_ffn_Wu"].T,
        "gamma": a["L0_ffn_gamma"],
    }
    nc = bacc.Bacc("TRN2", target_bir_lowering=False, num_devices=1)
    arrays, args = {}, []
    for name, v in data.items():
        arrays[f"in_{name}"] = np.ascontiguousarray(v)
        args.append(nc.dram_tensor(f"in_{name}", v.shape, mybir.dt.from_np(v.dtype), kind="ExternalInput").ap())
    args.append(nc.dram_tensor("out_0", (N, D), F32, kind="ExternalOutput").ap())
    build(nc, *args)
    r = run_bass_kernel_spmd(nc, [arrays], core_ids=[0])
    return r.results[0]["out_0"]
```

```python
from contextlib import ExitStack

import concourse.bass as bass
from concourse import mybir

F32 = mybir.dt.float32
F32R = mybir.dt.float32r
BF16 = mybir.dt.bfloat16
FP16 = mybir.dt.float16
I16 = mybir.dt.int16
I32 = mybir.dt.int32
U8 = mybir.dt.uint8
ALU = mybir.AluOpType
ACT = mybir.ActivationFunctionType
AX = mybir.AxisListType

N = 1250
P = 125
NT = N // P
D = 768
KT = D // 128
LAYERS = 3
HL = 4
C = D // HL
HEADS = LAYERS * HL
PAIRS = HEADS // 2
PC = 2 * C
PK = PC // 128
E = 20000
ET = E // P
CE = 4
CHUNKS = ET // CE
R = 64
EX = 4
CLS = 5
EPS = 1e-5
SLOPE = 0.2


def whole(n):
    return -(-n // 32) * 32


ROW = 4 * N
X1_AT = whole(2 * NT * N)
MASK_AT = whole(X1_AT + KT * ROW)
XN_AT = whole(MASK_AT + NT * N)
XL_AT = whole(XN_AT + KT * ROW)
STAGE_AT = whole(XL_AT + KT * ROW)
ACC_AT = MASK_AT + 4 * 3008
ARENA = 206720

CH = [(0, 418), (418, 416), (834, 416)]
DH = 64




class Counter:

    def __init__(self, engine, sem):
        self.engine, self.sem, self.n = engine, sem, 0

    def done(self, instruction):
        self.n += 1
        instruction.then_inc(self.sem, 1)
        self.engine.wait_ge(self.sem, self.n)


def split_matmul(nc, psum, stationary, moving, first, last):
    (s_high, s_low), (m_high, m_low) = stationary, moving
    nc.tensor.matmul(psum, s_high, m_high, start=first, stop=False)
    nc.tensor.matmul(psum, s_high, m_low, start=False, stop=False)
    return nc.tensor.matmul(psum, s_low, m_high, start=False, stop=last)


def build(nc, x, src_t, dst_t, dst_c, w_ah, b_ah, w_gat, a_gat, w_pair, b_gat, w_out, b_out,
          w_qkv, w_proj, b_proj, w_down, w_route, b_exp, w_up, gamma, out):
    def scratch(name, shape):
        return nc.dram_tensor("scratch_" + name, shape, F32, kind="Internal").ap()

    dram_ends = scratch("ends", (CHUNKS, 2))
    dram_a, dram_low = scratch("a", (HEADS, N)), scratch("low", (HEADS, 1))
    dram_uv = scratch("uv", (2 * HEADS, N))
    dram_den, dram_rec = scratch("den", (HEADS, N)), scratch("rec", (HEADS, N))
    dram_y = scratch("y", (PAIRS, 128, N))
    dram_res = scratch("res", (NT, P, D))
    ctx = ExitStack()
    with ctx:
        def sb(name, shape, dt=F32):
            return ctx.enter_context(nc.sbuf_tensor(name, shape, dt))

        base = -(-nc.sbuf_base // 32) * 32
        sb("arena", [128, ARENA // 4])

        def at(name, offset, shape, dt=F32):
            return nc.alloc_sbuf_tensor_at(name, shape, dt, offset=base + offset)

        cnt = at("cnt", 0, [P, NT, N], I16)
        x1T = at("x1T", X1_AT, [128, KT, N])
        mask = at("mask", MASK_AT, [P, NT, N], U8)
        xnh = at("xnh", XN_AT, [128, KT, N], F32R)
        xnl = at("xnl", XL_AT, [128, KT, N], F32R)
        acc = at("acc", ACC_AT, [P, NT, D])
        ident = sb("ident", [128, 128])
        identb = sb("identb", [128, 128], BF16)
        ones = sb("ones", [128, DH])
        ab = sb("ab", [P, NT, 2 * HEADS])
        acol = sb("acol", [P, HEADS, NT])
        ncol = sb("ncol", [P, HEADS, NT])
        bah = sb("bah", [128, KT])
        amax = sb("amax", [P, HEADS, NT])
        reach_row = sb("reach_row", [1, NT * 2], I32)

        psum = ctx.enter_context(nc.psum_tensor("psum", [128, 8 * 512], F32))

        def bank(b):
            return psum[:, 512 * b:512 * (b + 1)]

        wq_raw = at("wq_raw", STAGE_AT + 30720, [128, KT, 384])
        wq_high = at("wq_high", STAGE_AT + 39936, [128, KT, 384], F32R)
        wq_low = at("wq_low", STAGE_AT + 49152, [128, KT, 384], F32R)

        wp_first = at("wp_raw", ACC_AT + 4 * NT * D + 99520, [128, KT * PC])

        front(nc, locals())
        attention(nc, locals())
        projection(nc, locals())
        convolutions(nc, locals())
        adapter(nc, locals())


def front(nc, g):
    at, x1T, cnt, mask, xnh, xnl, ab, acol, ncol = (g[k] for k in "at x1T cnt mask xnh xnl ab acol ncol".split())
    ident, identb, ones, bank, psum = (g[k] for k in "ident identb ones bank psum".split())
    with ExitStack() as ctx:
        def sb(name, shape, dt=F32):
            return ctx.enter_context(nc.sbuf_tensor(name, shape, dt))

        def sem(name):
            return ctx.enter_context(nc.semaphore(name))

        xN = at("xN", STAGE_AT, [P, NT, D])
        wl = [at(f"wl{i}", 2 * KT * D * i, [128, KT // 2, D]) for i in range(2)]
        a_bc = at("a_bc", 4 * KT * D, [128, 2, D])
        prod = at("prod", MASK_AT + 4096, [128, C])
        hot_src = at("hot_src", STAGE_AT, [P, CE, N], BF16)
        hot_dst = at("hot_dst", STAGE_AT + 10016, [P, CE, 128], BF16)
        zero = at("zero", STAGE_AT + 11040, [P, 512], BF16)
        node_i = at("node_i", STAGE_AT + 12064, [P, N], I32)
        node_id = at("node_id", STAGE_AT + 17088, [P, N], FP16)
        some = [at(f"some{i}", STAGE_AT + 19616 + 2528 * i, [P, N], BF16) for i in range(2)]
        abT = at("abT", STAGE_AT + 24672, [2 * HEADS, N])
        WS = STAGE_AT + 30720
        w_raw = [at(f"wah_raw{i}", WS + 3072 * i, [128, KT, 128]) for i in range(2)]
        w_high = [at(f"wah_high{i}", WS + 3072 * (2 + i), [128, KT, 128], F32R) for i in range(2)]
        w_low = [at(f"wah_low{i}", WS + 3072 * (4 + i), [128, KT, 128], F32R) for i in range(2)]
        chunk_i = at("chunk_i", MASK_AT, [CHUNKS, CE * P], I32)
        chunk_f = at("chunk_f", MASK_AT + 2048, [CHUNKS, CE * P])
        wa = at("wa", MASK_AT + 7424, [128, KT, 2 * HEADS])
        spare = sb("spare", [1, 1])
        low = sb("low_a", [HEADS, 1])
        src_i, dst_i = at("src_i", MASK_AT + 4864, [P, ET], I32), at("dst_i", MASK_AT + 5504, [P, ET], I32)
        src_f, dst_f = at("src_f", MASK_AT + 6144, [P, ET]), at("dst_f", MASK_AT + 6784, [P, ET])
        ends = sb("ends", [CHUNKS, 2])
        ends_bc = sb("ends_bc", [NT, CHUNKS, 2])
        start_i, start = sb("start_i", [NT, 1], I32), sb("start", [NT, 2])
        chunk_no_i, chunk_no = sb("chunk_no_i", [NT, CHUNKS], I32), sb("chunk_no", [NT, CHUNKS])
        in_reach = sb("in_reach", [NT, CHUNKS])
        reach_f, reach = sb("reach_f", [NT, 2]), sb("reach", [NT, 2], I32)
        stats = sb("stats", [P, 2, 2, 6])
        moments = sb("moments", [P, NT, 2])
        rstd, std, eps = sb("rstd", [P, NT]), sb("std", [P, NT]), sb("eps", [P, 1])

        x_in = [sem(f"x_in{t}") for t in range(NT)]
        raw_in = [sem(f"raw_in{i}") for i in range(2)]
        wl_in = [sem(f"wl_in{i}") for i in range(2)]
        edges_in, high_ready, low_ready, xl_ready, a_low, bias_in, reach_in, wq_in, wq_ready = (sem(s) for s in "edges_in high_ready low_ready xl_ready a_low bias_in reach_in wq_in wq_ready".split())
        const_ready, wl_used, reach_ready, scores_out = (sem(s) for s in "const_ready wl_used reach_ready scores_out".split())
        xn_ready, xt_full, xt_free, x1_full, x1_free = (sem(s) for s in "xn_ready xt_full xt_free x1_full x1_free".split())
        ab_full, at_full, at_ready = (sem(s) for s in "ab_full at_full at_ready".split())
        hot_ready, hot_free, cnt_full, cnt_free = (sem(s) for s in "hot_ready hot_free cnt_full cnt_free".split())
        some_ready, some_full, some_free, dve_own, pool_own = (
            sem(s) for s in "some_ready some_full some_free dve_own pool_own".split())
        eps_ready, ends_ready, ends_in = sem("eps_ready"), sem("ends_ready"), sem("ends_in")
        node_ready, var_ready, std_ready = sem("node_ready"), sem("var_ready"), sem("std_ready")
        block = ctx.enter_context(nc.Block())

        @block.sync
        def _(sp):
            def half_layer(i):
                layer, half = i // 2, i % 2
                if i >= 2:
                    sp.wait_ge(wl_used, i - 1)
                sp.dma_start(wl[half][:, :, :], g["w_gat"][layer, :, half * KT // 2:(half + 1) * KT // 2, :])\
                    .then_inc(wl_in[half], 16)
                if not half:
                    if layer:
                        sp.wait_ge(wl_used, i)
                    sp.dma_start(a_bc[:, :, :], g["a_gat"][layer].partition_broadcast(128)).then_inc(wl_in[0], 16)

            for t in range(NT):
                sp.dma_start(xN[:, t, :], g["x"][t * P:(t + 1) * P, :]).then_inc(x_in[t], 16)
                if t == 1:
                    sp.dma_start(chunk_i[:, :], g["dst_c"]).then_inc(edges_in, 16)
                    sp.dma_start(src_i[:, :], g["src_t"]).then_inc(edges_in, 16)
                    sp.dma_start(dst_i[:, :], g["dst_t"]).then_inc(edges_in, 16)
            half_layer(0)
            half_layer(1)
            for o in range(2):
                sp.dma_start(w_raw[o][:, :, :], g["w_ah"][o]).then_inc(raw_in[o], 16)
            sp.dma_start(g["bah"][:, :], g["b_ah"]).then_inc(bias_in, 16)
            sp.wait_ge(ends_ready, 1)
            sp.dma_start(g["dram_ends"], ends[:, :]).then_inc(ends_in, 16)
            sp.wait_ge(ends_in, 16)
            sp.dma_start(ends_bc[:, :, :], g["dram_ends"].partition_broadcast(NT)).then_inc(ends_in, 16)
            for i in range(2, 2 * LAYERS):
                half_layer(i)
            sp.wait_ge(reach_ready, 1)
            sp.dma_start(g["reach_row"][0:1, :], reach[:, :]).then_inc(reach_in, 16)
            sp.wait_ge(x1_full, 3 * KT)
            sp.dma_start(g["wq_raw"][:, :, :], g["w_qkv"][PAIRS - 1]).then_inc(wq_in, 16)
            sp.wait_ge(a_low, 2)
            sp.dma_start(g["dram_a"], abT[0:HEADS, :]).then_inc(scores_out, 16)
            sp.dma_start(g["dram_low"], low[:, :]).then_inc(scores_out, 16)
            sp.wait_ge(scores_out, 32)
            sp.wait_ge(bias_in, 16)

        @block.gpsimd
        def _(pool):
            own = Counter(pool, pool_own)
            nc.gpsimd.iota(start_i[:, :], pattern=[[0, 1]], base=0, channel_multiplier=P).then_inc(const_ready, 1)
            nc.gpsimd.iota(chunk_no_i[:, :], pattern=[[1, CHUNKS]], base=0, channel_multiplier=0).then_inc(const_ready, 1)
            own.done(nc.gpsimd.memset(ident[:, :], 0.0))
            nc.gpsimd.affine_select(out=ident[:, :], in_=ident[:, :], compare_op=ALU.not_equal, fill=1.0,
                                    base=0, pattern=[[-1, 128]], channel_multiplier=1).then_inc(const_ready, 1)
            pool.wait_ge(const_ready, 3)
            nc.gpsimd.tensor_copy(identb[:, :], ident[:, :]).then_inc(const_ready, 1)
            nc.gpsimd.memset(ones[:, :], 1.0).then_inc(const_ready, 1)
            for o in range(KT):
                pool.wait_ge(high_ready, o + 1)
                if o >= 2:
                    pool.wait_ge(x1_full, 3 * (o - 1))
                nc.gpsimd.tensor_tensor(w_low[o % 2][:, :, :], w_raw[o % 2][:, :, :], w_high[o % 2][:, :, :].bitcast(F32),
                                        ALU.subtract).then_inc(low_ready, 1)
            pool.wait_ge(xt_full, 2 * NT)
            nc.gpsimd.iota(node_i[:, :], pattern=[[1, N]], base=0, channel_multiplier=0).then_inc(node_ready, 1)
            nc.gpsimd.memset(zero[:, :], 0.0).then_inc(node_ready, 1)
            pool.wait_ge(wq_ready, 1)
            nc.gpsimd.tensor_tensor(g["wq_low"][:, :, :], g["wq_raw"][:, :, :], g["wq_high"][:, :, :].bitcast(F32),
                                    ALU.subtract).then_inc(wq_ready, 1)
            pool.wait_ge(wq_ready, 2)

        @block.vector
        def _(dve):
            own = Counter(dve, dve_own)
            nc.vector.memset(eps[:, :], EPS).then_inc(eps_ready, 1)

            def statistics(t):
                dve.wait_ge(x_in[t], 16)
                nc.vector.bn_stats(stats[:, t % 2, 0, :], xN[:, t, 0:D // 2]).then_inc(dve_own, 1)
                own.n += 1
                own.done(nc.vector.bn_stats(stats[:, t % 2, 1, :], xN[:, t, D // 2:D]))
                nc.vector.bn_aggr(moments[:, t, :], stats[:, t % 2, :, :]).then_inc(var_ready, 1)

            def low_part(i):
                t, half = i // 2, i % 2
                dve.wait_ge(xt_free, i + 1)
                part = (slice(None), slice(3 * half, 3 * half + 3), slice(t * P, (t + 1) * P))
                nc.vector.tensor_tensor(xnl[part], bank(i % 4)[:, 0:3 * P].rearrange("p (k n) -> p k n", k=3),
                                        xnh[part].bitcast(F32), ALU.subtract).then_inc(xl_ready, 1)

            statistics(0)
            for t in range(NT):
                if t + 1 < NT:
                    statistics(t + 1)
                if t >= 1:
                    low_part(2 * t - 2)
                    low_part(2 * t - 1)
                dve.wait_ge(std_ready, t + 1)
                own.done(nc.vector.reciprocal(rstd[:, t:t + 1], std[:, t:t + 1]))
                nc.vector.tensor_scalar(xN[:, t, :], xN[:, t, :], moments[:, t, 0:1], rstd[:, t:t + 1],
                                        ALU.subtract, ALU.mult).then_inc(xn_ready, 1)
                if t == 2:
                    dve.wait_ge(edges_in, 48)
                    own.done(nc.vector.tensor_copy(chunk_f[:, :], chunk_i[:, :]))
                    own.done(nc.vector.tensor_copy(src_f[:, :], src_i[:, :]))
                    own.done(nc.vector.tensor_copy(dst_f[:, :], dst_i[:, :]))
                    own.done(nc.vector.tensor_reduce(ends[:, 0:1], chunk_f[:, :], axis=AX.X, op=ALU.min))
                    nc.vector.tensor_reduce(ends[:, 1:2], chunk_f[:, :], axis=AX.X, op=ALU.max).then_inc(ends_ready, 1)
            low_part(2 * NT - 2)
            low_part(2 * NT - 1)
            dve.wait_ge(const_ready, 2)
            own.done(nc.vector.tensor_copy(start[:, 0:1], start_i[:, :]))
            own.done(nc.vector.tensor_scalar(start[:, 1:2], start[:, 0:1], float(P), None, ALU.add))
            own.done(nc.vector.tensor_copy(chunk_no[:, :], chunk_no_i[:, :]))
            dve.wait_ge(ends_in, 32)
            own.done(nc.vector.tensor_scalar(in_reach[:, :], ends_bc[:, :, 0], start[:, 1:2], None, ALU.is_lt))
            own.done(nc.vector.scalar_tensor_tensor(in_reach[:, :], ends_bc[:, :, 1], start[:, 0:1], in_reach[:, :],
                                                    op0=ALU.is_ge, op1=ALU.mult))
            far = float(2 * CHUNKS)
            own.done(nc.vector.tensor_scalar(in_reach[:, :], in_reach[:, :], -1.0, -far, ALU.add, ALU.mult))
            own.done(nc.vector.tensor_tensor(ends_bc[:, :, 0], chunk_no[:, :], in_reach[:, :], ALU.add))
            own.done(nc.vector.tensor_tensor(ends_bc[:, :, 1], chunk_no[:, :], in_reach[:, :], ALU.subtract))
            own.done(nc.vector.tensor_reduce(reach_f[:, 0:1], ends_bc[:, :, 0], axis=AX.X, op=ALU.min))
            own.done(nc.vector.tensor_reduce(reach_f[:, 1:2], ends_bc[:, :, 1], axis=AX.X, op=ALU.max))
            own.done(nc.vector.tensor_scalar(reach_f[:, 0:1], reach_f[:, 0:1], float(CHUNKS - 1), None, ALU.min))
            own.done(nc.vector.tensor_scalar(reach_f[:, 1:2], reach_f[:, 1:2], 0.0, 1.0, ALU.max, ALU.add))
            nc.vector.tensor_copy(reach[:, :], reach_f[:, :]).then_inc(reach_ready, 1)
            for layer in range(LAYERS):
                for k in range(KT):
                    half = k * 2 // KT
                    if k % (KT // 2) == 0:
                        dve.wait_ge(wl_in[half], (16 if half else 32) * (layer + 1))
                    for s in range(2):
                        for h in range(HL):
                            col = s * HEADS + layer * HL + h
                            last = nc.vector.tensor_tensor_reduce(
                                out=prod[:, :], in0=wl[half][:, k % (KT // 2), h * C:(h + 1) * C],
                                in1=a_bc[:, s, h * C:(h + 1) * C],
                                scale=1.0, scalar=0.0, op0=ALU.mult, op1=ALU.add, accum_out=wa[:, k, col:col + 1])
                            if (k + 1) % (KT // 2) == 0 and s and h == HL - 1:
                                last.then_inc(wl_used, 1)
                                dve.wait_ge(wl_used, 2 * layer + half + 1)
                            else:
                                own.done(last)
            dve.wait_ge(node_ready, 1)
            own.done(nc.vector.tensor_copy(node_id[:, :], node_i[:, :]))
            dve.sem_inc(hot_free, CE)
            dve.wait_ge(reach_in, 16)
            units = dve.alloc_register("dve_units")
            dve.reg_mov(units, 0)
            with dve.Fori(0, NT) as it:
                first = dve.value_load(g["reach_row"][0:1, bass.ds(2 * it, 1)], min_val=0, max_val=CHUNKS - 1)
                final = dve.value_load(g["reach_row"][0:1, bass.ds(2 * it + 1, 1)], min_val=1, max_val=CHUNKS)
                with dve.Fori(first, final) as c:
                    for e in range(CE):
                        dve.reg_add(units, units, 1)
                        dve.wait_ge(hot_free, dve.snap(units))
                        nc.vector.tensor_scalar(hot_dst[:, e, 0:P], node_id[:, bass.ds(it * P, P)],
                                                dst_f[:, bass.ds(c * CE + e, 1)], None, ALU.is_equal)\
                            .then_inc(hot_ready, 1)
                        nc.vector.tensor_scalar(hot_src[:, e, :], node_id[:, :], src_f[:, bass.ds(c * CE + e, 1)],
                                                None, ALU.is_equal).then_inc(hot_ready, 1)
            for j in range(NT):
                dve.wait_ge(cnt_free, 1 + 4 * NT)
                if j >= 2:
                    dve.wait_ge(some_full, 2 * (j - 1))
                nc.vector.tensor_scalar(some[j % 2][:, :], cnt[:, j, :], 1.0, None, ALU.min).then_inc(some_ready, 1)
            aT = abT[0:HEADS, :]
            dve.wait_ge(at_ready, len(CH))
            own.done(nc.vector.tensor_reduce(low[:, :], aT, axis=AX.X, op=ALU.min))
            dve.wait_ge(ab_full, 1)
            own.done(nc.vector.tensor_copy(ab[:, :, :], bank(7)[0:P, 0:NT * 2 * HEADS].rearrange("p (t h) -> p t h", t=NT)))
            own.done(nc.vector.tensor_copy(acol[:, :, :], ab[:, :, 0:HEADS].rearrange("p t h -> p h t")))
            own.done(nc.vector.tensor_scalar(ncol[:, :, :], acol[:, :, :], SLOPE - 1.0, None, ALU.mult))
            nc.vector.tensor_scalar(aT, aT, low[:, :], None, ALU.subtract).then_inc(a_low, 2)


        @block.scalar
        def _(act):
            def deviation(t):
                act.wait_ge(var_ready, t + 1)
                nc.scalar.activation(std[:, t:t + 1], moments[:, t, 1:2], ACT.Sqrt, bias=eps[:, :]).then_inc(std_ready, 1)

            act.wait_ge(eps_ready, 1)
            deviation(0)
            for i in range(2 * NT):
                t, half = i // 2, i % 2
                if half == 0 and t + 1 < NT:
                    deviation(t + 1)
                act.wait_ge(xt_full, i + 1)
                nc.scalar.activation(xnh[:, 3 * half:3 * half + 3, t * P:(t + 1) * P],
                                     bank(i % 4)[:, 0:3 * P].rearrange("p (k n) -> p k n", k=3), ACT.Copy)\
                    .then_inc(xt_free, 1)

            def high_part(o):
                act.wait_ge(raw_in[o % 2], 16 * (o // 2 + 1))
                if o >= 2:
                    act.wait_ge(x1_full, 3 * (o - 1))
                nc.scalar.activation(w_high[o % 2][:, :, :], w_raw[o % 2][:, :, :], ACT.Copy).then_inc(high_ready, 1)

            high_part(0)
            high_part(1)
            act.wait_ge(bias_in, 16)
            for i in range(KT * 3):
                o, (c0, n) = i // 3, CH[i % 3]
                if i % 3 == 0 and 1 <= o < KT - 1:
                    high_part(o + 1)
                act.wait_ge(x1_full, i + 1)
                nc.scalar.activation(x1T[:, o, c0:c0 + n], bank(4 + i % 3)[:, 0:n], ACT.Relu,
                                     bias=g["bah"][:, o:o + 1]).then_inc(x1_free, 1)
                if i % 3 == 0 and o + 2 < KT:
                    act.wait_ge(low_ready, o + 1)
                    act.dma_start(w_raw[o % 2][:, :, :], g["w_ah"][o + 2]).then_inc(raw_in[o % 2], 16)
            act.wait_ge(wq_in, 16)
            act.wait_ge(x1_full, 3 * KT)
            nc.scalar.activation(g["wq_high"][:, :, :], g["wq_raw"][:, :, :], ACT.Copy).then_inc(wq_ready, 1)
            act.sem_inc(cnt_free, 1)
            with act.Fori(0, NT) as it:
                act.wait_ge(cnt_full, it + 1)
                nc.scalar.activation(spare[:, :], eps[0:1, :], ACT.Copy).then_inc(cnt_free, 1)
                for b, tiles in enumerate((4, 4, 2)):
                    nc.scalar.activation(cnt[:, 4 * b:4 * b + tiles, bass.ds(it * P, P)],
                                         bank(b)[0:P, 0:128 * tiles].rearrange("p (j n) -> p j n", n=128)[:, :, 0:P],
                                         ACT.Copy).then_inc(cnt_free, 1)
            for i, (c0, n) in enumerate(CH):
                act.wait_ge(at_full, i + 1)
                nc.scalar.activation(abT[:, c0:c0 + n], bank(4 + i)[0:2 * HEADS, 0:n], ACT.Copy).then_inc(at_ready, 1)
            for i in range(2 * NT):
                j, half = i // 2, i % 2
                act.wait_ge(some_full, i + 1)
                nc.scalar.activation(mask[:, 5 * half:5 * half + 5, j * P:(j + 1) * P],
                                     bank(3 + i % 4)[0:P, :].bitcast(BF16)[:, 0:640].rearrange("p (t n) -> p t n", n=128)[:, :, 0:P],
                                     ACT.Copy).then_inc(some_free, 1)

        @block.tensor
        def _(pe):
            pe.wait_ge(const_ready, 5)
            for i in range(2 * NT):
                t, half = i // 2, i % 2
                if not half:
                    pe.wait_ge(xn_ready, t + 1)
                if i >= 4:
                    pe.wait_ge(xl_ready, i - 3)
                for k in range(3):
                    f = 3 * half + k
                    last = nc.tensor.transpose(bank(i % 4)[:, k * P:(k + 1) * P], xN[:, t, f * 128:(f + 1) * 128],
                                               ident[0:P, 0:P])
                last.then_inc(xt_full, 1)
            pe.wait_ge(xl_ready, 2 * NT)
            for i in range(KT * 3):
                o, (c0, n) = i // 3, CH[i % 3]
                if i % 3 == 0:
                    pe.wait_ge(low_ready, o + 1)
                if i >= 3:
                    pe.wait_ge(x1_free, i - 2)
                for k in range(KT):
                    last = split_matmul(nc, bank(4 + i % 3)[:, 0:n], (w_high[o % 2][:, k, :], w_low[o % 2][:, k, :]),
                                        (xnh[:, k, c0:c0 + n], xnl[:, k, c0:c0 + n]), k == 0, k == KT - 1)
                last.then_inc(x1_full, 1)
            pe.wait_ge(x1_free, KT * 3)
            pe.wait_ge(node_ready, 2)
            pe.wait_ge(reach_in, 16)
            units = pe.alloc_register("pe_units")
            pe.reg_mov(units, 0)
            with pe.Fori(0, NT) as it:
                pe.wait_ge(cnt_free, 4 * it + 1)
                for b, n in enumerate((512, 512, 256)):
                    nc.tensor.matmul(bank(b)[0:P, 0:n], zero[:, 0:P], zero[:, 0:n], start=True,
                                     stop=False, skip_group_check=True)
                first = pe.value_load(g["reach_row"][0:1, bass.ds(2 * it, 1)], min_val=0, max_val=CHUNKS - 1)
                final = pe.value_load(g["reach_row"][0:1, bass.ds(2 * it + 1, 1)], min_val=1, max_val=CHUNKS)
                with pe.Fori(first, final) as c:
                    for e in range(CE):
                        pe.reg_add(units, units, 2)
                        pe.wait_ge(hot_ready, pe.snap(units))
                        for j in range(NT):
                            last = nc.tensor.matmul(psum[0:P, 128 * j:128 * j + P], hot_src[:, e, j * P:(j + 1) * P],
                                                    hot_dst[:, e, 0:P], start=False, stop=False, skip_group_check=True)
                        last.then_inc(hot_free, 1)
                nc.tensor.matmul(psum[0:P, bass.ds(it * 128, P)], identb[0:P, 0:P], identb[0:P, 0:P], start=False,
                                 stop=True, skip_group_check=True).then_inc(cnt_full, 1)
            pe.wait_ge(wl_used, 2 * LAYERS)
            for i, (c0, n) in enumerate(CH):
                for k in range(KT):
                    last = nc.tensor.matmul(bank(4 + i)[0:2 * HEADS, 0:n], wa[:, k, :], x1T[:, k, c0:c0 + n],
                                            start=k == 0, stop=k == KT - 1)
                last.then_inc(at_full, 1)
            pe.wait_ge(at_ready, len(CH))
            for t in range(NT):
                last = nc.tensor.transpose(bank(7)[0:P, t * 2 * HEADS:(t + 1) * 2 * HEADS], abT[:, t * P:(t + 1) * P],
                                           ident[0:2 * HEADS, 0:2 * HEADS])
            last.then_inc(ab_full, 1)
            for i in range(2 * NT):
                j, half = i // 2, i % 2
                if not half:
                    pe.wait_ge(some_ready, j + 1)
                if i >= 4:
                    pe.wait_ge(some_free, i - 3)
                for k in range(5):
                    t = 5 * half + k
                    last = nc.tensor.transpose(bank(3 + i % 4)[0:P, :].bitcast(BF16)[:, 128 * k:128 * k + P],
                                               some[j % 2][:, t * P:(t + 1) * P], identb[0:P, 0:P])
                last.then_inc(some_full, 1)


def attention(nc, g):
    at, xnh, xnl, mask, amax, ones, bank = (g[k] for k in "at xnh xnl mask amax ones bank".split())
    with ExitStack() as ctx:
        def sb(name, shape, dt=F32):
            return ctx.enter_context(nc.sbuf_tensor(name, shape, dt))

        def sem(name):
            return ctx.enter_context(nc.semaphore(name))

        w_raw, w_high, w_low = g["wq_raw"], g["wq_high"], g["wq_low"]
        S = STAGE_AT
        kf = at("kf", S, [P, NT, 128])
        vf = at("vf", S + 5120, [P, NT, 129])
        qf = at("qf", S + 10304, [128, N])
        ke = at("ke", S + 15328, [P, 2, 2, 128])
        qe = [at(f"qe{i}", S + 17376 + 1696 * i, [128, 418]) for i in range(2)]
        y = at("y", S + 20768, [128, N])
        junk = at("junk", S + 25792, [P, N], BF16)
        arow = [at(f"arow{i}", S + 58368 + 5024 * i, [P, N]) for i in range(2)]
        den = at("den", S + 68416, [128, N])
        kvb, ksb = sb("kvb", [128, 128]), sb("ksb", [128, 128])
        ksum = sb("ksum", [128, 1])
        head_amax = sb("head_amax", [P, 2, NT])
        spare = sb("spare2", [1, 1])

        arow_in = [sem(f"arow_in{i}") for i in range(2)]
        (raw_in, kv_high, kv_low, q_high, q_low_w, kv_full, k_exp, k_ready, q_full,
         q_exp, q_ready, acc_full, kvb_ready, num_full, y_ready, y_out, head_max, dve_own, zeroed, ones_col) = (sem(s) for s in (
             "raw_in kv_high kv_low q_high q_low_w kv_full k_exp k_ready q_full "
             "q_exp q_ready acc_full kvb_ready num_full y_ready y_out head_max attn_own zeroed ones_col").split())
        block = ctx.enter_context(nc.Block())
        KG = NT // 2
        ND = [(6, 7), (5, 2), (6, 7)]

        @block.sync
        def _(sp):
            with sp.Fori(0, PAIRS) as i:
                sp.wait_ge(q_low_w, 1 + i)
                sp.dma_start(w_raw[:, :, :], g["w_qkv"][bass.ds(i, 1), :, :, :].rearrange("a p k c -> (a p) k c"))\
                    .then_inc(raw_in, 16)
                sp.wait_ge(y_ready, 1 + 6 * (i + 1))
                sp.dma_start(g["dram_y"][bass.ds(i, 1), :, :].rearrange("a p n -> (a p) n"), y[:, :]).then_inc(y_out, 16)
                for h in range(2):
                    sp.dma_start(g["dram_den"][bass.ds(2 * i + h, 1), :], den[DH * h:DH * h + 1, :]).then_inc(y_out, 16)
            sp.wait_ge(y_out, 1 + 48 * PAIRS)
            sp.wait_ge(raw_in, 16 * PAIRS)

        @block.gpsimd
        def _(pool):
            nc.gpsimd.memset(kvb[:, :], 0.0).then_inc(zeroed, 1)
            nc.gpsimd.memset(ksb[:, :], 0.0).then_inc(zeroed, 1)
            nc.gpsimd.memset(vf[:, :, 128:129], 1.0).then_inc(ones_col, 1)

            def low_parts(part, high, low_sem, n):
                pool.wait_ge(high, n)
                nc.gpsimd.tensor_tensor(w_low[:, :, part], w_raw[:, :, part], w_high[:, :, part].bitcast(F32),
                                        ALU.subtract).then_inc(low_sem, 1)

            with pool.Fori(0, PAIRS) as i:
                for s in range(2):
                    pool.wait_ge(head_max, 2 * i + s + 1)
                    pool.dma_start(arow[s][:, :], g["dram_a"][bass.ds(2 * i + s, 1), :].to_broadcast([P, N]))\
                        .then_inc(arow_in[s], 16)
                low_parts(slice(128, 384), kv_high, kv_low, i + 1)
                low_parts(slice(0, 128), q_high, q_low_w, i + 1)

        @block.vector
        def _(dve):
            dve.sem_inc(head_max, 2)
            dve.wait_ge(zeroed, 2)
            LINKS_PER_PAIR = 2 * NT + 1
            with dve.Fori(0, PAIRS) as i:
                steps = [(s, t) for s in range(2) for t in range(NT)]
                link = [0]

                def chain(instruction):
                    link[0] += 1
                    instruction.then_inc(dve_own, 1)
                    dve.wait_ge(dve_own, i * LINKS_PER_PAIR + link[0])

                def maxima(n):
                    for _ in range(n):
                        s, t = steps.pop(0)
                        if t == 0:
                            dve.wait_ge(arow_in[s], 16 * (i + 1))
                        nc.vector.memset(spare[:, :], 0.0)
                        chain(nc.vector.tensor_tensor_reduce(
                            out=junk[:, :], in0=mask[:, t, :], in1=arow[s][:, :], scale=1.0, scalar=0.0, op0=ALU.mult,
                            op1=ALU.max, accum_out=head_amax[:, s, t:t + 1]))
                        if t == NT - 1:
                            nc.vector.tensor_copy(amax[:, bass.ds(2 * i + s, 1), :].rearrange("p a t -> p (a t)"),
                                                  head_amax[:, s, :]).then_inc(head_max, 1)
                            dve.wait_ge(head_max, 2 * i + s + 3)

                def k_features(gr):
                    dve.wait_ge(k_exp, 1 + KG * i + gr + 1)
                    here = kf[:, 2 * gr:2 * gr + 2, :]
                    nc.vector.scalar_tensor_tensor(here, ke[:, gr % 2, :, :], 1.0, here, op0=ALU.min, op1=ALU.max)\
                        .then_inc(k_ready, 1)

                def q_features(c):
                    c0, n = CH[c]
                    dve.wait_ge(q_exp, 1 + 3 * i + c + 1)
                    nc.vector.scalar_tensor_tensor(qf[:, c0:c0 + n], qe[c % 2][:, 0:n], 1.0, qf[:, c0:c0 + n],
                                                   op0=ALU.min, op1=ALU.max).then_inc(q_ready, 1)

                for gr in range(KG):
                    maxima(2)
                    k_features(gr)
                for c, (c0, n) in enumerate(CH):
                    maxima(2)
                    q_features(c)
                    if c == 1:
                        dve.wait_ge(acc_full, i + 1)
                        for h in range(2):
                            b = slice(DH * h, DH * (h + 1))
                            nc.vector.tensor_copy(kvb[b, b], bank(5)[b, b]).then_inc(kvb_ready, 1)
                        chain(nc.vector.tensor_copy(ksum[:, :], bank(5)[:, 128:129]))
                        for h in range(2):
                            b = slice(DH * h, DH * (h + 1))
                            nc.vector.tensor_scalar(ksb[b, b], ones[b, :], ksum[b, :], None, ALU.mult).then_inc(kvb_ready, 1)
                maxima(len(steps))

        @block.scalar
        def _(act):
            def high_parts(part, high, turn, used, count):
                act.wait_ge(raw_in, 16 * turn)
                act.wait_ge(used, count)
                nc.scalar.activation(w_high[:, :, part], w_raw[:, :, part], ACT.Copy).then_inc(high, 1)

            with act.Fori(0, PAIRS) as i:
                for gr in range(KG):
                    kb = bank(gr % 3)[0:P, :].rearrange("p (t c) -> p t c", t=2)
                    act.wait_ge(kv_full, KG * i + gr + 1)
                    nc.scalar.activation(kf[:, 2 * gr:2 * gr + 2, :], kb[:, :, 0:128], ACT.Copy, bias=1.0)
                    nc.scalar.activation(vf[:, 2 * gr:2 * gr + 2, 0:128], kb[:, :, 128:256], ACT.Copy)
                    act.wait_ge(k_ready, 1 + KG * i + gr - 1 if gr else 1 + KG * i)
                    nc.scalar.activation(ke[:, gr % 2, :, :], kb[:, :, 0:128], ACT.Exp).then_inc(k_exp, 1)
                high_parts(slice(128, 384), kv_high, i + 1, kv_full, KG * (i + 1))
                for c, (c0, n) in enumerate(CH):
                    act.wait_ge(q_full, 3 * i + c + 1)
                    nc.scalar.activation(qf[:, c0:c0 + n], bank(3 + c % 2)[:, 0:n], ACT.Copy, bias=1.0)
                    act.wait_ge(q_ready, 1 + 3 * i + c - 1 if c else 1 + 3 * i)
                    nc.scalar.activation(qe[c % 2][:, 0:n], bank(3 + c % 2)[:, 0:n], ACT.Exp).then_inc(q_exp, 1)
                high_parts(slice(0, 128), q_high, i + 1, q_full, 3 * (i + 1))
                act.wait_ge(y_out, 1 + 48 * i)
                for c, (c0, n) in enumerate(CH):
                    num, dn = ND[c]
                    act.wait_ge(num_full, 3 * i + c + 1)
                    nc.scalar.activation(y[:, c0:c0 + n], bank(num)[:, 0:n], ACT.Copy).then_inc(y_ready, 1)
                    nc.scalar.activation(den[:, c0:c0 + n], bank(dn)[:, 0:n], ACT.Copy).then_inc(y_ready, 1)

        @block.tensor
        def _(pe):
            for s in (y_ready, y_out, kvb_ready, k_ready, k_exp, q_ready, q_exp, kv_low, q_low_w):
                pe.sem_inc(s, 1)
            pe.wait_ge(ones_col, 1)
            with pe.Fori(0, PAIRS) as i:
                pe.wait_ge(kv_low, 1 + i)
                for gr in range(KG):
                    pe.wait_ge(k_exp, 1 + KG * i + (gr - 2 if gr >= 3 else 0))
                    if gr == 2:
                        pe.wait_ge(y_ready, 1 + 6 * i)
                    for t in range(2):
                        nt = slice((2 * gr + t) * P, (2 * gr + t + 1) * P)
                        for k in range(KT):
                            last = split_matmul(nc, bank(gr % 3)[0:P, 256 * t:256 * (t + 1)],
                                                (xnh[:, k, nt], xnl[:, k, nt]),
                                                (w_high[:, k, 128:384], w_low[:, k, 128:384]), k == 0, k == KT - 1)
                    last.then_inc(kv_full, 1)
                pe.wait_ge(q_low_w, 1 + i)
                pe.wait_ge(q_exp, 1 + 3 * i)
                for c, (c0, n) in enumerate(CH):
                    if c == 2:
                        pe.wait_ge(k_ready, 1 + KG * (i + 1))
                        for t in range(NT):
                            last = nc.tensor.matmul(bank(5)[:, 0:129], kf[:, t, :], vf[:, t, :], start=t == 0, stop=t == NT - 1)
                        last.then_inc(acc_full, 1)
                        pe.wait_ge(q_exp, 1 + 3 * i + 1)
                    for k in range(KT):
                        last = split_matmul(nc, bank(3 + c % 2)[:, 0:n], (w_high[:, k, 0:128], w_low[:, k, 0:128]),
                                            (xnh[:, k, c0:c0 + n], xnl[:, k, c0:c0 + n]), k == 0, k == KT - 1)
                    last.then_inc(q_full, 1)
                pe.wait_ge(kvb_ready, 1 + 4 * (i + 1))
                for c, (c0, n) in enumerate(CH):
                    num, dn = ND[c]
                    pe.wait_ge(q_ready, 1 + 3 * i + c + 1)
                    if c == 2:
                        pe.wait_ge(y_ready, 1 + 6 * i + 2)
                    nc.tensor.matmul(bank(dn)[:, 0:n], ksb[:, :], qf[:, c0:c0 + n], start=True, stop=True)
                    nc.tensor.matmul(bank(num)[:, 0:n], kvb[:, :], qf[:, c0:c0 + n], start=True, stop=True)\
                        .then_inc(num_full, 1)


def projection(nc, g):
    at, bank, ab, amax, ident = (g[k] for k in "at bank ab amax ident".split())
    with ExitStack() as ctx:
        def sb(name, shape, dt=F32):
            return ctx.enter_context(nc.sbuf_tensor(name, shape, dt))

        def sem(name):
            return ctx.enter_context(nc.semaphore(name))

        yh = at("yh", XN_AT, [128, KT, N], F32R)
        yl = at("yl", XL_AT, [128, KT, N], F32R)
        wh = at("wproj_high", STAGE_AT, [128, KT, D], F32R)
        wl = at("wproj_low", STAGE_AT + 18432, [128, KT, D], F32R)
        S = STAGE_AT + 36864
        w_raw = [at(f"wproj_raw{i}", S + 3072 * i, [128, D]) for i in range(2)]
        y_raw = [at(f"y_raw{i}", o, [128, N]) for i, o in enumerate((MASK_AT, MASK_AT + 5024, S + 14240))]
        head_of = at("head_of", S + 6144, [HEADS, D])
        recT = at("recT", S + 9216, [HEADS, N])
        xt = [at(f"xt{i}", S + 14240 + 3072 * i, [P, D]) for i in range(3)]
        bp = at("bp", S + 23456, [P, D])
        uvT = at("uvT", S + 26528, [2 * HEADS, N])
        DR = HEADS * N // P
        den = sb("den_rows", [DR, P])
        low, m, uv = sb("low", [P, HEADS]), sb("m", [P, NT, HEADS]), sb("uv", [P, NT, 2 * HEADS])
        y_in = [sem(f"y_in{i}") for i in range(3)]
        w_in = [sem(f"wproj_in{i}") for i in range(2)]
        x_in = [sem(f"xt_in{i}") for i in range(3)]
        res_out = [sem(f"res_out{i}") for i in range(3)]
        rec_in, wp_in, heads_own, rec_full, den_in, den_ready, rec_out, low_in = (
            sem(s) for s in "rec_in wp_in heads_own rec_full den_in den_ready rec_out low_in".split())
        uv_ready, uvt_full, uvt_ready, uv_out, norm_own, y_norm = (
            sem(s) for s in "uv_ready uvt_full uvt_ready uv_out norm_own y_norm".split())
        bp_in, wh_ready, wl_ready, yh_ready, yl_ready, xb_ready, p_full, p_free = (
            sem(s) for s in "bp_in wph_ready wpl_ready yh_ready yl_ready xb_ready p_full p_free".split())
        block = ctx.enter_context(nc.Block())

        RB = (6, 7)
        EARLY = 6

        @block.sync
        def _(sp):
            rows = [g[d].rearrange("h (r n) -> (h r) n", n=P) for d in ("dram_den", "dram_rec")]
            sp.dma_start(den[:, :], rows[0]).then_inc(den_in, 16)
            sp.dma_start(low[:, :], g["dram_low"].rearrange("h a -> (h a)").partition_broadcast(P)).then_inc(low_in, 16)
            for k in range(KT):
                if k >= 2:
                    sp.wait_ge(wl_ready, k - 1)
                if k >= 3:
                    sp.wait_ge(yl_ready, k - 2)
                sp.dma_start(w_raw[k % 2][:, :], g["w_proj"][:, k, :]).then_inc(w_in[k % 2], 16)
                sp.dma_start(y_raw[k % 3][:, :], g["dram_y"][k]).then_inc(y_in[k % 3], 16)
                if k == 0:
                    sp.wait_ge(den_ready, 1)
                    sp.dma_start(rows[1], den[:, :]).then_inc(rec_out, 16)
                    sp.wait_ge(rec_out, 16)
                    sp.dma_start(recT[:, :], g["dram_rec"]).then_inc(rec_in, 16)
            sp.dma_start(bp[:, :], g["b_proj"].partition_broadcast(P)).then_inc(bp_in, 16)
            sp.dma_start(g["wp_first"][:, :], g["w_pair"][PAIRS - 1].rearrange("p k c -> p (k c)")).then_inc(wp_in, 16)
            sp.wait_ge(uvt_ready, 3)
            sp.dma_start(g["dram_uv"], uvT[:, :]).then_inc(uv_out, 16)
            sp.wait_ge(yl_ready, KT)
            for t in range(NT + 2):
                if t < NT:
                    if t >= 3:
                        sp.wait_ge(res_out[t % 3], 16 * (t // 3))
                    sp.dma_start(xt[t % 3][:, :], g["x"][t * P:(t + 1) * P, :]).then_inc(x_in[t % 3], 16)
                if t >= 2:
                    sp.wait_ge(p_free, 2 * (t - 1))
                    sp.dma_start(g["dram_res"][t - 2], xt[(t - 2) % 3][:, :]).then_inc(res_out[(t - 2) % 3], 16)
            sp.wait_ge(uv_out, 16)
            sp.wait_ge(wp_in, 16)
            for i in range(3):
                sp.wait_ge(res_out[i], 16 * len(range(i, NT, 3)))

        @block.gpsimd
        def _(pool):
            own = Counter(pool, heads_own)
            own.done(nc.gpsimd.memset(head_of[:, :], 1.0))
            own.done(nc.gpsimd.affine_select(out=head_of[:, :], in_=head_of[:, :], compare_op=ALU.is_ge, fill=0.0,
                                             base=0, pattern=[[1, D]], channel_multiplier=-DH))
            own.done(nc.gpsimd.affine_select(out=head_of[:, :], in_=head_of[:, :], compare_op=ALU.is_ge, fill=0.0,
                                             base=DH - 1, pattern=[[-1, D]], channel_multiplier=DH))
            for k in range(KT):
                pool.wait_ge(wh_ready, k + 1)
                nc.gpsimd.tensor_tensor(wl[:, k, :], w_raw[k % 2][:, :], wh[:, k, :].bitcast(F32), ALU.subtract)\
                    .then_inc(wl_ready, 1)
            pool.wait_ge(bp_in, 16)
            for t in range(NT):
                pool.wait_ge(x_in[t % 3], 16 * (t // 3 + 1))
                nc.gpsimd.tensor_tensor(xt[t % 3][:, :], xt[t % 3][:, :], bp[:, :], ALU.add).then_inc(xb_ready, 1)

        @block.scalar
        def _(act):
            for k in range(KT):
                act.wait_ge(w_in[k % 2], 16 * (k // 2 + 1))
                nc.scalar.activation(wh[:, k, :], w_raw[k % 2][:, :], ACT.Copy).then_inc(wh_ready, 1)
                if k == 0:
                    for b, (t0, n) in enumerate(((0, 4), (4, 4), (8, 2))):
                        act.wait_ge(uvt_full, b + 1)
                        nc.scalar.activation(uvT[:, t0 * P:(t0 + n) * P].rearrange("p (t n) -> p t n", t=n),
                                             bank(b)[0:2 * HEADS, 0:128 * n].rearrange("p (t n) -> p t n", t=n)[:, :, 0:P],
                                             ACT.Copy).then_inc(uvt_ready, 1)
                act.wait_ge(y_norm, 3 * (k + 1))
                nc.scalar.activation(yh[:, k, :], y_raw[k % 3][:, :], ACT.Copy).then_inc(yh_ready, 1)

        @block.vector
        def _(dve):
            own = Counter(dve, norm_own)
            dve.wait_ge(den_in, 16)
            own.done(nc.vector.tensor_scalar(den[:, :], den[:, :], 1e-6, None, ALU.add))
            nc.vector.reciprocal(den[:, :], den[:, :]).then_inc(den_ready, 1)
            b_, mx = ab[:, :, HEADS:2 * HEADS], amax[:, :, :].rearrange("p h t -> p t h")
            dve.wait_ge(low_in, 16)
            own.done(nc.vector.tensor_tensor(uv[:, :, 0:HEADS], mx, low[:, :].unsqueeze(1).to_broadcast([P, NT, HEADS]), ALU.add))
            own.done(nc.vector.tensor_tensor(uv[:, :, 0:HEADS], b_, uv[:, :, 0:HEADS], ALU.add))
            own.done(nc.vector.scalar_tensor_tensor(m[:, :, :], uv[:, :, 0:HEADS], SLOPE, uv[:, :, 0:HEADS],
                                                    op0=ALU.mult, op1=ALU.max))
            own.done(nc.vector.tensor_tensor(uv[:, :, 0:HEADS], b_, m[:, :, :], ALU.subtract))
            nc.vector.scalar_tensor_tensor(uv[:, :, HEADS:2 * HEADS], b_, SLOPE, m[:, :, :],
                                           op0=ALU.mult, op1=ALU.subtract).then_inc(uv_ready, 1)

            def normalise(k):
                dve.wait_ge(y_in[k % 3], 16 * (k // 3 + 1))
                for c, (c0, n) in enumerate(CH):
                    dve.wait_ge(rec_full, 3 * k + c + 1)
                    here = y_raw[k % 3][:, c0:c0 + n]
                    nc.vector.tensor_tensor(here, here, bank(RB[(3 * k + c) % 2])[:, 0:n], ALU.mult).then_inc(y_norm, 1)

            for k in range(KT):
                normalise(k)
                dve.wait_ge(yh_ready, k + 1)
                nc.vector.tensor_tensor(yl[:, k, :], y_raw[k % 3][:, :], yh[:, k, :].bitcast(F32), ALU.subtract)\
                    .then_inc(yl_ready, 1)
            for t in range(NT):
                dve.wait_ge(xb_ready, t + 1)
                for half in range(2):
                    i, c = 2 * t + half, slice(384 * half, 384 * (half + 1))
                    dve.wait_ge(p_full, i + 1)
                    nc.vector.tensor_tensor(xt[t % 3][:, c], xt[t % 3][:, c], bank(i % 8)[0:P, 0:384], ALU.add)\
                        .then_inc(p_free, 1)

        @block.tensor
        def _(pe):
            pe.wait_ge(uv_ready, 1)
            for b, (t0, n) in enumerate(((0, 4), (4, 4), (8, 2))):
                for t in range(n):
                    last = nc.tensor.transpose(bank(b)[0:2 * HEADS, 128 * t:128 * t + P], uv[:, t0 + t, :], ident[0:P, 0:P])
                last.then_inc(uvt_full, 1)
            pe.wait_ge(uvt_ready, 3)
            pe.wait_ge(heads_own, 3)
            pe.wait_ge(rec_in, 16)

            def reciprocals(k, chunks):
                for c in chunks:
                    c0, n = CH[c]
                    if 3 * k + c >= 2:
                        pe.wait_ge(y_norm, 3 * k + c - 1)
                    nc.tensor.matmul(bank(RB[(3 * k + c) % 2])[:, 0:n], head_of[:, 128 * k:128 * (k + 1)], recT[:, c0:c0 + n],
                                     start=True, stop=True).then_inc(rec_full, 1)

            reciprocals(0, (0, 1, 2))
            for k in range(KT):
                pe.wait_ge(yl_ready, k + 1)
                pe.wait_ge(wl_ready, k + 1)
                if k + 1 < KT:
                    reciprocals(k + 1, (0, 1))
                for i in range(EARLY):
                    if i == EARLY // 2 and k + 1 < KT:
                        reciprocals(k + 1, (2,))
                    t, c = i // 2, slice(384 * (i % 2), 384 * (i % 2 + 1))
                    nodes = slice(t * P, (t + 1) * P)
                    last = split_matmul(nc, bank(i)[0:P, 0:384], (yh[:, k, nodes], yl[:, k, nodes]),
                                        (wh[:, k, c], wl[:, k, c]), k == 0, k == KT - 1)
                    if k == KT - 1:
                        last.then_inc(p_full, 1)
            for i in range(EARLY, 2 * NT):
                t, c = i // 2, slice(384 * (i % 2), 384 * (i % 2 + 1))
                nodes = slice(t * P, (t + 1) * P)
                if i < 8:
                    pe.wait_ge(y_norm, 3 * KT)
                else:
                    pe.wait_ge(p_free, i - 7)
                for k in range(KT):
                    last = split_matmul(nc, bank(i % 8)[0:P, 0:384], (yh[:, k, nodes], yl[:, k, nodes]),
                                        (wh[:, k, c], wl[:, k, c]), k == 0, k == KT - 1)
                last.then_inc(p_full, 1)


def convolutions(nc, g):
    at, acc, x1T, cnt, acol, ncol, ident, bank = (g[k] for k in "at acc x1T cnt acol ncol ident bank".split())
    with ExitStack() as ctx:
        def sb(name, shape, dt=F32):
            return ctx.enter_context(nc.sbuf_tensor(name, shape, dt))

        def sem(name):
            return ctx.enter_context(nc.semaphore(name))

        RING = 5
        LEAD = 2
        x1h = [at(f"x1h{i}", MASK_AT + 3008 * i, [128, KT, P], F32R) for i in range(2)]
        x1l = [at(f"x1l{i}", MASK_AT + 3008 * (2 + i), [128, KT, P], F32R) for i in range(2)]
        S = ACC_AT + 4 * NT * D
        prob = [at(f"prob{i}", S + 5024 * i, [P, N]) for i in range(RING)]
        urow, vrow = at("urow", S + 25120, [P, N]), at("vrow", S + 30144, [P, N])
        hN = at("hN", S + 35168, [P, NT, PC + 2])
        gN = hN[:, :, 1:PC + 1]
        xlh = [at(f"xlh{i}", S + 50624 + 3008 * i, [128, PK, 2 * P], F32R) for i in range(2)]
        xll = [at(f"xll{i}", S + 56640 + 3008 * i, [128, PK, 2 * P], F32R) for i in range(2)]
        w_raw = g["wp_first"]
        wp_raw = w_raw[:, :].rearrange("p (k c) -> p k c", k=KT)
        wo_raw = w_raw[:, :].rearrange("p (k c) -> p k c", k=PK)
        wph, wpl = (at(n, S + 62656 + 9216 * i, [128, KT, PC], F32R) for i, n in enumerate(("wph", "wpl")))
        woh, wol = (at(n, S + 81088 + 9216 * i, [128, PK, D], F32R) for i, n in enumerate(("woh", "wol")))
        a_pair, b_pair = sb("a_pair", [P, 2, NT]), sb("b_pair", [P, PC])
        total = sb("total", [P, 5, 2])
        (raw_in, row_in, bias_in, acc_in, ones_col, wh_ready, wl_ready, xh_ready, xl_ready, h_full, h_ready,
         pair_ready, z_ready, e_ready, prob_ready, prob_free, sum_full, g_ready, t_full, t_high, t_ready, o_full, o_free,
         total_own) = (sem(s) for s in (
             "raw_in row_in bias_in acc_in h_ones wh_ready wl_ready xh_ready xl_ready h_full h_ready pair_ready "
             "z_ready e_ready prob_ready prob_free sum_full g_ready t_full t_high t_ready o_full o_free total_own").split())
        block = ctx.enter_context(nc.Block())
        TILES = 2 * NT
        GR = NT // 2
        OT = 2 * NT
        TB = [(5, 6), (7, 0)]
        OB = [1, 2, 3, 4]

        @block.sync
        def _(sp):
            with sp.Fori(0, PAIRS) as i:
                sp.wait_ge(z_ready, 1 + TILES * i)
                for s in range(2):
                    if s:
                        sp.wait_ge(z_ready, 1 + TILES * i + NT)
                    for row, off in ((urow, 0), (vrow, HEADS)):
                        sp.dma_start(row[:, :], g["dram_uv"][bass.ds(2 * i + s + off, 1), :].to_broadcast([P, N]))\
                            .then_inc(row_in, 16)
                    if not s:
                        sp.wait_ge(wl_ready, 2 * i + 1)
                        sp.dma_start(wo_raw, g["w_out"][bass.ds(i, 1), :, :, :].rearrange("a p k c -> (a p) k c"))\
                            .then_inc(raw_in, 16)
                        sp.wait_ge(g_ready, 1 + TILES * i)
                        sp.dma_start(b_pair[:, :], g["b_gat"][bass.ds(i, 1), :].to_broadcast([P, PC])).then_inc(bias_in, 16)
                sp.wait_ge(wl_ready, 2 * i + 2)
                sp.dma_start(wp_raw, g["w_pair"][bass.ds(i, 1), :, :, :].rearrange("a p k c -> (a p) k c"))\
                    .then_inc(raw_in, 16)
            sp.wait_ge(raw_in, 16 * 2 * PAIRS)

        @block.gpsimd
        def _(pool):
            pool.dma_start(acc[:, :, :], g["b_out"].partition_broadcast(P).unsqueeze(1).to_broadcast([P, NT, D]))\
                .then_inc(acc_in, 16)
            nc.gpsimd.memset(hN[:, :, 0:1], 1.0).then_inc(ones_col, 1)
            nc.gpsimd.memset(hN[:, :, PC + 1:PC + 2], 1.0).then_inc(ones_col, 1)

            def low_part(low, raw, high, n):
                pool.wait_ge(wh_ready, n)
                nc.gpsimd.tensor_tensor(low[:, :, :], raw, high[:, :, :].bitcast(F32), ALU.subtract).then_inc(wl_ready, 1)

            with pool.Fori(0, PAIRS) as i:
                low_part(wol, wo_raw, woh, 2 * i + 2)
                low_part(wpl, wp_raw, wph, 2 * i + 3)

        @block.vector
        def _(dve):
            dve.wait_ge(wh_ready, 1)
            nc.vector.tensor_tensor(wpl[:, :, :], wp_raw, wph[:, :, :].bitcast(F32), ALU.subtract).then_inc(wl_ready, 1)
            dve.sem_inc(prob_free, RING - 1)
            with dve.Fori(0, PAIRS) as i:
                chain = [0]

                def own(instruction):
                    chain[0] += 1
                    instruction.then_inc(total_own, 1)
                    dve.wait_ge(total_own, i * 20 + chain[0])

                def scores(n):
                    s, j = n // NT, n % NT
                    if j == 0:
                        dve.wait_ge(row_in, 64 * i + 32 * (s + 1))
                    used = (n - RING) % TILES
                    if used % NT == NT - 1:
                        dve.wait_ge(sum_full, 1 + 10 * i + (0 if n < RING else 5))
                    else:
                        dve.wait_ge(prob_free, (TILES - 2) * i + (1 + n if n < RING else RING + used - used // NT))
                    nc.vector.scalar_tensor_tensor(
                        prob[n % RING][:, :], vrow[:, :], ncol[:, bass.ds(2 * i + s, 1), j:j + 1].rearrange("p a t -> p (a t)"),
                        urow[:, :], op0=ALU.add, op1=ALU.max).then_inc(z_ready, 1)

                def weigh(n):
                    dve.wait_ge(e_ready, TILES * i + n + 1)
                    nc.vector.scalar_tensor_tensor(prob[n % RING][:, :], prob[n % RING][:, :], 1.0, cnt[:, n % NT, :],
                                                   op0=ALU.min, op1=ALU.mult).then_inc(prob_ready, 1)

                def normalise(s):
                    if s == 0:
                        dve.wait_ge(bias_in, 16 * (i + 1))
                    for b in range(5):
                        dve.wait_ge(sum_full, 1 + 10 * i + 5 * s + b + 1)
                        both = bank(b)[0:P, 0:386].rearrange("p (t c) -> p t c", t=2)
                        own(nc.vector.tensor_scalar(total[:, b, :], both[:, :, C * s], 1e-16, None, ALU.add))
                        own(nc.vector.reciprocal(total[:, b, :], total[:, b, :]))
                        for t in range(2):
                            nc.vector.scalar_tensor_tensor(gN[:, 2 * b + t, C * s:C * (s + 1)], both[:, t, 1 - s:C + 1 - s], total[:, b, t:t + 1],
                                                           b_pair[:, C * s:C * (s + 1)], op0=ALU.mult, op1=ALU.add)\
                                .then_inc(g_ready, 1)

                for t in range(NT):
                    dve.wait_ge(xh_ready, NT * i + t + 1)
                    nc.vector.tensor_tensor(x1l[t % 2][:, :, 0:P], x1T[:, :, t * P:(t + 1) * P],
                                            x1h[t % 2][:, :, 0:P].bitcast(F32), ALU.subtract).then_inc(xl_ready, 1)
                    if t >= NT - RING:
                        scores(t - (NT - RING))
                for n in range(TILES):
                    if RING <= n + LEAD < TILES:
                        scores(n + LEAD)
                    weigh(n)
                    if n == NT:
                        normalise(0)
                normalise(1)

                def low_part(gr):
                    for part, (ks, b) in enumerate(((slice(0, 2), TB[gr % 2][0]), (slice(2, 3), TB[gr % 2][1]))):
                        n = ks.stop - ks.start
                        dve.wait_ge(t_high, 2 * (GR * i + gr) + part + 1)
                        nc.vector.scalar_tensor_tensor(
                            xll[gr % 2][:, ks, :], bank(b)[:, 0:n * 2 * P].rearrange("p (k n) -> p k n", k=n), 0.0,
                            xlh[gr % 2][:, ks, :].bitcast(F32), op0=ALU.max, op1=ALU.subtract).then_inc(t_ready, 1)

                low_part(0)
                dve.wait_ge(acc_in, 16)
                for gr in range(GR):
                    if gr + 1 < GR:
                        low_part(gr + 1)
                    for o in range(4 * gr, 4 * gr + 4):
                        t, half = o // 2, o % 2
                        dve.wait_ge(o_full, 1 + OT * i + o + 1)
                        here = acc[:, t, 384 * half:384 * (half + 1)]
                        nc.vector.tensor_tensor(here, here, bank(OB[o % 4])[0:P, 0:384], ALU.add).then_inc(o_free, 1)
                dve.wait_ge(o_free, 1 + OT * (i + 1))

        @block.scalar
        def _(act):
            def high_part(high, raw, n, used, count):
                if used is not None:
                    act.wait_ge(raw_in, 16 * (n - 1))
                    act.wait_ge(used, count)
                nc.scalar.activation(high[:, :, :], raw, ACT.Copy).then_inc(wh_ready, 1)

            high_part(wph, wp_raw, 1, None, 0)
            act.wait_ge(ones_col, 2)
            with act.Fori(0, PAIRS) as i:
                def exponential(n):
                    act.wait_ge(z_ready, 1 + TILES * i + n + 1)
                    nc.scalar.activation(prob[n % RING][:, :], prob[n % RING][:, :], ACT.Exp,
                                         bias=a_pair[:, n // NT, n % NT:n % NT + 1]).then_inc(e_ready, 1)

                def take_h(t):
                    act.wait_ge(h_full, 1 + NT * i + t + 1)
                    nc.scalar.activation(hN[:, t, 1:PC + 1], bank(5 + t % 3)[0:P, 0:PC], ACT.Copy).then_inc(h_ready, 1)

                for t in range(NT):
                    act.wait_ge(h_full, 1 + NT * i + (t - 1 if t >= 2 else 0))
                    nc.scalar.activation(x1h[t % 2][:, :, 0:P], x1T[:, :, t * P:(t + 1) * P], ACT.Copy).then_inc(xh_ready, 1)
                    if t == 1:
                        nc.scalar.activation(a_pair[:, :, :], acol[:, bass.ds(2 * i, 2), :], ACT.Copy).then_inc(pair_ready, 1)
                        act.wait_ge(pair_ready, i + 1)
                    if t >= 1:
                        take_h(t - 1)
                    if t >= NT - RING + 1:
                        exponential(t - (NT - RING + 1))
                take_h(NT - 1)
                for n in range(RING - 1, TILES):
                    exponential(n)
                    if n == 6:
                        high_part(woh, wo_raw, 2 * i + 2, o_full, 1 + OT * i)
                    if n == 13:
                        high_part(wph, wp_raw, 2 * i + 3, h_full, 1 + NT * (i + 1))
                for gr in range(GR):
                    for part, (ks, b) in enumerate(((slice(0, 2), TB[gr % 2][0]), (slice(2, 3), TB[gr % 2][1]))):
                        n = ks.stop - ks.start
                        act.wait_ge(t_full, 2 * (GR * i + gr) + part + 1)
                        if gr >= 2 and part == 0:
                            act.wait_ge(o_full, 1 + OT * i + 4 * (gr - 1))
                        nc.scalar.activation(xlh[gr % 2][:, ks, :], bank(b)[:, 0:n * 2 * P].rearrange("p (k n) -> p k n", k=n),
                                             ACT.Relu).then_inc(t_high, 1)

        @block.tensor
        def _(pe):
            for s in (h_full, z_ready, o_full, o_free, g_ready, sum_full, t_ready):
                pe.sem_inc(s, 1)
            pe.wait_ge(ones_col, 2)
            with pe.Fori(0, PAIRS) as i:
                pe.wait_ge(wl_ready, 2 * i + 1)
                pe.wait_ge(t_ready, 1 + 2 * GR * i)
                for t in range(NT):
                    pe.wait_ge(xl_ready, NT * i + t + 1)
                    if t >= 3:
                        pe.wait_ge(h_ready, NT * i + t - 2)
                    for k in range(KT):
                        last = split_matmul(nc, bank(5 + t % 3)[0:P, 0:PC], (x1h[t % 2][:, k, 0:P], x1l[t % 2][:, k, 0:P]),
                                            (wph[:, k, :], wpl[:, k, :]), k == 0, k == KT - 1)
                    last.then_inc(h_full, 1)
                for s in range(2):
                    for j in range(NT):
                        n = NT * s + j
                        if not s:
                            pe.wait_ge(h_ready, NT * i + j + 1)
                        pe.wait_ge(prob_ready, TILES * i + n + 1)
                        for t in range(NT):
                            if j == 0 and t % 2 == 0:
                                if s:
                                    pe.wait_ge(g_ready, 1 + 20 * i + t + 2)
                                elif t == 0:
                                    pe.wait_ge(o_free, 1 + OT * i)
                            last = nc.tensor.matmul(bank(t // 2)[0:P, 193 * (t % 2):193 * (t % 2) + 193],
                                                    prob[n % RING][:, t * P:(t + 1) * P], hN[:, j, 193 * s:193 * (s + 1)],
                                                    start=j == 0 and t % 2 == 0, stop=j == NT - 1, skip_group_check=True)
                            if j == NT - 1 and t % 2:
                                last.then_inc(sum_full, 1)
                        if j < NT - 1:
                            last.then_inc(prob_free, 1)

                def transposes(gr):
                    pe.wait_ge(g_ready, 1 + 20 * i + 10 + 2 * (gr + 1))
                    if gr == 1:
                        pe.wait_ge(g_ready, 1 + 20 * (i + 1))
                    for k in range(PK):
                        b, c0 = (TB[gr % 2][0], 250 * k) if k < 2 else (TB[gr % 2][1], 0)
                        for t in range(2):
                            last = nc.tensor.transpose(bank(b)[:, c0 + t * P:c0 + (t + 1) * P],
                                                       gN[:, 2 * gr + t, 128 * k:128 * (k + 1)], ident[0:P, 0:P])
                        if k:
                            last.then_inc(t_full, 1)

                def outputs(gr):
                    pe.wait_ge(t_ready, 1 + 2 * (GR * i + gr) + 2)
                    for o in range(4 * gr, 4 * gr + 4):
                        t, c = o // 2 % 2, slice(384 * (o % 2), 384 * (o % 2 + 1))
                        if o >= 4:
                            pe.wait_ge(o_free, 1 + OT * i + o - 3)
                        nodes = slice(t * P, (t + 1) * P)
                        for k in range(PK):
                            last = split_matmul(nc, bank(OB[o % 4])[0:P, 0:384], (xlh[gr % 2][:, k, nodes], xll[gr % 2][:, k, nodes]),
                                                (woh[:, k, c], wol[:, k, c]), k == 0, k == PK - 1)
                        last.then_inc(o_full, 1)

                transposes(0)
                transposes(1)
                pe.wait_ge(wl_ready, 2 * i + 2)
                for gr in range(GR):
                    outputs(gr)
                    if gr + 2 < GR:
                        transposes(gr + 2)


def adapter(nc, g):
    at, acc, ident, bank = (g[k] for k in "at acc ident bank".split())
    with ExitStack() as ctx:
        def sb(name, shape, dt=F32):
            return ctx.enter_context(nc.sbuf_tensor(name, shape, dt))

        def sem(name):
            return ctx.enter_context(nc.semaphore(name))

        W = EX + EX * R
        S = ACC_AT + 4 * NT * D
        xn2T = at("xn2T", X1_AT, [128, KT, N])
        xn = [at(f"xn2_{i}", S + 3072 * i, [P, D])[:, :] for i in range(3)]
        res = [at(f"res{i}", S + 9216 + 3072 * i, [P, D])[:, :] for i in range(4)]
        wd = at("wd", S + 21504, [128, KT, R])[:, :, :]
        wr = at("wr", S + 23040, [R, W])[:, :]
        wu = at("wu", S + 24128, [R, D])[:, :]
        gam = at("gam", S + 27200, [R, D])[:, :]
        be = at("be", S + 30272, [P, EX * R])[:, :]
        fT = at("fT", S + 31296, [R, N])[:, :]
        le = at("le", S + 36320, [P, NT, W])[:, :, :]
        pick = at("pick", S + 46720, [P, NT, EX, R])[:, :, :, :]
        comb = at("comb", S + 56960, [P, NT, R])[:, :, :]
        best, total = sb("best", [P, NT]), sb("esum", [P, NT])
        hot, taken, el = sb("hot", [P, NT, EX]), sb("taken", [P, NT]), sb("el", [P, NT, EX])
        stats = sb("stats2", [P, 2, 2, 6])
        moments, rstd = sb("moments2", [P, NT, 2]), sb("rstd2", [P, NT])
        std, eps = sb("std2", [P, NT]), sb("eps2", [P, 1])
        res_in = [sem(f"res_in{i}") for i in range(4)]
        eps_ready = sem("eps2_ready")
        x2_ready, var_ready, std_ready = sem("x2_ready"), sem("var2_ready"), sem("std2_ready")
        (w_in, own_s, xn_ready, xt_full, xt_free, d_full, f_ready, r_full, r_free, el_ready, ex_ready, wu_ready,
         comb_ready, c_full, full_ready, up_full, y_ready, out_done) = (sem(s) for s in (
             "aw_in own2 xn2_ready xt2_full xt2_free d_full f_ready r_full r_free el_ready ex_ready wu_ready comb_ready "
             "c_full full_ready up_full ay_ready out_done").split())
        block = ctx.enter_context(nc.Block())

        GROUPS = ((0, 4), (4, 4), (8, 2))

        @block.sync
        def _(sp):
            for t in range(NT):
                if t >= 4:
                    sp.wait_ge(x2_ready, t - 3)
                sp.dma_start(res[t % 4], g["dram_res"][t]).then_inc(res_in[t % 4], 16)
                if t == 3:
                    sp.dma_start(wd, g["w_down"]).then_inc(w_in, 16)
                    sp.dma_start(wr, g["w_route"]).then_inc(w_in, 16)
                    sp.dma_start(wu, g["w_up"]).then_inc(w_in, 16)
                    sp.dma_start(gam, g["gamma"].partition_broadcast(R)).then_inc(w_in, 16)
                    sp.dma_start(be, g["b_exp"].partition_broadcast(P)).then_inc(w_in, 16)
            for t in range(NT):
                sp.wait_ge(y_ready, 2 * (t + 1))
                sp.dma_start(g["out"][t * P:(t + 1) * P, :], acc[:, t, :]).then_inc(out_done, 16)
            sp.wait_ge(out_done, 16 * NT)

        @block.vector
        def _(dve):
            own = Counter(dve, own_s)
            nc.vector.memset(eps[:, :], EPS).then_inc(eps_ready, 1)

            def statistics(t):
                dve.wait_ge(res_in[t % 4], 16 * (t // 4 + 1))
                nc.vector.scalar_tensor_tensor(acc[:, t, :], acc[:, t, :], 0.0, res[t % 4], op0=ALU.max, op1=ALU.add)\
                    .then_inc(x2_ready, 1)
                dve.wait_ge(x2_ready, t + 1)
                nc.vector.bn_stats(stats[:, t % 2, 0, :], acc[:, t, 0:D // 2]).then_inc(own_s, 1)
                own.n += 1
                own.done(nc.vector.bn_stats(stats[:, t % 2, 1, :], acc[:, t, D // 2:D]))
                nc.vector.bn_aggr(moments[:, t, :], stats[:, t % 2, :, :]).then_inc(var_ready, 1)

            statistics(0)
            for t in range(NT):
                if t + 1 < NT:
                    statistics(t + 1)
                dve.wait_ge(std_ready, t + 1)
                own.done(nc.vector.reciprocal(rstd[:, t:t + 1], std[:, t:t + 1]))
                if t >= 3:
                    dve.wait_ge(xt_full, 2 * (t - 2))
                nc.vector.tensor_scalar(xn[t % 3], acc[:, t, :], moments[:, t, 0:1], rstd[:, t:t + 1],
                                        ALU.subtract, ALU.mult).then_inc(xn_ready, 1)
            dve.wait_ge(w_in, 80)
            nc.vector.tensor_tensor(wu, wu, gam, ALU.mult).then_inc(wu_ready, 1)
            dve.wait_ge(r_free, NT)
            logit = le[:, :, 0:EX]
            own.done(nc.vector.tensor_reduce(best[:, :], logit, axis=AX.X, op=ALU.max))
            best_b = best[:, :].unsqueeze(2).to_broadcast([P, NT, EX])
            nc.vector.tensor_tensor(el[:, :, :], logit, best_b, ALU.subtract).then_inc(el_ready, 1)
            own.done(nc.vector.tensor_tensor(hot[:, :, :], logit, best_b, ALU.is_ge))
            own.done(nc.vector.tensor_copy(taken[:, :], hot[:, :, 0]))
            for e in range(1, EX):
                own.done(nc.vector.tensor_tensor(hot[:, :, e], hot[:, :, e], taken[:, :], ALU.is_gt))
                if e < EX - 1:
                    own.done(nc.vector.tensor_tensor(taken[:, :], hot[:, :, e], taken[:, :], ALU.max))
            dve.wait_ge(ex_ready, 1)
            own.done(nc.vector.tensor_reduce(total[:, :], el[:, :, :], axis=AX.X, op=ALU.add))
            own.done(nc.vector.reciprocal(total[:, :], total[:, :]))
            own.done(nc.vector.memset(total[0:CLS, 0:1], 0.0))
            own.done(nc.vector.tensor_tensor(hot[:, :, :], hot[:, :, :], total[:, :].unsqueeze(2).to_broadcast([P, NT, EX]), ALU.mult))
            own.done(nc.vector.tensor_tensor(pick, le[:, :, EX:W].rearrange("p t (e r) -> p t e r", e=EX),
                                             be.rearrange("p (e r) -> p e r", e=EX).unsqueeze(1).to_broadcast([P, NT, EX, R]), ALU.add))
            own.done(nc.vector.tensor_tensor(pick, pick, hot[:, :, :].unsqueeze(3).to_broadcast([P, NT, EX, R]), ALU.mult))
            own.done(nc.vector.tensor_tensor(pick[:, :, 0:2, :], pick[:, :, 0:2, :], pick[:, :, 2:4, :], ALU.add))
            nc.vector.tensor_tensor(comb, pick[:, :, 0, :], pick[:, :, 1, :], ALU.add).then_inc(comb_ready, 1)
            for b, (t0, n) in enumerate(GROUPS):
                dve.wait_ge(c_full, b + 1)
                here = fT[:, t0 * P:(t0 + n) * P]
                nc.vector.tensor_tensor(here, here, bank(b)[0:R, 0:n * P], ALU.add).then_inc(full_ready, 1)
            for t in range(NT):
                for half in range(2):
                    i = 2 * t + half
                    dve.wait_ge(up_full, i + 1)
                    here = acc[:, t, 384 * half:384 * (half + 1)]
                    nc.vector.tensor_tensor(here, here, bank(3 + i % 5)[0:P, 0:384], ALU.add).then_inc(y_ready, 1)

        @block.scalar
        def _(act):
            def deviation(t):
                act.wait_ge(var_ready, t + 1)
                nc.scalar.activation(std[:, t:t + 1], moments[:, t, 1:2], ACT.Sqrt, bias=eps[:, :]).then_inc(std_ready, 1)

            def gelu(b):
                t0, n = GROUPS[b]
                act.wait_ge(d_full, b + 1)
                nc.scalar.activation(fT[:, t0 * P:(t0 + n) * P], bank(4 + b)[0:R, 0:n * P], ACT.Gelu).then_inc(f_ready, 1)

            act.wait_ge(eps_ready, 1)
            deviation(0)
            for i in range(2 * NT):
                t, half = i // 2, i % 2
                if half == 0 and t + 1 < NT:
                    deviation(t + 1)
                    if t + 1 == NT - 1:
                        gelu(0)
                        gelu(1)
                act.wait_ge(xt_full, i + 1)
                nc.scalar.activation(xn2T[:, 3 * half:3 * half + 3, t * P:(t + 1) * P],
                                     bank(i % 4)[:, 0:3 * P].rearrange("p (k n) -> p k n", k=3), ACT.Copy).then_inc(xt_free, 1)
            gelu(2)
            for t in range(NT):
                act.wait_ge(r_full, t + 1)
                nc.scalar.activation(le[:, t, :], bank(t % 4)[0:P, 0:W], ACT.Copy).then_inc(r_free, 1)
            act.wait_ge(el_ready, 1)
            nc.scalar.activation(el[:, :, :], el[:, :, :], ACT.Exp).then_inc(ex_ready, 1)

        @block.tensor
        def _(pe):
            def down(b):
                t0, n = GROUPS[b]
                nodes = slice(t0 * P, (t0 + n) * P)
                pe.wait_ge(xt_free, 2 * (t0 + n))
                pe.wait_ge(w_in, 80)
                for k in range(KT):
                    last = nc.tensor.matmul(bank(4 + b)[0:R, 0:n * P], wd[:, k, :], xn2T[:, k, nodes], start=k == 0, stop=k == KT - 1)
                last.then_inc(d_full, 1)

            for i in range(2 * NT):
                t, half = i // 2, i % 2
                if not half:
                    pe.wait_ge(xn_ready, t + 1)
                if i >= 4:
                    pe.wait_ge(xt_free, i - 3)
                for k in range(3):
                    f = 3 * half + k
                    last = nc.tensor.transpose(bank(i % 4)[:, k * P:(k + 1) * P], xn[t % 3][:, f * 128:(f + 1) * 128], ident[0:P, 0:P])
                last.then_inc(xt_full, 1)
                if i in (9, 17):
                    down((i - 9) // 8)
            down(2)
            pe.wait_ge(xt_free, 2 * NT)
            for t in range(NT):
                if t % 4 == 0:
                    pe.wait_ge(f_ready, t // 4 + 1)
                if t >= 4:
                    pe.wait_ge(r_free, t - 3)
                nc.tensor.matmul(bank(t % 4)[0:P, 0:W], fT[:, t * P:(t + 1) * P], wr, start=True, stop=True).then_inc(r_full, 1)
            pe.wait_ge(comb_ready, 1)
            for b, (t0, n) in enumerate(GROUPS):
                for t in range(n):
                    last = nc.tensor.transpose(bank(b)[0:R, t * P:(t + 1) * P], comb[:, t0 + t, :], ident[0:P, 0:P])
                last.then_inc(c_full, 1)
            pe.wait_ge(wu_ready, 1)
            for t in range(NT):
                if t in (0, 4, 8):
                    pe.wait_ge(full_ready, t // 4 + 1)
                for half in range(2):
                    i = 2 * t + half
                    if i >= 5:
                        pe.wait_ge(y_ready, i - 4)
                    nc.tensor.matmul(bank(3 + i % 5)[0:P, 0:384], fT[:, t * P:(t + 1) * P], wu[:, 384 * half:384 * (half + 1)],
                                     start=True, stop=True).then_inc(up_full, 1)


def kernel(**inputs):
    import numpy as np
    import concourse.bacc as bacc
    from concourse.bass_utils import run_bass_kernel_spmd

    a = {k: np.asarray(v) for k, v in inputs.items()}

    def tiles(w):
        return w.reshape(-1, 128, w.shape[-1]).transpose(1, 0, 2)

    gat = [a[f"L0_gnn_W{i}"] for i in range(LAYERS)]
    qkv = a["L0_mix_W_qkv"].T.reshape(KT, 128, 3, PAIRS, 128).transpose(3, 1, 0, 2, 4).reshape(PAIRS, 128, KT, 384)
    data = {
        "x": a["x"],
        "src_t": a["src"].reshape(ET, P).T,
        "dst_t": a["dst"].reshape(ET, P).T,
        "dst_c": a["dst"].reshape(CHUNKS, CE * P),
        "w_ah": a["L0_gnn_W_ah"].reshape(KT, 128, KT, 128).transpose(2, 1, 0, 3),
        "b_ah": a["L0_gnn_b_ah"].reshape(KT, 128).T,
        "w_gat": np.stack([tiles(w) for w in gat]),
        "a_gat": np.stack([np.stack([a[f"L0_gnn_a_src{i}"].reshape(D), a[f"L0_gnn_a_dst{i}"].reshape(D)]) for i in range(LAYERS)]),
        "w_pair": np.stack(([tiles(w[:, c:c + PC]) for w in gat for c in (0, PC)] * 2)[1:PAIRS + 1]),
        "b_gat": np.stack([a[f"L0_gnn_b{i}"] for i in range(LAYERS)]).reshape(PAIRS, PC),
        "w_out": a["L0_gnn_W_out"].reshape(PAIRS, PK, 128, D).transpose(0, 2, 1, 3),
        "b_out": a["L0_gnn_b_out"],
        "w_qkv": np.concatenate([qkv[1:], qkv[:1]]),
        "w_proj": tiles(a["L0_mix_W_proj"].T),
        "b_proj": a["L0_mix_b_proj"],
        "w_down": tiles(a["L0_ffn_Wd"].T),
        "w_route": np.concatenate([a["L0_ffn_Wg"].T, a["L0_ffn_We"].reshape(EX * R, R).T], axis=1),
        "b_exp": a["L0_ffn_be"].reshape(EX * R),
        "w_up": a["L0_ffn_Wu"].T,
        "gamma": a["L0_ffn_gamma"],
    }
    nc = bacc.Bacc("TRN2", target_bir_lowering=False, num_devices=1)
    arrays, args = {}, []
    for name, v in data.items():
        arrays[f"in_{name}"] = np.ascontiguousarray(v)
        args.append(nc.dram_tensor(f"in_{name}", v.shape, mybir.dt.from_np(v.dtype), kind="ExternalInput").ap())
    args.append(nc.dram_tensor("out_0", (N, D), F32, kind="ExternalOutput").ap())
    build(nc, *args)
    r = run_bass_kernel_spmd(nc, [arrays], core_ids=[0])
    return r.results[0]["out_0"]
```
